# Optimizing a Trainium2 kernel written in Bass

```python
import numpy as np
import jax
import jax.numpy as jnp

def _softmax(x, axis=-1):
    return jax.nn.softmax(x, axis=axis)

def _gelu(x):
    return jax.nn.gelu(x, approximate=True)

def _silu(x):
    return jax.nn.silu(x)

def _sigmoid(x):
    return jax.nn.sigmoid(x)

def _layernorm(x, axis=-1, eps=1e-05):
    m = jnp.mean(x, axis=axis, keepdims=True)
    v = jnp.var(x, axis=axis, keepdims=True)
    return (x - m) / jnp.sqrt(v + eps)

def _scatter_add(tgt, idx, src, axis=0):
    return tgt.at[idx].add(src)

def _segment_sum(src, seg, n):
    return jax.ops.segment_sum(src, seg, n)
kernel_name = 'mk_adj_resnorm_d2_adj_r2_546a28'

def setup_inputs(seed: int=0):
    np.random.seed(seed)
    _w = jnp.asarray

    def _rec_inputs():
        import jax
        import jax.numpy as jnp
        _gk = jax.random.key(seed)
        x = -0.0004776 + 1.001 * jax.random.normal(jax.random.fold_in(_gk, 1), (1354, 512), jnp.float32)
        _a = jax.random.bernoulli(jax.random.fold_in(_gk, 2), 0.00295421, (1354, 1354))
        _a = jnp.logical_or(_a, jnp.eye(1354, dtype=bool))
        _af = _a.astype(jnp.float32)
        adj = _af
        return (x, adj)
    x, adj = _rec_inputs()

    def _L0_gnn_setup():
        import jax, jax.numpy as jnp
        import numpy as np
        N, H, E, HEADS = (1500, 512, 10000, 8)
        DK = H // HEADS
        key = jax.random.key(seed)
        k1, k2, k3, k4 = jax.random.split(key, 4)
        inst_feature = jax.random.normal(k1, (N, H), dtype=jnp.float32)
        rel_pair_index = jax.random.randint(k2, (E, 2), 0, N, dtype=jnp.int64)
        agg = jnp.zeros((N, N), dtype=jnp.float32)
        agg = agg.at[rel_pair_index[:, 0], rel_pair_index[:, 1]].set(1.0)
        agg = agg.at[jnp.arange(N), jnp.arange(N)].set(1.0)
        std = float(np.sqrt(2.0 / (H + DK)))
        Wq = jax.random.normal(k3, (H, H), dtype=jnp.float32) * std
        Wk = jax.random.normal(k4, (H, H), dtype=jnp.float32) * std
        bq = jnp.zeros((H,), dtype=jnp.float32)
        bk = jnp.zeros((H,), dtype=jnp.float32)
        return {'inst_feature': inst_feature, 'aggregator_matrix': agg, 'rel_pair_index': rel_pair_index, 'Wq': Wq, 'bq': bq, 'Wk': Wk, 'bk': bk}
    _L0_gnn_all = _L0_gnn_setup()
    _L0_gnn_in = {k: v for k, v in _L0_gnn_all.items() if k in ('rel_pair_index', 'Wq', 'bq', 'Wk', 'bk')}
    del _L0_gnn_all

    def _L1_gnn_setup():
        import jax, jax.numpy as jnp
        import numpy as np
        N = 4096
        IN_FEATURES = 512
        OUT_FEATURES = 512
        key = jax.random.key(seed)
        k_x, k_adj, k_w, k_b = jax.random.split(key, 4)
        x = jax.random.normal(k_x, (N, IN_FEATURES), dtype=jnp.float32)
        adj = jax.random.uniform(k_adj, (N, N), dtype=jnp.float32)
        stdv = 1.0 / np.sqrt(OUT_FEATURES)
        weight = jax.random.uniform(k_w, (IN_FEATURES, OUT_FEATURES), dtype=jnp.float32, minval=-stdv, maxval=stdv)
        bias = jax.random.uniform(k_b, (OUT_FEATURES,), dtype=jnp.float32, minval=-stdv, maxval=stdv)
        return {'x': x, 'adj': adj, 'weight': weight, 'bias': bias}
    _L1_gnn_all = _L1_gnn_setup()
    _L1_gnn_in = {k: v for k, v in _L1_gnn_all.items() if k in ('weight', 'bias')}
    del _L1_gnn_all
    return {'x': x, 'adj': adj, 'L0_gnn_rel_pair_index': _L0_gnn_in['rel_pair_index'], 'L0_gnn_Wq': _L0_gnn_in['Wq'], 'L0_gnn_bq': _L0_gnn_in['bq'], 'L0_gnn_Wk': _L0_gnn_in['Wk'], 'L0_gnn_bk': _L0_gnn_in['bk'], 'L1_gnn_weight': _L1_gnn_in['weight'], 'L1_gnn_bias': _L1_gnn_in['bias']}

def reference(x, adj, L0_gnn_rel_pair_index, L0_gnn_Wq, L0_gnn_bq, L0_gnn_Wk, L0_gnn_bk, L1_gnn_weight, L1_gnn_bias):
    import jax
    import jax.numpy as jnp

    def _L0_gnn_ref(inst_feature, aggregator_matrix, rel_pair_index, Wq, bq, Wk, bk):
        import jax, jax.numpy as jnp
        import numpy as np
        N, H, E, HEADS = (1500, 512, 10000, 8)
        DK = H // HEADS
        n = inst_feature.shape[0]
        sub = rel_pair_index[:, 0]
        obj = rel_pair_index[:, 1]
        q = (inst_feature[sub] @ Wq.T + bq).reshape(-1, HEADS, DK)
        k = (inst_feature[obj] @ Wk.T + bk).reshape(-1, HEADS, DK)
        att = ((q * k).sum(-1) / np.sqrt(DK)).T.astype(inst_feature.dtype)
        scores = jnp.zeros((HEADS, n, n), dtype=inst_feature.dtype)
        scores = scores.at[:, sub, obj].set(att)
        mask = (1.0 - aggregator_matrix).astype(bool)
        scores = jnp.where(mask[None], -jnp.inf, scores)
        di = jnp.arange(n)
        scores = scores.at[:, di, di].set(1e-07)
        attn = jax.nn.softmax(scores, axis=2)
        aggregator_factor = attn.sum(axis=0) / HEADS
        return aggregator_factor @ inst_feature

    def _L1_gnn_ref(x, adj, weight, bias):
        import jax, jax.numpy as jnp
        import numpy as np
        N = 4096
        IN_FEATURES = 512
        OUT_FEATURES = 512
        support = jnp.matmul(x, weight)
        output = jnp.matmul(adj, support)
        return output + bias
    x = _layernorm(x + _L0_gnn_ref(x, adj, L0_gnn_rel_pair_index, L0_gnn_Wq, L0_gnn_bq, L0_gnn_Wk, L0_gnn_bk), axis=-1)
    x = _layernorm(x + _L1_gnn_ref(x, adj, L1_gnn_weight, L1_gnn_bias), axis=-1)
    return x

_drawn_inputs = setup_inputs


def setup_inputs(seed=0):
    import zlib

    import numpy as np

    out = dict(_drawn_inputs(seed))
    spreads = {'L0_gnn_bq': (0.0, 2.0), 'L0_gnn_bk': (0.0, 2.0)}
    factors = {'L0_gnn_Wq': 40.394, 'L0_gnn_Wk': 46.139, 'L1_gnn_bias': 3.95}
    for name, (base, spread) in spreads.items():
        noise = np.random.default_rng([zlib.crc32(name.encode()), seed]).standard_normal(out[name].shape)
        drawn = base * np.exp(spread * noise) if base else spread * noise
        out[name] = jnp.asarray(drawn.astype(out[name].dtype))
    for name, factor in factors.items():
        out[name] = (out[name] * factor).astype(out[name].dtype)
    return out
```

```python
import numpy as np
import concourse.bass as bass
from concourse import mybir
from contextlib import ExitStack

N = 1354
H = 512
E = 10000
HEADS = 8
DK = H // HEADS
P = 128
T = (N + P - 1) // P
LAST = N - (T - 1) * P
NP = T * P
KF = H // P
EP = 125
EC = E // EP
SLOTS = 64
CHUNKS = [0, 24, 48, 72, EC]
CHUNK_AT = [3, 6, 9]
RING = 3
GW = H + 2
XS = 64.0
WS = 256.0
SS = 256.0
TINY = float(np.float32(1e-7))
A0 = float(np.float32(np.exp(-1e-7)))
EPS = 1e-5
FAR = 4096.0
GONE = -1e30


def resnorm_graph(nc, x, adj, pairs, wq, bq, wk, bk, w1, b1, out):
    f32, f16, i32 = mybir.dt.float32, mybir.dt.float16, mybir.dt.int32
    ALU, ACT, AX = mybir.AluOpType, mybir.ActivationFunctionType, mybir.AxisListType
    width = [P] * (T - 1) + [LAST]

    with ExitStack() as ctx:
        def sb(name, shape, dt=f32):
            return ctx.enter_context(nc.sbuf_tensor(name, shape, dt))

        def sem(name):
            return ctx.enter_context(nc.semaphore(name))

        sums_dram = nc.dram_tensor("sums_dram", [NP, GW], f32, kind="Internal").ap()
        live_map = nc.dram_tensor("live_map", [N, N], f32, kind="Internal").ap()
        live_flat = live_map.rearrange("i (j o) -> (i j) o", o=1)
        adj_flat = adj.rearrange("i (j o) -> (i j) o", o=1)

        x_sb = sb("x_sb", [P, T, H])
        xs = sb("xs", [P, 2, T, H], f16)
        ss = sb("ss", [P, 2, T, H], f16)
        adjT = sb("adjT", [P, T, NP], f16)
        stage = sb("stage", [P, RING, N])
        sums = sb("sums", [P, 2, GW])
        wraw = sb("wraw", [P, 3, KF, H])
        wT = sb("wT", [P, 2, KF, H])
        whl = sb("whl", [P, 2, KF, H], f16)
        bias = sb("bias", [P, 3, H])
        x1T = sb("x1T", [P, 2, 2, H], f16)
        xd = sb("xd", [P, 2, H])
        y = sb("y", [P, 2, H])
        co = sb("co", [P, 2, 8])
        st = sb("st", [P, 2, 12])
        onehot = sb("onehot", [P, 24, P], f16)
        stackL = sb("stackL", [P, NP], f16)
        stackR = sb("stackR", [P, 2, H], f16)

        ident = sb("ident", [P, P])
        ones = sb("ones", [P, P])
        ones16 = sb("ones16", [P, P], f16)
        below16 = sb("below16", [P, P], f16)
        slot_no = sb("slot_no", [P, 2, SLOTS])
        earlier = sb("earlier", [P, SLOTS])
        col_no = sb("col_no", [P, NP], f16)
        eps = sb("eps", [P, 1])
        junk16 = sb("junk16", [P, P], f16)
        row_no = sb("row_no", [P, T])

        ed_i = sb("ed_i", [P, EC, 2], i32)
        ed = sb("ed", [P, EC, 2])
        ok2 = sb("ok2", [P, EC, 2])
        ed_ok = sb("ed_ok", [P, EC])
        ed_in = sb("ed_in", [P, EC])
        ed_lin = sb("ed_lin", [P, EC])
        ed_idx = sb("ed_idx", [P, EC], i32)
        ed_adj = sb("ed_adj", [P, EC])
        ed3 = sb("ed3", [P, EC, 3], f16)
        flag = sb("flag", [P, EC], f16)
        seen = sb("seen", [P, EC])
        pos = sb("pos", [P, 3, 24])
        pos_all = seen[0:EP]
        slot = sb("slot", [P, 16])
        slot_i = sb("slot_i", [P, 2], i32)
        count_i = sb("count_i", [P, 1], i32)

        raw = wraw[:, :, :, :].rearrange("p a b c -> p (a b c)")
        xsub, xobj = raw[:, 0:H], raw[:, H:2 * H]
        gsub = raw[:, 2 * H:2 * H + GW]
        at = 2 * H + GW

        def take(n):
            nonlocal at
            at += n
            return raw[:, at - n:at]
        xsT, xoT, q, kk = take(H), take(H), take(H), take(H)
        spread = take(H)
        EXTRA = SLOTS + 3
        score = take(HEADS * EXTRA).rearrange("p (h g) -> p h g", h=HEADS)
        same, keq, vsame = take(P), take(SLOTS), take(P)
        dx1 = take(H)
        small = take(80)
        assert at <= 3 * KF * H
        slot_row = sb("slot_row", [P, T, SLOTS], f16)
        dT = x1T[:, 0, :, 0:KF * SLOTS]

        d_adj, d_live, d_mask, d_score = (raw[:, n * N:(n + 1) * N] for n in range(4))
        d_x = raw[:, 4 * N:4 * N + H]
        flat_stage = stage[:, :, :].rearrange("p r n -> p (r n)")
        d_prob, d_share = flat_stage[:, 0:N], flat_stage[:, N:2 * N]
        d_shareT = onehot[:, :, :].rearrange("p a b -> p (a b)").bitcast(f32)[:, 0:NP].rearrange("p (k i) -> p k i", k=T)
        d_xT, d_qT = y[:, 0, :], y[:, 1, :]
        d_x1, d_y = xd[:, 0, :], xd[:, 1, :]
        x32 = xs[:, :, :, :].rearrange("p a t h -> p (a t h)").bitcast(f32).rearrange("p (t h) -> p t h", t=T)
        kT = ss[:, :, :, :].rearrange("p a t h -> p (a t h)").bitcast(f32).rearrange("p (k i) -> p k i", k=KF)
        bias_col = sb("bias_col", [P, 2, KF])
        d_no = sb("d_no", [P, 1])
        d_st = sb("d_st", [P, 12])
        d_s = sb("d_s", [P, 24])

        tr = [ctx.enter_context(nc.psum_tensor(f"tr{i}", [P, 512], f32)) for i in range(3)]
        acc = [ctx.enter_context(nc.psum_tensor(f"acc{i}", [P, 512], f32)) for i in range(5)]
        PRE, TOT, CMP = 0, 24, 48
        WB = [0, 1, 2, 4]

        edges_loaded, w1_loaded, wqk_loaded, bias_loaded = map(sem, ("edges_loaded", "w1_loaded", "wqk_loaded", "bias_loaded"))
        x_loaded = [sem(f"x_loaded{i}") for i in range(4)]
        adj_loaded = [sem(f"adj_loaded{i}") for i in range(RING)]
        sums_stored = [sem(f"sums_stored{i}") for i in range(2)]
        edges_looked_up = [sem(f"edges_looked_up{i}") for i in range(4)]
        pad_zeroed, tr_zeroed, consts = sem("pad_zeroed"), sem("tr_zeroed"), sem("consts")
        dve_step, pool_step = sem("dve_step"), sem("pool_step")
        x_hi, x_lo, w1_hi, w1_lo = map(sem, ("x_hi", "x_lo", "w1_hi", "w1_lo"))
        adj_transposed, adjT_ready, adj_read = map(sem, ("adj_transposed", "adjT_ready", "adj_read"))
        sums_done, sums_copied, coefs_ready, xd_ready = map(sem, ("sums_done", "sums_copied", "coefs_ready", "xd_ready"))
        y_ready, stats_ready, x1_ready, x1_transposed = map(sem, ("y_ready", "stats_ready", "x1_ready", "x1_transposed"))
        x1T_hi, x1T_lo, support_done, support_hi, support_lo = map(sem, ("x1T_hi", "x1T_lo", "support_done", "support_hi", "support_lo"))
        moments_ready, root_ready, slot_moments, slot_root, z_moments, z_root = map(sem, ("moments_ready", "root_ready", "slot_moments", "slot_root", "z_moments", "z_root"))
        idx_ready, flags_ready, numbered, onehot_ready, compacted = map(sem, ("idx_ready", "flags_ready", "numbered", "onehot_ready", "compacted"))
        wqk_transposed, wqkT_ready, count_ready = map(sem, ("wqk_transposed", "wqkT_ready", "count_ready"))
        slot_idx_ready, xsub_in, xobj_in, gsub_in = map(sem, ("slot_idx_ready", "xsub_in", "xobj_in", "gsub_in"))
        spread_ready, subs_spread, same_ready, rows_ready = map(sem, ("spread_ready", "subs_spread", "same_ready", "rows_ready"))
        xsub_T, xobj_T, xsT_ready, xoT_ready, q_done, k_done = map(sem, ("xsub_T", "xobj_T", "xsT_ready", "xoT_ready", "q_done", "k_done"))
        cols_done, cols_copied, scores_ready, scores_spread = map(sem, ("cols_done", "cols_copied", "scores_ready", "scores_spread"))
        live_done, exps_in, exps_done, shares_ready, mixed = map(sem, ("live_done", "exps_in", "exps_done", "shares_ready", "mixed"))
        qk_read, change_ready, change_T, dT_hi, dT_lo = map(sem, ("qk_read", "change_ready", "change_T", "dT_hi", "dT_lo"))
        dS_done, right_hi, right_lo, low_ready = map(sem, ("dS_done", "right_hi", "right_lo", "low_ready"))
        biased, out_done, z_ready, z_stats, z_normed = map(sem, ("biased", "out_done", "z_ready", "z_stats", "z_normed"))
        map_clear, map_idx_ready, map_zeroed, map_marked = map(sem, ("map_clear", "map_idx_ready", "map_zeroed", "map_marked"))
        general_in, rows_in, general_step = map(sem, ("general_in", "rows_in", "general_step"))
        turn = sem("turn")
        out_stored = [sem(f"out_stored{i}") for i in range(4)]

        block = ctx.enter_context(nc.Block())

        def rows(ap2d, t):
            return ap2d[t * P:t * P + width[t], :]

        KEYS = 1
        KEY_TURNS = 5
        ROWS = KEYS + T * KEY_TURNS
        HEAD_TURNS = 4
        TAIL = 5 + HEADS * HEAD_TURNS
        ROW_TURNS = TAIL + 9
        SUPPORT = ROWS + T * ROW_TURNS
        SUPPORT_TURNS = 7
        FINISHED = SUPPORT + T * SUPPORT_TURNS
        ROW_STEPS = 7 + HEADS * 11 + 3 + 3
        SPANS = [(0, 512), (512, 1024), (1024, N)]

        def overflow(eng):
            eng.wait_ge(count_ready, 1)
            return eng.If(eng.value_load(count_i[0:1, 0:1], min_val=0, max_val=E) > SLOTS)

        def general_sp(sp):
            sp.wait_ge(turn, KEYS)
            for n, b in enumerate((bq, bk)):
                for k in range(KF):
                    sp.dma_start(bias_col[:, n, k:k + 1], b[k * P:(k + 1) * P].rearrange("(p o) -> p o", o=1)).then_inc(general_in, 16)
            for t in range(T):
                sp.dma_start(x32[0:width[t], t, :], rows(x, t)).then_inc(general_in, 16)
            sp.wait_ge(map_clear, 1)
            for t in range(T):
                sp.dma_start(rows(live_map, t), d_adj[0:width[t]]).then_inc(map_zeroed, 16)
            sp.wait_ge(map_marked, 16 * EC)
            for t in range(T):
                sp.wait_ge(turn, ROWS + t * ROW_TURNS)
                sp.dma_start(d_adj[0:width[t]], rows(adj, t)).then_inc(rows_in, 16)
                sp.dma_start(d_live[0:width[t]], rows(live_map, t)).then_inc(rows_in, 16)
            sp.wait_ge(turn, FINISHED)

        def general_pool(pool):
            pool.wait_ge(map_idx_ready, 1)
            pool.wait_ge(map_zeroed, 16 * T)
            for c in range(EC):
                nc.gpsimd.indirect_dma_start(
                    out=live_flat, out_offset=bass.IndirectOffsetOnAxis(ap=ed_idx[0:EP, c:c + 1], axis=0),
                    in_=ones[0:EP, 0:1], in_offset=None, bounds_check=N * N - 1, oob_is_err=False).then_inc(map_marked, 16)
                pool.wait_ge(map_marked, 16 * (c + 1))
            pool.wait_ge(turn, FINISHED)

        def general_pe(pe):
            mm = nc.tensor.matmul
            with pe.Fori(0, T) as t:
                at = KEYS + t * KEY_TURNS
                pe.wait_ge(turn, at + 1)
                for k in range(KF):
                    last = nc.tensor.transpose(tr[0][:, k * P:(k + 1) * P], d_x[:, k * P:(k + 1) * P], ident[:])
                last.then_inc(turn, 1)
                pe.wait_ge(turn, at + 3)
                for o in range(KF):
                    for k in range(KF):
                        last = mm(tr[1][:, o * P:(o + 1) * P], wT[:, 1, k, o * P:(o + 1) * P], d_xT[:, k * P:(k + 1) * P],
                                  start=(k == 0), stop=(k == KF - 1))
                last.then_inc(turn, 1)
            with pe.Fori(0, T) as t:
                at = ROWS + t * ROW_TURNS
                pe.wait_ge(turn, at + 1)
                for k in range(KF):
                    last = nc.tensor.transpose(tr[0][:, k * P:(k + 1) * P], d_x[:, k * P:(k + 1) * P], ident[:])
                last.then_inc(turn, 1)
                pe.wait_ge(turn, at + 3)
                for o in range(KF):
                    for k in range(KF):
                        last = mm(tr[1][:, o * P:(o + 1) * P], wT[:, 0, k, o * P:(o + 1) * P], d_xT[:, k * P:(k + 1) * P],
                                  start=(k == 0), stop=(k == KF - 1))
                last.then_inc(turn, 1)
                for h in range(HEADS):
                    lo, o = DK * (h % 2), h // 2
                    pe.wait_ge(turn, at + 5 + HEAD_TURNS * h)
                    for b, (i, j) in enumerate(SPANS):
                        last = mm(acc[b][:, 0:j - i], d_qT[lo:lo + DK, o * P:(o + 1) * P], kT[lo:lo + DK, o, i:j],
                                  start=True, stop=True)
                    last.then_inc(turn, 1)
                pe.wait_ge(turn, at + TAIL + 1)
                for k in range(T):
                    last = nc.tensor.transpose(tr[k // 4][0:width[k], (k % 4) * P:(k % 4 + 1) * P],
                                               d_share[:, k * P:k * P + width[k]], ident[:])
                last.then_inc(turn, 1)
                pe.wait_ge(turn, at + TAIL + 3)
                for k in range(T):
                    last = mm(acc[3][:, :], d_shareT[0:width[k], k, :], x32[0:width[k], k, :], start=(k == 0), stop=(k == T - 1))
                last.then_inc(turn, 1)
            with pe.Fori(0, T) as t:
                at = SUPPORT + t * SUPPORT_TURNS
                pe.wait_ge(turn, at + 1)
                for k in range(KF):
                    last = nc.tensor.transpose(tr[0][:, k * P:(k + 1) * P], d_x1[:, k * P:(k + 1) * P], ident[:])
                last.then_inc(turn, 1)
                pe.wait_ge(turn, at + 4)
                for k in range(KF):
                    for n, (a, b) in enumerate(((0, 0), (0, 1), (1, 0))):
                        last = mm(tr[1][:, :], x1T[:, 0, a, k * P:(k + 1) * P], whl[:, b, k, :],
                                  start=(k == 0 and n == 0), stop=(k == KF - 1 and n == 2))
                last.then_inc(turn, 1)
            pe.wait_ge(turn, FINISHED)

        def general_act(act):
            A = nc.scalar
            act.wait_ge(general_in, 16 * (2 * KF + T))
            with act.Fori(0, T) as t:
                at = KEYS + t * KEY_TURNS
                act.wait_ge(turn, at + 2)
                A.copy(d_xT, tr[0][:, :]).then_inc(turn, 1)
                act.wait_ge(turn, at + 4)
                for o in range(KF):
                    last = A.activation(kT[:, o, bass.ts(t, P)], tr[1][:, o * P:(o + 1) * P], ACT.Identity, bias=bias_col[:, 1, o:o + 1])
                last.then_inc(turn, 1)
            with act.Fori(0, T) as t:
                at = ROWS + t * ROW_TURNS
                act.wait_ge(turn, at + 2)
                A.copy(d_xT, tr[0][:, :]).then_inc(turn, 1)
                act.wait_ge(turn, at + 4)
                for o in range(KF):
                    last = A.activation(d_qT[:, o * P:(o + 1) * P], tr[1][:, o * P:(o + 1) * P], ACT.Identity, bias=bias_col[:, 0, o:o + 1])
                last.then_inc(turn, 1)
                for h in range(HEADS):
                    act.wait_ge(turn, at + 5 + HEAD_TURNS * h + 2)
                    A.activation(d_prob, d_score, ACT.Exp, bias=d_s[:, 4:5], accum_out=d_s[:, 7:8])
                    A.activation(d_s[:, 8:10], d_s[:, 5:7], ACT.Exp).then_inc(turn, 1)
                act.wait_ge(turn, at + TAIL + 2)
                for b in range(3):
                    n = min(4, T - 4 * b)
                    last = A.copy(d_shareT[:, 4 * b:4 * b + n, :], tr[b][:, 0:n * P].rearrange("p (k i) -> p k i", k=n))
                last.then_inc(turn, 1)
                act.wait_ge(turn, at + TAIL + 5)
                A.activation(d_st[:, 10:11], d_st[:, 7:8], ACT.Sqrt, bias=eps[:]).then_inc(turn, 1)
                act.wait_ge(turn, at + TAIL + 7)
                A.activation(d_x1, d_y, ACT.Identity, bias=d_st[:, 9:10], scale=d_st[:, 8:9]).then_inc(turn, 1)
            with act.Fori(0, T) as t:
                at = SUPPORT + t * SUPPORT_TURNS
                act.wait_ge(turn, at + 2)
                A.mul(x1T[:, 0, 0, :], tr[0][:, :], XS).then_inc(turn, 1)
                act.wait_ge(turn, at + 5)
                A.mul(ss[:, 0, bass.ds(t, 1), :].rearrange("p o h -> p (o h)"), tr[1][:, :], SS / (XS * WS)).then_inc(turn, 1)
            act.wait_ge(turn, FINISHED)

        def general_dve(dve):
            V = nc.vector
            done = 0
            k = 0
            base = 0

            def step(ins):
                nonlocal k
                k += 1
                ins.then_inc(general_step, 1)
                dve.wait_ge(general_step, base + k)

            dve.wait_ge(wqkT_ready, 8)
            dve.wait_ge(compacted, 4)
            dve.wait_ge(support_lo, T)
            dve.wait_ge(bias_loaded, 48)
            for b in range(2):
                dve.wait_ge(sums_stored[b], 16 * len(range(b, T, 2)))
            step(V.tensor_scalar(pos_all, flag[0:EP], -float(N * N), float(N * N), ALU.mult, ALU.add))
            step(V.tensor_tensor(pos_all, pos_all, ed_lin[0:EP], ALU.add))
            V.tensor_copy(ed_idx[0:EP], pos_all).then_inc(map_idx_ready, 1)
            V.memset(d_adj, 0.0).then_inc(map_clear, 1)
            V.memset(d_live, 0.0).then_inc(turn, 1)
            dve.wait_ge(general_in, 16 * (2 * KF + T))
            done = k
            with dve.Fori(0, T) as t:
                at = KEYS + t * KEY_TURNS
                dve.wait_ge(turn, at)
                V.tensor_copy(d_x, x32[:, bass.ds(t, 1), :].rearrange("p o h -> p (o h)")).then_inc(turn, 1)
            s = d_s
            with dve.Fori(0, T) as t:
                base = done + t * ROW_STEPS
                k = 0
                at = ROWS + t * ROW_TURNS
                dve.wait_ge(turn, at)
                dve.wait_ge(rows_in, t * 32 + 32)
                V.tensor_copy(d_x, x32[:, bass.ds(t, 1), :].rearrange("p o h -> p (o h)"))
                step(V.tensor_copy(d_no[:], row_no[:, bass.ds(t, 1)]))
                step(V.reduce_sum(s[:, 0:1], d_adj, AX.X))
                step(V.reduce_sum(s[:, 1:2], d_live, AX.X))
                step(V.scalar_tensor_tensor(d_mask, col_no[:, 0:N], d_no[:], d_adj, ALU.is_equal, ALU.mult, accum_out=s[:, 2:3]))
                step(V.tensor_tensor(s[:, 0:1], s[:, 0:1], s[:, 1:2], ALU.subtract))
                step(V.tensor_tensor(s[:, 3:4], s[:, 0:1], s[:, 2:3], ALU.subtract))
                step(V.memset(s[:, 12:14], 0.0))
                V.tensor_scalar(d_mask, d_live, -1.0, -GONE, ALU.add, ALU.mult).then_inc(turn, 1)
                for h in range(HEADS):
                    here = at + 5 + HEAD_TURNS * h
                    dve.wait_ge(turn, here + 1)
                    for b, (i, j) in enumerate(SPANS):
                        step(V.scalar_tensor_tensor(d_score[:, i:j], acc[b][:, 0:j - i], 1.0 / float(np.sqrt(DK)), d_mask[:, i:j],
                                                    ALU.mult, ALU.add))
                    step(V.reduce_max(s[:, 10:11], d_score, AX.X))
                    step(V.tensor_scalar(s[:, 4:5], s[:, 10:11], TINY, -1.0, ALU.max, ALU.mult))
                    step(V.tensor_scalar(s[:, 5:6], s[:, 4:5], 1.0, None, ALU.mult))
                    V.tensor_scalar(s[:, 6:7], s[:, 4:5], TINY, None, ALU.add).then_inc(turn, 1)
                    dve.wait_ge(turn, here + 3)
                    step(V.scalar_tensor_tensor(s[:, 11:12], s[:, 8:9], s[:, 3:4], s[:, 7:8], ALU.mult, ALU.add))
                    step(V.tensor_tensor(s[:, 11:12], s[:, 11:12], s[:, 9:10], ALU.add))
                    step(V.reciprocal(s[:, 14:15], s[:, 11:12]))
                    step(V.tensor_scalar(s[:, 14:15], s[:, 14:15], 1.0 / HEADS, None, ALU.mult))
                    step(V.scalar_tensor_tensor(s[:, 12:14], s[:, 8:10], s[:, 14:15], s[:, 12:14], ALU.mult, ALU.add))
                    if h == 0:
                        ins = V.tensor_scalar(d_share, d_prob, s[:, 14:15], None, ALU.mult)
                    else:
                        ins = V.scalar_tensor_tensor(d_share, d_prob, s[:, 14:15], d_share, ALU.mult, ALU.add)
                    ins.then_inc(turn, 1)
                dve.wait_ge(turn, at + TAIL)
                step(V.tensor_tensor(d_live, d_adj, d_live, ALU.subtract))
                step(V.tensor_tensor(s[:, 15:16], s[:, 12:13], s[:, 2:3], ALU.mult))
                step(V.scalar_tensor_tensor(s[:, 16:17], s[:, 13:14], 1.0, s[:, 15:16], ALU.add, ALU.subtract))
                V.scalar_tensor_tensor(d_share, d_live, s[:, 12:13], d_share, ALU.mult, ALU.add).then_inc(turn, 1)
                dve.wait_ge(turn, at + TAIL + 4)
                step(V.scalar_tensor_tensor(d_y, d_x, s[:, 16:17], acc[3][:, :], ALU.mult, ALU.add))
                step(V.bn_stats(d_st[:, 0:6], d_y))
                V.tensor_copy(s[:, 17:18], s[:, 16:17])
                V.bn_aggr(d_st[:, 6:8], d_st[:, 0:6]).then_inc(turn, 1)
                dve.wait_ge(turn, at + TAIL + 6)
                step(V.reciprocal(d_st[:, 8:9], d_st[:, 10:11]))
                V.tensor_scalar(d_st[:, 9:10], d_st[:, 6:7], -1.0, d_st[:, 8:9], ALU.mult, ALU.mult).then_inc(turn, 1)
                dve.wait_ge(turn, at + TAIL + 8)
                V.tensor_copy(x_sb[:, bass.ds(t, 1), :].rearrange("p o h -> p (o h)"), d_x1).then_inc(turn, 1)
                assert k == ROW_STEPS, k
            with dve.Fori(0, T) as t:
                at = SUPPORT + t * SUPPORT_TURNS
                dve.wait_ge(turn, at)
                V.tensor_copy(d_x1, x_sb[:, bass.ds(t, 1), :].rearrange("p o h -> p (o h)")).then_inc(turn, 1)
                dve.wait_ge(turn, at + 3)
                V.scalar_tensor_tensor(x1T[:, 0, 1, :], tr[0][:, :], XS, x1T[:, 0, 0, :], ALU.mult, ALU.subtract).then_inc(turn, 1)
                dve.wait_ge(turn, at + 6)
                V.scalar_tensor_tensor(ss[:, 1, bass.ds(t, 1), :].rearrange("p o h -> p (o h)"), tr[1][:, :], SS / (XS * WS),
                                       ss[:, 0, bass.ds(t, 1), :].rearrange("p o h -> p (o h)"), ALU.mult, ALU.subtract).then_inc(turn, 1)
            dve.wait_ge(turn, FINISHED)

        def y4(t):
            return (y if t % 4 < 2 else xd)[:, t % 2, :]

        def number(pe, n):
            a, b = CHUNKS[n], CHUNKS[n + 1]
            pe.wait_ge(flags_ready, n + 1)
            nc.tensor.matmul(acc[3][:, PRE:PRE + b - a], below16[0:EP, :], flag[0:EP, a:b], start=True, stop=True)
            nc.tensor.matmul(acc[3][:, TOT:TOT + b - a], ones16[0:EP, :], flag[0:EP, a:b], start=True, stop=True).then_inc(numbered, 1)

        def compact(pe, n):
            a, b = CHUNKS[n], CHUNKS[n + 1]
            pe.wait_ge(onehot_ready, n + 1)
            for c in range(a, b):
                last = nc.tensor.matmul(acc[3][:, CMP + 3 * n:CMP + 3 * n + 3], onehot[0:EP, c - a, :], ed3[0:EP, c, :],
                                        start=(c == a), stop=(c == b - 1))
            last.then_inc(compacted, 1)

        @block.sync
        def _(sp):
            sp.dma_start(ed_i[0:EP], pairs.rearrange("(p c) two -> p c two", p=EP)).then_inc(edges_loaded, 16)
            for g in range(3):
                sp.dma_start(x_sb[:, 3 * g:3 * g + 3, :],
                             x[3 * g * P:(3 * g + 3) * P, :].rearrange("(t p) h -> p t h", p=P)).then_inc(x_loaded[g], 16)
                if g == 0:
                    sp.dma_start(stage[:, 0, :], rows(adj, 0)).then_inc(adj_loaded[0], 16)
            sp.dma_start(x_sb[:, 9, :], rows(x, 9)).then_inc(x_loaded[3], 16)
            sp.wait_ge(pad_zeroed, 1)
            sp.dma_start(x_sb[0:LAST, T - 1, :], rows(x, T - 1)).then_inc(x_loaded[3], 16)
            sp.dma_start(stage[:, 1, :], rows(adj, 1)).then_inc(adj_loaded[1], 16)
            sp.dma_start(wraw[:, 2], w1.rearrange("(k p) o -> p k o", p=P)).then_inc(w1_loaded, 16)

            def store_sums(t):
                sp.wait_ge(sums_copied, t + 1)
                sp.wait_ge(coefs_ready, t + 1)
                sp.dma_start(sums_dram[t * P:(t + 1) * P, :], sums[:, t % 2, :]).then_inc(sums_stored[t % 2], 16)

            for t in range(2, T + 4):
                if t < T:
                    if t >= RING:
                        sp.wait_ge(adj_transposed, 3 * (t - RING + 1))
                        sp.wait_ge(adj_read, t - RING + 1)
                    sp.dma_start(stage[0:width[t], t % RING, :], rows(adj, t)).then_inc(adj_loaded[t % RING], 16)
                if t == 4:
                    sp.dma_start(wraw[:, 0], wq.rearrange("(k p) i -> p k i", p=P)).then_inc(wqk_loaded, 16)
                    sp.dma_start(wraw[:, 1], wk.rearrange("(k p) i -> p k i", p=P)).then_inc(wqk_loaded, 16)
                    for n, b in enumerate((bq, bk, b1)):
                        sp.dma_start(bias[:, n, :], b.partition_broadcast(P)).then_inc(bias_loaded, 16)
                if t >= 4:
                    store_sums(t - 4)
            with overflow(sp):
                general_sp(sp)
            for t in range(T):
                sp.wait_ge(z_normed, t + 1)
                sp.dma_start(rows(out, t), y4(t)[0:width[t]]).then_inc(out_stored[t % 4], 16)
            for b in range(4):
                sp.wait_ge(out_stored[b], 16 * len(range(b, T, 4)))

        @block.gpsimd
        def _(pool):
            nc.gpsimd.memset(x_sb[64:P, T - 1, :], 0.0).then_inc(pad_zeroed, 1)
            pool.wait_ge(pad_zeroed, 1)
            nc.gpsimd.memset(eps[:], EPS).then_inc(consts, 1)
            nc.gpsimd.memset(ident[:], 0.0).then_inc(pool_step, 1)
            nc.gpsimd.memset(ones[:], 1.0).then_inc(pool_step, 1)
            nc.gpsimd.memset(ones16[:], 1.0).then_inc(pool_step, 1)
            nc.gpsimd.memset(earlier[:], 1.0).then_inc(pool_step, 1)
            pool.wait_ge(pool_step, 4)
            nc.gpsimd.affine_select(out=ident[:], in_=ident[:], compare_op=ALU.not_equal, fill=1.0,
                                    base=0, pattern=[[-1, P]], channel_multiplier=1).then_inc(consts, 1)
            nc.gpsimd.affine_select(out=below16[:], in_=ones16[:], compare_op=ALU.is_gt, fill=0.0,
                                    base=0, pattern=[[1, P]], channel_multiplier=-1).then_inc(consts, 1)
            for half in range(2):
                pool.wait_ge(consts, 3 + half)
                part = earlier[64 * half:64 * half + 64, :]
                nc.gpsimd.affine_select(out=part, in_=part, compare_op=ALU.is_gt, fill=0.0,
                                        base=0, pattern=[[-1, SLOTS]], channel_multiplier=1).then_inc(consts, 1)
            pool.wait_ge(consts, 5)
            nc.gpsimd.iota(slot_no[:], pattern=[[0, 2], [1, SLOTS]], base=0, channel_multiplier=0,
                           allow_small_or_imprecise_dtypes=True).then_inc(consts, 1)
            nc.gpsimd.iota(col_no[:], pattern=[[1, NP]], base=0, channel_multiplier=0,
                           allow_small_or_imprecise_dtypes=True).then_inc(consts, 1)
            nc.gpsimd.iota(row_no[:], pattern=[[P, T]], base=0, channel_multiplier=1,
                           allow_small_or_imprecise_dtypes=True).then_inc(consts, 1)
            pool.wait_ge(idx_ready, 1)
            for c in range(EC):
                n = sum(c >= b for b in CHUNKS[1:])
                nc.gpsimd.indirect_dma_start(
                    out=ed_adj[0:EP, c:c + 1], out_offset=None, in_=adj_flat,
                    in_offset=bass.IndirectOffsetOnAxis(ap=ed_idx[0:EP, c:c + 1], axis=0)).then_inc(edges_looked_up[n], 16)
            with overflow(pool):
                general_pool(pool)
            pool.wait_ge(slot_idx_ready, 1)
            pool.wait_ge(wqkT_ready, 8)
            nc.gpsimd.indirect_dma_start(
                out=xsub, out_offset=None, in_=x,
                in_offset=bass.IndirectOffsetOnAxis(ap=slot_i[:, 0:1], axis=0)).then_inc(xsub_in, 16)
            nc.gpsimd.indirect_dma_start(
                out=xobj, out_offset=None, in_=x,
                in_offset=bass.IndirectOffsetOnAxis(ap=slot_i[:, 1:2], axis=0)).then_inc(xobj_in, 16)
            pool.wait_ge(sums_stored[0], 16 * len(range(0, T, 2)))
            pool.wait_ge(sums_stored[1], 16 * len(range(1, T, 2)))
            nc.gpsimd.indirect_dma_start(
                out=gsub, out_offset=None, in_=sums_dram,
                in_offset=bass.IndirectOffsetOnAxis(ap=slot_i[:, 0:1], axis=0)).then_inc(gsub_in, 16)
            pool.wait_ge(same_ready, 1)
            for rows_in in (xsub_in, xobj_in, gsub_in):
                pool.wait_ge(rows_in, 16)
            nc.gpsimd.tensor_scalar(stackL[64:P, :], col_no[64:P, :], slot[64:P, 3:4], None, ALU.is_equal).then_inc(low_ready, 1)
            pool.wait_ge(low_ready, 1)
            pool.wait_ge(bias_loaded, 48)
            for t in range(T):
                pool.wait_ge(x1_transposed, t + 1)
                nc.gpsimd.tensor_tensor(x_sb[:, t, :], x_sb[:, t, :], bias[:, 2, :], ALU.add).then_inc(biased, 1)

        @block.scalar
        def _(act):
            def copy_adjT(t):
                for b in range(3):
                    n = min(4, T - 4 * b)
                    act.wait_ge(adj_transposed, 3 * t + b + 1)
                    nc.scalar.copy(adjT[:, 4 * b:4 * b + n, t * P:(t + 1) * P],
                                   tr[b][:, 0:n * P].rearrange("p (k i) -> p k i", k=n)).then_inc(adjT_ready, 1)

            def root(s):
                return nc.scalar.activation(s[:, 10:11], s[:, 7:8], ACT.Sqrt, bias=eps[:])

            for g in range(4):
                act.wait_ge(x_loaded[g], 16 if g < 3 else 32)
                hi = min(3 * g + 3, T)
                nc.scalar.mul(xs[:, 0, 3 * g:hi, :], x_sb[:, 3 * g:hi, :], XS).then_inc(x_hi, 1)
            act.wait_ge(tr_zeroed, 1)
            copy_adjT(0)
            copy_adjT(1)
            act.wait_ge(w1_loaded, 16)
            nc.scalar.mul(whl[:, 0], wraw[:, 2], WS).then_inc(w1_hi, 1)
            for i in range(T + 1):
                if i < T:
                    act.wait_ge(coefs_ready, i + 1)
                    if i >= 2:
                        act.wait_ge(y_ready, i - 1)
                    nc.scalar.mul(xd[:, i % 2, :], x_sb[:, i, :], co[:, i % 2, 4:5]).then_inc(xd_ready, 1)
                    act.wait_ge(sums_done, i + 1)
                    nc.scalar.copy(sums[:, i % 2, 0:H], acc[i % 2][:, :]).then_inc(sums_copied, 1)
                if i >= 1:
                    act.wait_ge(x1_transposed, i)
                    if i >= 3:
                        act.wait_ge(support_done, i - 2)
                    nc.scalar.mul(x1T[:, (i - 1) % 2, 0, :], acc[4][:, :], XS).then_inc(x1T_hi, 1)
                if i < T:
                    act.wait_ge(moments_ready, i + 1)
                    root(st[:, i % 2]).then_inc(root_ready, 1)
                if i + 2 < T:
                    copy_adjT(i + 2)
                if i < T:
                    act.wait_ge(stats_ready, i + 1)
                    nc.scalar.activation(x_sb[:, i, :], y[:, i % 2, :], ACT.Identity, bias=st[:, i % 2, 9:10],
                                         scale=st[:, i % 2, 8:9]).then_inc(x1_ready, 1)
                if i >= 1:
                    act.wait_ge(support_done, i)
                    nc.scalar.mul(ss[:, 0, i - 1, :], acc[2][:, :], SS / (XS * WS)).then_inc(support_hi, 1)
            for n in range(8):
                act.wait_ge(wqk_transposed, n + 1)
                nc.scalar.copy(wT[:, n // 4, n % 4, :], acc[WB[n % 4]][:, :]).then_inc(wqkT_ready, 1)
            with overflow(act):
                general_act(act)
            act.wait_ge(xsub_T, 1)
            nc.scalar.copy(xsT, tr[1][:, :]).then_inc(xsT_ready, 1)
            for n in range(2):
                act.wait_ge(cols_done, n + 1)
                nc.scalar.copy(stackL[0:64, 512 * n:512 * n + 512], tr[0][0:64, :]).then_inc(cols_copied, 1)
            act.wait_ge(exps_in, 1)
            nc.scalar.activation(score, score, ACT.Exp).then_inc(exps_done, 1)
            act.wait_ge(cols_done, 3)
            nc.scalar.copy(stackL[0:64, 1024:NP], tr[0][0:64, 0:NP - 1024]).then_inc(cols_copied, 1)
            for n in range(2):
                act.wait_ge(slot_moments, n + 1)
                root(st[:, n]).then_inc(slot_root, 1)
            act.wait_ge(change_ready, 1)
            nc.scalar.mul(stackR[64:P, 0, :], dx1[64:P, :], SS).then_inc(right_hi, 1)
            act.wait_ge(change_T, 1)
            nc.scalar.mul(dT[:, 0, :], tr[0][:, 0:KF * SLOTS], XS).then_inc(dT_hi, 1)
            act.wait_ge(dS_done, 1)
            nc.scalar.mul(stackR[0:64, 0, :], tr[1][0:64, :], SS / (XS * WS)).then_inc(right_hi, 1)
            act.wait_ge(z_moments, 1)
            root(st[:, 0]).then_inc(z_root, 1)
            for t in range(T):
                if t + 1 < T:
                    act.wait_ge(z_moments, t + 2)
                    root(st[:, (t + 1) % 2]).then_inc(z_root, 1)
                act.wait_ge(z_stats, t + 1)
                nc.scalar.activation(y4(t), y4(t), ACT.Identity, bias=st[:, t % 2, 9:10],
                                     scale=st[:, t % 2, 8:9]).then_inc(z_normed, 1)

        @block.vector
        def _(dve):
            steps = 0

            def step(ins):
                nonlocal steps
                steps += 1
                ins.then_inc(dve_step, 1)
                dve.wait_ge(dve_step, steps)

            V = nc.vector
            V.memset(tr[2][:, :], 0.0).then_inc(tr_zeroed, 1)
            dve.wait_ge(edges_loaded, 16)
            e_i, e, o2, eok = ed_i[0:EP], ed[0:EP], ok2[0:EP], ed_ok[0:EP]
            step(V.tensor_copy(e, e_i))
            step(V.tensor_scalar(o2, e, 0.0, float(N), ALU.is_lt, ALU.mult))
            step(V.tensor_tensor(e, e, o2, ALU.add))
            step(V.tensor_scalar(o2, e, float(N), None, ALU.is_lt))
            step(V.scalar_tensor_tensor(o2, e, 0.0, o2, ALU.is_ge, ALU.mult))
            ein, lin = ed_in[0:EP], ed_lin[0:EP]
            step(V.tensor_tensor(ein, o2[:, :, 0], o2[:, :, 1], ALU.mult))
            step(V.scalar_tensor_tensor(lin, e[:, :, 0], float(N), e[:, :, 1], ALU.mult, ALU.add))
            step(V.tensor_tensor(lin, lin, ein, ALU.mult))
            V.tensor_copy(ed_idx[0:EP], lin).then_inc(idx_ready, 1)
            step(V.tensor_tensor(eok, e[:, :, 0], e[:, :, 1], ALU.not_equal))
            step(V.tensor_tensor(eok, eok, ein, ALU.mult))
            V.memset(ed3[0:EP, :, 2:3], 1.0).then_inc(dve_step, 1)
            steps += 1
            step(V.tensor_tensor(ed3[0:EP, :, 0:2], e, ein.unsqueeze(2).broadcast_to([EP, EC, 2]), ALU.mult))
            for g in range(4):
                hi = min(3 * g + 3, T)
                dve.wait_ge(x_hi, g + 1)
                V.scalar_tensor_tensor(xs[:, 1, 3 * g:hi, :], x_sb[:, 3 * g:hi, :], XS, xs[:, 0, 3 * g:hi, :],
                                       ALU.mult, ALU.subtract).then_inc(x_lo, 1)

            def coefs(t):
                c, s = co[:, t % 2], sums[:, t % 2]
                dve.wait_ge(adj_loaded[t % RING], 16 * (t // RING + 1))
                if t >= 2:
                    dve.wait_ge(sums_stored[t % 2], 16 * (t // 2))
                    dve.wait_ge(xd_ready, t - 1)
                step(V.reduce_sum(s[:, H:H + 1], stage[:, t % RING, :], AX.X))
                step(V.scalar_tensor_tensor(junk16[:, 0:width[t]], stage[:, t % RING, t * P:t * P + width[t]], 1.0,
                                            ident[:, 0:width[t]], ALU.mult, ALU.mult, accum_out=s[:, H + 1:H + 2]))
                step(V.tensor_tensor(s[:, H:H + 1], s[:, H:H + 1], s[:, H + 1:H + 2], ALU.subtract))
                V.tensor_scalar(c[:, 0:1], s[:, H:H + 1], A0, 1.0, ALU.mult, ALU.add).then_inc(adj_read, 1)
                dve.wait_ge(adj_read, t + 1)
                step(V.reciprocal(c[:, 1:2], c[:, 0:1]))
                step(V.tensor_scalar(c[:, 2:3], c[:, 1:2], A0, None, ALU.mult))
                step(V.tensor_tensor(c[:, 3:4], c[:, 2:3], s[:, H + 1:H + 2], ALU.mult))
                step(V.scalar_tensor_tensor(c[:, 4:5], c[:, 1:2], 1.0, c[:, 3:4], ALU.add, ALU.subtract))
                V.tensor_scalar(c[:, 5:6], c[:, 2:3], 1.0 / XS, None, ALU.mult).then_inc(coefs_ready, 1)

            def moments(s, v):
                step(V.bn_stats(s[:, 0:6], v))
                return V.bn_aggr(s[:, 6:8], s[:, 0:6])

            def scale_shift(s):
                step(V.reciprocal(s[:, 8:9], s[:, 10:11]))
                return V.tensor_scalar(s[:, 9:10], s[:, 6:7], -1.0, s[:, 8:9], ALU.mult, ALU.mult)

            def flag_chunk(n):
                a, b = CHUNKS[n], CHUNKS[n + 1]
                dve.wait_ge(edges_looked_up[n], 16 * (b - a))
                V.scalar_tensor_tensor(flag[0:EP, a:b], ed_adj[0:EP, a:b], 1.0, eok[:, a:b],
                                       ALU.is_equal, ALU.mult).then_inc(flags_ready, 1)

            def number_chunk(n):
                a, b = CHUNKS[n], CHUNKS[n + 1]
                m = b - a
                dve.wait_ge(numbered, n + 1)
                step(V.tensor_tensor_scan(seen[:, a:b], ones[:, 0:m], acc[3][:, TOT:TOT + m],
                                          seen[:, a - 1:a] if n else 0.0, ALU.mult, ALU.add))
                step(V.tensor_tensor(pos[:, 0, 0:m], seen[:, a:b], acc[3][:, TOT:TOT + m], ALU.subtract))
                step(V.tensor_tensor(pos[:, 1, 0:m], pos[:, 0, 0:m], acc[3][:, PRE:PRE + m], ALU.add))
                step(V.tensor_scalar(pos[0:EP, 2, 0:m], flag[0:EP, a:b], -FAR, FAR, ALU.mult, ALU.add))
                step(V.tensor_tensor(pos[0:EP, 0, 0:m], pos[0:EP, 1, 0:m], pos[0:EP, 2, 0:m], ALU.add))
                if n:
                    dve.wait_ge(compacted, n)
                V.tensor_tensor(onehot[0:EP, 0:m, :], pos[0:EP, 0, 0:m].unsqueeze(2).broadcast_to([EP, m, P]),
                                slot_no[0:EP].rearrange("p a b -> p (a b)").unsqueeze(1).broadcast_to([EP, m, P]),
                                ALU.is_equal).then_inc(onehot_ready, 1)

            dve.wait_ge(consts, 8)
            coefs(0)
            dve.wait_ge(w1_hi, 1)
            V.scalar_tensor_tensor(whl[:, 1], wraw[:, 2], WS, whl[:, 0], ALU.mult, ALU.subtract).then_inc(w1_lo, 1)
            for i in range(T + 1):
                if i - 1 in CHUNK_AT:
                    number_chunk(CHUNK_AT.index(i - 1))
                if i in CHUNK_AT:
                    flag_chunk(CHUNK_AT.index(i))
                if i + 1 < T:
                    coefs(i + 1)
                if i >= 1:
                    dve.wait_ge(x1T_hi, i)
                    V.scalar_tensor_tensor(x1T[:, (i - 1) % 2, 1, :], acc[4][:, :], XS, x1T[:, (i - 1) % 2, 0, :],
                                           ALU.mult, ALU.subtract).then_inc(x1T_lo, 1)
                if i < T:
                    dve.wait_ge(sums_copied, i + 1)
                    dve.wait_ge(xd_ready, i + 1)
                    if i >= 2:
                        dve.wait_ge(x1_ready, i - 1)
                    V.scalar_tensor_tensor(y[:, i % 2, :], acc[i % 2][:, :], co[:, i % 2, 5:6], xd[:, i % 2, :],
                                           ALU.mult, ALU.add).then_inc(y_ready, 1)
                    dve.wait_ge(y_ready, i + 1)
                    moments(st[:, i % 2], y[:, i % 2, :]).then_inc(moments_ready, 1)
                    dve.wait_ge(root_ready, i + 1)
                    scale_shift(st[:, i % 2]).then_inc(stats_ready, 1)
                if i >= 1:
                    dve.wait_ge(support_hi, i)
                    V.scalar_tensor_tensor(ss[:, 1, i - 1, :], acc[2][:, :], SS / (XS * WS), ss[:, 0, i - 1, :],
                                           ALU.mult, ALU.subtract).then_inc(support_lo, 1)
            flag_chunk(3)
            number_chunk(3)
            fits = slot[:, 8:9]
            V.tensor_copy(count_i[:], seen[:, EC - 1:EC]).then_inc(count_ready, 1)
            step(V.tensor_scalar(fits, seen[:, EC - 1:EC], float(SLOTS), None, ALU.is_le))
            dve.wait_ge(compacted, 4)
            step(V.tensor_reduce(slot[:, 0:3], acc[3][:, CMP:CMP + 12].rearrange("p (n v) -> p v n", v=3), AX.X, ALU.add))
            with overflow(dve):
                general_dve(dve)
            V.tensor_copy(slot_i[:], slot[:, 0:2]).then_inc(slot_idx_ready, 1)
            sub, key, valid = slot[:, 3:4], slot[:, 4:5], slot[:, 2:3]
            step(V.tensor_scalar(slot[:, 5:6], valid, -1.0, FAR, ALU.add, ALU.mult))
            step(V.tensor_tensor(sub, slot[:, 0:1], slot[:, 5:6], ALU.add))
            step(V.scalar_tensor_tensor(key, sub, 2048.0, slot[:, 1:2], ALU.mult, ALU.add))
            dve.wait_ge(wqkT_ready, 8)
            eye = ident[0:64, 0:64]
            step(V.tensor_scalar(spread[0:64, 0:64], eye, sub[0:64], None, ALU.mult))
            step(V.tensor_scalar(spread[0:64, 64:128], eye, sub[0:64], None, ALU.mult))
            V.tensor_scalar(spread[0:64, 128:192], eye, key[0:64], None, ALU.mult).then_inc(spread_ready, 1)
            dve.wait_ge(subs_spread, 1)
            V.tensor_tensor(slot_row[:, :, :], tr[0][:, 0:SLOTS].unsqueeze(1).broadcast_to([P, T, SLOTS]),
                            row_no[:, :].unsqueeze(2).broadcast_to([P, T, SLOTS]), ALU.is_equal).then_inc(rows_ready, 1)
            step(V.tensor_scalar(same, tr[0][:, 0:P], sub, None, ALU.is_equal))
            V.tensor_scalar(keq, tr[0][:, P:P + SLOTS], key, None, ALU.is_equal).then_inc(same_ready, 1)
            dve.wait_ge(same_ready, 1)
            dup_row, dup_key, rep, keep = small[:, 0:1], small[:, 1:2], small[:, 2:3], small[:, 3:4]
            junk = small[:, 16:80]
            step(V.tensor_tensor_reduce(out=junk, in0=same[:, 0:SLOTS], in1=earlier[:], scale=1.0, scalar=0.0,
                                        op0=ALU.mult, op1=ALU.max, accum_out=dup_row))
            step(V.tensor_tensor_reduce(out=junk, in0=keq, in1=earlier[:], scale=1.0, scalar=0.0,
                                        op0=ALU.mult, op1=ALU.max, accum_out=dup_key))
            step(V.scalar_tensor_tensor(rep, dup_row, 0.0, valid, ALU.is_equal, ALU.mult))
            step(V.tensor_tensor(rep, rep, fits, ALU.mult))
            step(V.scalar_tensor_tensor(keep, dup_key, 0.0, valid, ALU.is_equal, ALU.mult))
            dve.wait_ge(xobj_T, 1)
            V.tensor_copy(xoT, tr[2][:, :]).then_inc(xoT_ready, 1)
            dve.wait_ge(bias_loaded, 48)
            dve.wait_ge(q_done, 1)
            step(V.tensor_tensor(q, tr[1][:, :], bias[:, 0, :], ALU.add))
            dve.wait_ge(k_done, 1)
            step(V.tensor_tensor(kk, tr[2][:, :], bias[:, 1, :], ALU.add))
            V.tensor_tensor(q, q, kk, ALU.mult).then_inc(qk_read, 1)
            dve.wait_ge(qk_read, 1)
            sc = small[:, 4:12]
            step(V.reduce_sum(sc, q.rearrange("p (h d) -> p h d", h=HEADS), AX.X))
            gone = slot[:, 6:7]
            step(V.tensor_scalar(gone, keep, -1.0, -GONE, ALU.add, ALU.mult))
            step(V.tensor_scalar(sc, sc, 1.0 / np.sqrt(DK), keep, ALU.mult, ALU.mult))
            step(V.tensor_scalar(sc, sc, gone, None, ALU.add))
            V.tensor_tensor(spread[0:64].rearrange("p (h g) -> p h g", h=HEADS), eye.unsqueeze(1).broadcast_to([64, HEADS, SLOTS]),
                            sc[0:64].unsqueeze(2).broadcast_to([64, HEADS, SLOTS]), ALU.mult).then_inc(scores_ready, 1)
            step(V.tensor_scalar(keq, same[:, 0:SLOTS], -1.0, -GONE, ALU.add, ALU.mult))
            V.memset(score[:, :, SLOTS:SLOTS + 1], 0.0).then_inc(dve_step, 1)
            V.memset(score[:, :, SLOTS + 1:SLOTS + 2], TINY).then_inc(dve_step, 1)
            steps += 2
            step(V.tensor_copy(score[:, :, SLOTS + 2], sc))
            dve.wait_ge(scores_spread, 1)
            step(V.tensor_tensor(score[:, :, 0:SLOTS], tr[1][:, :].rearrange("p (h g) -> p h g", h=HEADS),
                                 keq.unsqueeze(1).broadcast_to([P, HEADS, SLOTS]), ALU.add))
            top = small[:, 16:24]
            step(V.reduce_max(top, score[:, :, 0:SLOTS + 2], AX.X))
            V.tensor_tensor(score, score, top.unsqueeze(2).broadcast_to([P, HEADS, EXTRA]), ALU.subtract).then_inc(exps_in, 1)
            dve.wait_ge(gsub_in, 16)
            dve.wait_ge(live_done, 1)
            off = gsub[:, H:H + 1]
            aii = gsub[:, H + 1:H + 2]
            plain = slot[:, 7:8]
            step(V.tensor_tensor(plain, off, tr[2][:, 0:1], ALU.subtract))
            b = small[:, 24:32]
            step(V.tensor_scalar(b[:, 0:1], off, A0, 1.0, ALU.mult, ALU.add))
            step(V.reciprocal(b[:, 1:2], b[:, 0:1]))
            step(V.tensor_scalar(b[:, 2:3], b[:, 1:2], A0, None, ALU.mult))
            step(V.tensor_tensor(b[:, 3:4], b[:, 2:3], aii, ALU.mult))
            step(V.scalar_tensor_tensor(b[:, 4:5], b[:, 1:2], 1.0, b[:, 3:4], ALU.add, ALU.subtract))
            step(V.tensor_scalar(b[:, 5:6], b[:, 2:3], 1.0 / XS, None, ALU.mult))
            step(V.tensor_scalar(kk, xsub, b[:, 4:5], None, ALU.mult))
            step(V.scalar_tensor_tensor(kk, gsub[:, 0:H], b[:, 5:6], kk, ALU.mult, ALU.add))
            norm_a, norm_b = st[:, 0], st[:, 1]
            moments(norm_a, kk).then_inc(slot_moments, 1)
            dve.wait_ge(exps_done, 1)
            sumf, z = small[:, 44:52], small[:, 52:60]
            step(V.reduce_sum(sumf, score[:, :, 0:SLOTS], AX.X))
            step(V.scalar_tensor_tensor(z, score[:, :, SLOTS], plain, sumf, ALU.mult, ALU.add))
            step(V.tensor_tensor(z, z, score[:, :, SLOTS + 1], ALU.add))
            step(V.reciprocal(z, z))
            share8 = score[:, :, SLOTS:SLOTS + 3]
            step(V.tensor_tensor(share8, share8, z.unsqueeze(2).broadcast_to([P, HEADS, 3]), ALU.mult))
            cdw = small[:, 60:63]
            step(V.reduce_sum(cdw, share8.rearrange("p h c -> p c h"), AX.X))
            step(V.tensor_scalar(cdw, cdw, 1.0 / HEADS, None, ALU.mult))
            vv = small[:, 63:64]
            step(V.tensor_tensor(vv, cdw[:, 2:3], cdw[:, 0:1], ALU.subtract))
            step(V.tensor_tensor(vv, vv, keep, ALU.mult))
            V.tensor_scalar(vsame[0:64], same[0:64], vv[0:64], None, ALU.mult).then_inc(shares_ready, 1)
            n = small[:, 64:68]
            step(V.tensor_tensor(n[:, 0:1], cdw[:, 0:1], aii, ALU.mult))
            step(V.scalar_tensor_tensor(n[:, 1:2], cdw[:, 1:2], 1.0, n[:, 0:1], ALU.add, ALU.subtract))
            step(V.tensor_scalar(n[:, 2:3], cdw[:, 0:1], 1.0 / XS, None, ALU.mult))
            step(V.tensor_scalar(q, xsub, n[:, 1:2], None, ALU.mult))
            step(V.scalar_tensor_tensor(q, gsub[:, 0:H], n[:, 2:3], q, ALU.mult, ALU.add))
            dve.wait_ge(mixed, 1)
            step(V.tensor_tensor(q, q, tr[2][:, :], ALU.add))
            moments(norm_b, q).then_inc(slot_moments, 1)
            dve.wait_ge(slot_root, 1)
            step(scale_shift(norm_a))
            step(V.tensor_scalar(kk, kk, norm_a[:, 8:9], norm_a[:, 9:10], ALU.mult, ALU.add))
            dve.wait_ge(slot_root, 2)
            step(scale_shift(norm_b))
            step(V.tensor_scalar(q, q, norm_b[:, 8:9], norm_b[:, 9:10], ALU.mult, ALU.add))
            step(V.tensor_tensor(dx1, q, kk, ALU.subtract))
            V.tensor_scalar(dx1, dx1, rep, None, ALU.mult).then_inc(change_ready, 1)
            dve.wait_ge(dT_hi, 1)
            V.scalar_tensor_tensor(dT[:, 1, :], tr[0][:, 0:KF * SLOTS], XS, dT[:, 0, :], ALU.mult, ALU.subtract).then_inc(dT_lo, 1)
            dve.wait_ge(right_hi, 1)
            V.scalar_tensor_tensor(stackR[64:P, 1, :], dx1[64:P, :], SS, stackR[64:P, 0, :], ALU.mult, ALU.subtract).then_inc(right_lo, 1)
            dve.wait_ge(right_hi, 2)
            V.scalar_tensor_tensor(stackR[0:64, 1, :], tr[1][0:64, :], SS / (XS * WS), stackR[0:64, 0, :],
                                   ALU.mult, ALU.subtract).then_inc(right_lo, 1)
            for t in range(T):
                dve.wait_ge(out_done, t + 1)
                dve.wait_ge(biased, t + 1)
                if t >= 4:
                    dve.wait_ge(out_stored[t % 4], 16 * (t // 4))
                if t >= 2:
                    dve.wait_ge(z_normed, t - 1)
                V.scalar_tensor_tensor(y4(t), acc[t % 5][:, :], 1.0 / SS, x_sb[:, t, :], ALU.mult, ALU.add).then_inc(z_ready, 1)
                dve.wait_ge(z_ready, t + 1)
                moments(st[:, t % 2], y4(t)).then_inc(z_moments, 1)
                if t >= 1:
                    dve.wait_ge(z_root, t)
                    scale_shift(st[:, (t - 1) % 2]).then_inc(z_stats, 1)
            dve.wait_ge(z_root, T)
            scale_shift(st[:, (T - 1) % 2]).then_inc(z_stats, 1)

        @block.tensor
        def _(pe):
            mm = nc.tensor.matmul

            def transpose_adj(t):
                pe.wait_ge(adj_loaded[t % RING], 16 * (t // RING + 1))
                for b in range(3):
                    if t >= 1:
                        pe.wait_ge(adjT_ready, 3 * (t - 1) + b + 1)
                    for k in range(4 * b, min(4 * b + 4, T)):
                        last = nc.tensor.transpose(tr[b][0:width[k], (k % 4) * P:(k % 4 + 1) * P],
                                                   stage[:, t % RING, k * P:k * P + width[k]], ident[:])
                    last.then_inc(adj_transposed, 1)

            pe.wait_ge(consts, 8)
            pe.wait_ge(tr_zeroed, 1)
            transpose_adj(0)
            transpose_adj(1)
            for i in range(T + 1):
                if i < T:
                    pe.wait_ge(adjT_ready, 3 * (i + 1))
                    if i >= 2:
                        pe.wait_ge(y_ready, i - 1)
                    for k in range(T):
                        if i == 0 and k % 3 == 0:
                            pe.wait_ge(x_lo, min(k // 3 + 1, 4))
                        for half in range(2):
                            last = mm(acc[i % 2][:, :], adjT[0:width[k], k, i * P:(i + 1) * P], xs[0:width[k], half, k, :],
                                      start=(k == 0 and half == 0), stop=(k == T - 1 and half == 1))
                    last.then_inc(sums_done, 1)
                if i >= 1:
                    pe.wait_ge(x1_ready, i)
                    if i >= 2:
                        pe.wait_ge(x1T_lo, i - 1)
                    for k in range(KF):
                        last = nc.tensor.transpose(acc[4][:, k * P:(k + 1) * P], x_sb[:, i - 1, k * P:(k + 1) * P], ident[:])
                    last.then_inc(x1_transposed, 1)
                if i + 2 < T:
                    transpose_adj(i + 2)
                if i - 1 in CHUNK_AT:
                    compact(pe, CHUNK_AT.index(i - 1))
                if i in CHUNK_AT:
                    number(pe, CHUNK_AT.index(i))
                if i >= 1:
                    pe.wait_ge(x1T_lo, i)
                    pe.wait_ge(w1_lo, 1)
                    if i >= 2:
                        pe.wait_ge(support_lo, i - 1)
                    for k in range(KF):
                        for n, (a, b) in enumerate(((0, 0), (0, 1), (1, 0))):
                            last = mm(acc[2][:, :], x1T[:, (i - 1) % 2, a, k * P:(k + 1) * P], whl[:, b, k, :],
                                      start=(k == 0 and n == 0), stop=(k == KF - 1 and n == 2))
                    last.then_inc(support_done, 1)
            pe.wait_ge(wqk_loaded, 32)
            pe.wait_ge(y_ready, T)
            pe.wait_ge(support_lo, T)
            for n in range(8):
                if n >= 4:
                    pe.wait_ge(wqkT_ready, n - 3)
                for k in range(KF):
                    last = nc.tensor.transpose(acc[WB[n % 4]][:, k * P:(k + 1) * P],
                                               wraw[:, n // 4, k, (n % 4) * P:(n % 4 + 1) * P], ident[:])
                last.then_inc(wqk_transposed, 1)
            number(pe, 3)
            compact(pe, 3)
            with overflow(pe):
                general_pe(pe)

            def base(t):
                if t >= 5:
                    pe.wait_ge(z_ready, t - 4)
                elif t == 3:
                    pe.wait_ge(slot_idx_ready, 1)
                else:
                    pe.wait_ge(wqkT_ready, 5 + WB.index(t))
                for k in range(T):
                    for half in range(2):
                        mm(acc[t % 5][:, :], adjT[0:width[k], k, t * P:(t + 1) * P], ss[0:width[k], half, k, :],
                           start=(k == 0 and half == 0), stop=False)

            def cols(n):
                lo, hi = 512 * n, min(512 * n + 512, NP)
                for k in range(T):
                    last = mm(tr[0][0:64, 0:hi - lo], slot_row[0:width[k], k, :], adjT[0:width[k], k, lo:hi],
                              start=(k == 0), stop=(k == T - 1))
                last.then_inc(cols_done, 1)

            base(0)
            pe.wait_ge(spread_ready, 1)
            mm(tr[0][:, 0:192], ones[0:64, :], spread[0:64, 0:192], start=True, stop=True).then_inc(subs_spread, 1)
            pe.wait_ge(xsub_in, 16)
            for k in range(KF):
                last = nc.tensor.transpose(tr[1][:, k * P:(k + 1) * P], xsub[:, k * P:(k + 1) * P], ident[:])
            last.then_inc(xsub_T, 1)
            pe.wait_ge(xobj_in, 16)
            pe.wait_ge(slot_idx_ready, 1)
            for k in range(KF):
                last = nc.tensor.transpose(tr[2][:, k * P:(k + 1) * P], xobj[:, k * P:(k + 1) * P], ident[:])
            last.then_inc(xobj_T, 1)
            pe.wait_ge(rows_ready, 1)
            pe.wait_ge(same_ready, 1)
            cols(0)
            base(1)
            pe.wait_ge(xsT_ready, 1)
            for k in range(KF):
                last = mm(tr[1][:, :], xsT[:, k * P:(k + 1) * P], wT[:, 0, k, :], start=(k == 0), stop=(k == KF - 1))
            last.then_inc(q_done, 1)
            pe.wait_ge(xoT_ready, 1)
            for k in range(KF):
                last = mm(tr[2][:, :], xoT[:, k * P:(k + 1) * P], wT[:, 1, k, :], start=(k == 0), stop=(k == KF - 1))
            last.then_inc(k_done, 1)
            pe.wait_ge(cols_copied, 1)
            cols(1)
            base(2)
            pe.wait_ge(scores_ready, 1)
            mm(tr[1][:, :], ones[0:64, :], spread[0:64, :], start=True, stop=True).then_inc(scores_spread, 1)
            mm(tr[2][:, 0:1], same[0:64, :], small[0:64, 3:4], start=True, stop=True).then_inc(live_done, 1)
            pe.wait_ge(cols_copied, 2)
            cols(2)
            base(3)
            pe.wait_ge(shares_ready, 1)
            mm(tr[2][:, :], vsame[0:64, :], xobj[0:64, :], start=True, stop=True).then_inc(mixed, 1)
            base(4)
            pe.wait_ge(change_ready, 1)
            pe.wait_ge(cols_copied, 3)
            for k in range(KF):
                last = nc.tensor.transpose(tr[0][:, k * SLOTS:(k + 1) * SLOTS], dx1[0:64, k * P:(k + 1) * P], ident[0:64, 0:64])
            last.then_inc(change_T, 1)
            pe.wait_ge(dT_lo, 1)
            for k in range(KF):
                for n, (a, b) in enumerate(((0, 0), (0, 1), (1, 0))):
                    last = mm(tr[1][0:64, :], dT[:, a, k * SLOTS:(k + 1) * SLOTS], whl[:, b, k, :],
                              start=(k == 0 and n == 0), stop=(k == KF - 1 and n == 2))
            last.then_inc(dS_done, 1)
            pe.wait_ge(low_ready, 1)
            pe.wait_ge(right_hi, 2)
            pe.wait_ge(right_lo, 2)

            def close(t):
                mm(acc[t % 5][:, :], stackL[:, t * P:(t + 1) * P], stackR[:, 0, :], start=False, stop=False)
                mm(acc[t % 5][:, :], stackL[:, t * P:(t + 1) * P], stackR[:, 1, :], start=False, stop=True).then_inc(out_done, 1)

            for t in range(5):
                close(t)
            for t in range(5, T):
                base(t)
                close(t)


_INS = ['x', 'adj', 'L0_gnn_rel_pair_index', 'L0_gnn_Wq', 'L0_gnn_bq', 'L0_gnn_Wk', 'L0_gnn_bk', 'L1_gnn_weight', 'L1_gnn_bias']


def kernel(**inputs):
    import numpy as _np
    import concourse.bacc as _bacc
    from concourse import mybir as _mybir
    from concourse.bass_utils import run_bass_kernel_spmd as _run

    nc = _bacc.Bacc("TRN2", target_bir_lowering=False, num_devices=1)
    arrays, args = {}, []
    for name in _INS:
        a = _np.ascontiguousarray(inputs[name])
        arrays[f"in_{name}"] = a
        args.append(nc.dram_tensor(f"in_{name}", a.shape, _mybir.dt.from_np(a.dtype), kind="ExternalInput").ap())
    args.append(nc.dram_tensor("out_0", (N, H), _mybir.dt.float32, kind="ExternalOutput").ap())
    resnorm_graph(nc, *args)
    r = _run(nc, [arrays], core_ids=[0])
    return r.results[0]["out_0"]
```

```python
import numpy as np
import concourse.bass as bass
from concourse import mybir
from contextlib import ExitStack

N = 1354
H = 512
E = 10000
HEADS = 8
DK = H // HEADS
P = 128
T = (N + P - 1) // P
LAST = N - (T - 1) * P
NP = T * P
KF = H // P
EP = 125
EC = E // EP
SLOTS = 64
CHUNK = 9
CHUNKS = list(range(0, EC, CHUNK)) + [EC]
NC = len(CHUNKS) - 1
OUTS = 6
RING = 2
GW = H + 2
XS = 64.0
WS = 256.0
SS = 256.0
TINY = float(np.float32(1e-7))
A0 = float(np.float32(np.exp(-1e-7)))
EPS = 1e-5
FAR = 4096.0
GONE = -1e30


def resnorm_graph(nc, x, adj, pairs, wq, bq, wk, bk, w1, b1, out):
    f32, f16, i32 = mybir.dt.float32, mybir.dt.float16, mybir.dt.int32
    ALU, ACT, AX = mybir.AluOpType, mybir.ActivationFunctionType, mybir.AxisListType
    width = [P] * (T - 1) + [LAST]

    with ExitStack() as ctx:
        def sb(name, shape, dt=f32):
            return ctx.enter_context(nc.sbuf_tensor(name, shape, dt))

        def sem(name):
            return ctx.enter_context(nc.semaphore(name))

        sums_dram = nc.dram_tensor("sums_dram", [NP, GW], f32, kind="Internal").ap()
        live_map = nc.dram_tensor("live_map", [N, N], f32, kind="Internal").ap()
        live_flat = live_map.rearrange("i (j o) -> (i j) o", o=1)
        adj_flat = adj.rearrange("i (j o) -> (i j) o", o=1)

        x_sb = sb("x_sb", [P, T, H])
        xs = sb("xs", [P, 2, T, H], f16)
        ss = sb("ss", [P, 2, T, H], f16)
        adjT = sb("adjT", [P, T, NP], f16)
        stage = sb("stage", [P, RING, N])
        adj16 = sb("adj16", [P, RING, N], f16)
        sums = sb("sums", [P, 3, GW])
        wraw = sb("wraw", [P, 3, KF, H])
        wT = sb("wT", [P, 2, KF, H])
        whl = sb("whl", [P, 2, KF, H], f16)
        bias = sb("bias", [P, 3, H])
        x1T = sb("x1T", [P, 2, 2, H], f16)
        xd = sb("xd", [P, 2, H])
        y = sb("y", [P, 2, H])
        co = sb("co", [P, 2, 8])
        st = sb("st", [P, 2, 12])
        onehot = sb("onehot", [P, 2 * NP], f16)
        stackL = sb("stackL", [P, NP], f16)
        stackR = sb("stackR", [P, 2, H], f16)

        ident = sb("ident", [P, P])
        ident16 = sb("ident16", [P, P], f16)
        ones = sb("ones", [P, P])
        ones16 = sb("ones16", [P, P], f16)
        below16 = sb("below16", [P, P], f16)
        slot_no = sb("slot_no", [P, P])
        earlier = sb("earlier", [P, SLOTS])
        col_no = sb("col_no", [P, NP], f16)
        eps = sb("eps", [P, 1])
        junk16 = sb("junk16", [P, P], f16)
        row_no = sb("row_no", [P, T])

        ed_i = sb("ed_i", [P, EC, 2], i32)
        ed = sb("ed", [P, EC, 2])
        ok2 = sb("ok2", [P, EC, 2])
        ed_ok = sb("ed_ok", [P, EC])
        ed_in = sb("ed_in", [P, EC])
        ed_lin = sb("ed_lin", [P, EC])
        ed_idx = sb("ed_idx", [P, EC], i32)
        ed_adj = sb("ed_adj", [P, EC])
        ed3 = sb("ed3", [P, EC, 3], f16)
        flag = sb("flag", [P, EC], f16)
        seen = sb("seen", [P, EC])
        pos = sb("pos", [P, 3, CHUNK])
        pos_all = seen[0:EP]
        slot = sb("slot", [P, 16])
        slot_i = sb("slot_i", [P, 2], i32)
        count_i = sb("count_i", [P, 1], i32)

        raw = wraw[:, :, :, :].rearrange("p a b c -> p (a b c)")
        at = 2 * KF * H

        def take(n):
            nonlocal at
            at += n
            return raw[:, at - n:at]
        xsub, xobj, spread, same, keq, vsame, small = map(take, (H, H, H, P, SLOTS, P, 80))
        assert at <= 3 * KF * H
        at = 0
        EXTRA = SLOTS + 3
        gsub, xsT, xoT, q, kk, dx1 = map(take, (GW, H, H, H, H, H))
        score = take(HEADS * EXTRA).rearrange("p (h g) -> p h g", h=HEADS)
        assert at <= 2 * KF * H
        slot_row = sb("slot_row", [P, T, SLOTS], f16)
        dT = x1T[:, 0, :, 0:KF * SLOTS]

        d_adj, d_live, d_mask, d_score = (raw[:, n * N:(n + 1) * N] for n in range(4))
        d_x = raw[:, 4 * N:4 * N + H]
        flat_stage = stage[:, :, :].rearrange("p r n -> p (r n)")
        d_prob, d_share = flat_stage[:, 0:N], flat_stage[:, N:2 * N]
        d_shareT = onehot[:, :].bitcast(f32).rearrange("p (k i) -> p k i", k=T)
        d_xT, d_qT = y[:, 0, :], y[:, 1, :]
        d_x1, d_y = xd[:, 0, :], xd[:, 1, :]
        x32 = xs[:, :, :, :].rearrange("p a t h -> p (a t h)").bitcast(f32).rearrange("p (t h) -> p t h", t=T)
        kT = ss[:, :, :, :].rearrange("p a t h -> p (a t h)").bitcast(f32).rearrange("p (k i) -> p k i", k=KF)
        bias_col = sb("bias_col", [P, 2, KF])
        d_no = sb("d_no", [P, 1])
        d_st = sb("d_st", [P, 12])
        d_s = sb("d_s", [P, 24])

        tr = [ctx.enter_context(nc.psum_tensor(f"tr{i}", [P, 512], f32)) for i in range(3)]
        tr16 = [b[:, :].bitcast(f16) for b in tr]
        acc = [ctx.enter_context(nc.psum_tensor(f"acc{i}", [P, 512], f32)) for i in range(5)]
        PRE, TOT, CMP = 0, 16, 32

        edges_loaded, w1_loaded, wqk_loaded, bias_loaded = map(sem, ("edges_loaded", "w1_loaded", "wqk_loaded", "bias_loaded"))
        x_loaded = [sem(f"x_loaded{i}") for i in range(4)]
        adj_loaded = [sem(f"adj_loaded{i}") for i in range(RING)]
        sums_stored = [sem(f"sums_stored{i}") for i in range(3)]
        edges_looked_up = [sem(f"edges_looked_up{i}") for i in range(NC)]
        pad_zeroed, tr_zeroed, consts = sem("pad_zeroed"), sem("tr_zeroed"), sem("consts")
        dve_step, pool_step = sem("dve_step"), sem("pool_step")
        x_hi, x_lo, w1_hi, w1_lo = map(sem, ("x_hi", "x_lo", "w1_hi", "w1_lo"))
        adj_cast, adj_transposed, adjT_ready, adj_read = map(sem, ("adj_cast", "adj_transposed", "adjT_ready", "adj_read"))
        sums_done, sums_copied, coefs_ready, xd_ready = map(sem, ("sums_done", "sums_copied", "coefs_ready", "xd_ready"))
        y_ready, stats_ready, x1_ready, x1_transposed = map(sem, ("y_ready", "stats_ready", "x1_ready", "x1_transposed"))
        x1T_hi, x1T_lo, support_done, support_hi, support_lo = map(sem, ("x1T_hi", "x1T_lo", "support_done", "support_hi", "support_lo"))
        moments_ready, root_ready, slot_moments, slot_root, z_moments, z_root = map(sem, ("moments_ready", "root_ready", "slot_moments", "slot_root", "z_moments", "z_root"))
        idx_ready, flags_ready, numbered, onehot_ready, compacted = map(sem, ("idx_ready", "flags_ready", "numbered", "onehot_ready", "compacted"))
        wqk_transposed, wqkT_ready, count_ready = map(sem, ("wqk_transposed", "wqkT_ready", "count_ready"))
        slot_idx_ready, xsub_in, xobj_in, gsub_in = map(sem, ("slot_idx_ready", "xsub_in", "xobj_in", "gsub_in"))
        spread_ready, subs_spread, same_ready, rows_ready = map(sem, ("spread_ready", "subs_spread", "same_ready", "rows_ready"))
        xsub_T, xobj_T, xsT_ready, xoT_ready, q_done, k_done = map(sem, ("xsub_T", "xobj_T", "xsT_ready", "xoT_ready", "q_done", "k_done"))
        cols_done, cols_copied, scores_ready, scores_spread = map(sem, ("cols_done", "cols_copied", "scores_ready", "scores_spread"))
        live_done, exps_in, exps_done, shares_ready, mixed = map(sem, ("live_done", "exps_in", "exps_done", "shares_ready", "mixed"))
        qk_read, change_ready, change_T, dT_hi, dT_lo = map(sem, ("qk_read", "change_ready", "change_T", "dT_hi", "dT_lo"))
        dS_done, right_hi, right_lo, low_ready = map(sem, ("dS_done", "right_hi", "right_lo", "low_ready"))
        biased, out_done, z_ready, z_stats, z_normed = map(sem, ("biased", "out_done", "z_ready", "z_stats", "z_normed"))
        map_clear, map_idx_ready, map_zeroed, map_marked = map(sem, ("map_clear", "map_idx_ready", "map_zeroed", "map_marked"))
        general_in, rows_in, general_step = map(sem, ("general_in", "rows_in", "general_step"))
        turn = sem("turn")
        out_stored = [sem(f"out_stored{i}") for i in range(4)]

        block = ctx.enter_context(nc.Block())

        def rows(ap2d, t):
            return ap2d[t * P:t * P + width[t], :]

        KEYS = 1
        KEY_TURNS = 5
        ROWS = KEYS + T * KEY_TURNS
        HEAD_TURNS = 4
        TAIL = 5 + HEADS * HEAD_TURNS
        ROW_TURNS = TAIL + 9
        SUPPORT = ROWS + T * ROW_TURNS
        SUPPORT_TURNS = 7
        FINISHED = SUPPORT + T * SUPPORT_TURNS
        ROW_STEPS = 7 + HEADS * 11 + 3 + 3
        SPANS = [(0, 512), (512, 1024), (1024, N)]

        def overflow(eng):
            eng.wait_ge(count_ready, 1)
            return eng.If(eng.value_load(count_i[0:1, 0:1], min_val=0, max_val=E) > SLOTS)

        def general_sp(sp):
            sp.wait_ge(turn, KEYS)
            for n, b in enumerate((bq, bk)):
                for k in range(KF):
                    sp.dma_start(bias_col[:, n, k:k + 1], b[k * P:(k + 1) * P].rearrange("(p o) -> p o", o=1)).then_inc(general_in, 16)
            for t in range(T):
                sp.dma_start(x32[0:width[t], t, :], rows(x, t)).then_inc(general_in, 16)
            sp.wait_ge(map_clear, 1)
            for t in range(T):
                sp.dma_start(rows(live_map, t), d_adj[0:width[t]]).then_inc(map_zeroed, 16)
            sp.wait_ge(map_marked, 16 * EC)
            for t in range(T):
                sp.wait_ge(turn, ROWS + t * ROW_TURNS)
                sp.dma_start(d_adj[0:width[t]], rows(adj, t)).then_inc(rows_in, 16)
                sp.dma_start(d_live[0:width[t]], rows(live_map, t)).then_inc(rows_in, 16)
            sp.wait_ge(turn, FINISHED)

        def general_pool(pool):
            pool.wait_ge(map_idx_ready, 1)
            pool.wait_ge(map_zeroed, 16 * T)
            for c in range(EC):
                nc.gpsimd.indirect_dma_start(
                    out=live_flat, out_offset=bass.IndirectOffsetOnAxis(ap=ed_idx[0:EP, c:c + 1], axis=0),
                    in_=ones[0:EP, 0:1], in_offset=None, bounds_check=N * N - 1, oob_is_err=False).then_inc(map_marked, 16)
                pool.wait_ge(map_marked, 16 * (c + 1))
            pool.wait_ge(turn, FINISHED)

        def general_pe(pe):
            mm = nc.tensor.matmul
            with pe.Fori(0, T) as t:
                at = KEYS + t * KEY_TURNS
                pe.wait_ge(turn, at + 1)
                for k in range(KF):
                    last = nc.tensor.transpose(tr[0][:, k * P:(k + 1) * P], d_x[:, k * P:(k + 1) * P], ident[:])
                last.then_inc(turn, 1)
                pe.wait_ge(turn, at + 3)
                for o in range(KF):
                    for k in range(KF):
                        last = mm(tr[1][:, o * P:(o + 1) * P], wT[:, 1, k, o * P:(o + 1) * P], d_xT[:, k * P:(k + 1) * P],
                                  start=(k == 0), stop=(k == KF - 1))
                last.then_inc(turn, 1)
            with pe.Fori(0, T) as t:
                at = ROWS + t * ROW_TURNS
                pe.wait_ge(turn, at + 1)
                for k in range(KF):
                    last = nc.tensor.transpose(tr[0][:, k * P:(k + 1) * P], d_x[:, k * P:(k + 1) * P], ident[:])
                last.then_inc(turn, 1)
                pe.wait_ge(turn, at + 3)
                for o in range(KF):
                    for k in range(KF):
                        last = mm(tr[1][:, o * P:(o + 1) * P], wT[:, 0, k, o * P:(o + 1) * P], d_xT[:, k * P:(k + 1) * P],
                                  start=(k == 0), stop=(k == KF - 1))
                last.then_inc(turn, 1)
                for h in range(HEADS):
                    lo, o = DK * (h % 2), h // 2
                    pe.wait_ge(turn, at + 5 + HEAD_TURNS * h)
                    for b, (i, j) in enumerate(SPANS):
                        last = mm(acc[b][:, 0:j - i], d_qT[lo:lo + DK, o * P:(o + 1) * P], kT[lo:lo + DK, o, i:j],
                                  start=True, stop=True)
                    last.then_inc(turn, 1)
                pe.wait_ge(turn, at + TAIL + 1)
                for k in range(T):
                    last = nc.tensor.transpose(tr[k // 4][0:width[k], (k % 4) * P:(k % 4 + 1) * P],
                                               d_share[:, k * P:k * P + width[k]], ident[:])
                last.then_inc(turn, 1)
                pe.wait_ge(turn, at + TAIL + 3)
                for k in range(T):
                    last = mm(acc[3][:, :], d_shareT[0:width[k], k, :], x32[0:width[k], k, :], start=(k == 0), stop=(k == T - 1))
                last.then_inc(turn, 1)
            with pe.Fori(0, T) as t:
                at = SUPPORT + t * SUPPORT_TURNS
                pe.wait_ge(turn, at + 1)
                for k in range(KF):
                    last = nc.tensor.transpose(tr[0][:, k * P:(k + 1) * P], d_x1[:, k * P:(k + 1) * P], ident[:])
                last.then_inc(turn, 1)
                pe.wait_ge(turn, at + 4)
                for k in range(KF):
                    for n, (a, b) in enumerate(((0, 0), (0, 1), (1, 0))):
                        last = mm(tr[1][:, :], x1T[:, 0, a, k * P:(k + 1) * P], whl[:, b, k, :],
                                  start=(k == 0 and n == 0), stop=(k == KF - 1 and n == 2))
                last.then_inc(turn, 1)
            pe.wait_ge(turn, FINISHED)

        def general_act(act):
            A = nc.scalar
            act.wait_ge(general_in, 16 * (2 * KF + T))
            with act.Fori(0, T) as t:
                at = KEYS + t * KEY_TURNS
                act.wait_ge(turn, at + 2)
                A.copy(d_xT, tr[0][:, :]).then_inc(turn, 1)
                act.wait_ge(turn, at + 4)
                for o in range(KF):
                    last = A.activation(kT[:, o, bass.ts(t, P)], tr[1][:, o * P:(o + 1) * P], ACT.Identity, bias=bias_col[:, 1, o:o + 1])
                last.then_inc(turn, 1)
            with act.Fori(0, T) as t:
                at = ROWS + t * ROW_TURNS
                act.wait_ge(turn, at + 2)
                A.copy(d_xT, tr[0][:, :]).then_inc(turn, 1)
                act.wait_ge(turn, at + 4)
                for o in range(KF):
                    last = A.activation(d_qT[:, o * P:(o + 1) * P], tr[1][:, o * P:(o + 1) * P], ACT.Identity, bias=bias_col[:, 0, o:o + 1])
                last.then_inc(turn, 1)
                for h in range(HEADS):
                    act.wait_ge(turn, at + 5 + HEAD_TURNS * h + 2)
                    A.activation(d_prob, d_score, ACT.Exp, bias=d_s[:, 4:5], accum_out=d_s[:, 7:8])
                    A.activation(d_s[:, 8:10], d_s[:, 5:7], ACT.Exp).then_inc(turn, 1)
                act.wait_ge(turn, at + TAIL + 2)
                for b in range(3):
                    n = min(4, T - 4 * b)
                    last = A.copy(d_shareT[:, 4 * b:4 * b + n, :], tr[b][:, 0:n * P].rearrange("p (k i) -> p k i", k=n))
                last.then_inc(turn, 1)
                act.wait_ge(turn, at + TAIL + 5)
                A.activation(d_st[:, 10:11], d_st[:, 7:8], ACT.Sqrt, bias=eps[:]).then_inc(turn, 1)
                act.wait_ge(turn, at + TAIL + 7)
                A.activation(d_x1, d_y, ACT.Identity, bias=d_st[:, 9:10], scale=d_st[:, 8:9]).then_inc(turn, 1)
            with act.Fori(0, T) as t:
                at = SUPPORT + t * SUPPORT_TURNS
                act.wait_ge(turn, at + 2)
                A.mul(x1T[:, 0, 0, :], tr[0][:, :], XS).then_inc(turn, 1)
                act.wait_ge(turn, at + 5)
                A.mul(ss[:, 0, bass.ds(t, 1), :].rearrange("p o h -> p (o h)"), tr[1][:, :], SS / (XS * WS)).then_inc(turn, 1)
            act.wait_ge(turn, FINISHED)

        def general_dve(dve):
            V = nc.vector
            done = 0
            k = 0
            base = 0

            def step(ins):
                nonlocal k
                k += 1
                ins.then_inc(general_step, 1)
                dve.wait_ge(general_step, base + k)

            dve.wait_ge(wqkT_ready, 8)
            dve.wait_ge(compacted, NC)
            dve.wait_ge(support_lo, T)
            dve.wait_ge(bias_loaded, 48)
            for b in range(3):
                dve.wait_ge(sums_stored[b], 16 * len(range(b, T, 3)))
            step(V.tensor_scalar(pos_all, flag[0:EP], -float(N * N), float(N * N), ALU.mult, ALU.add))
            step(V.tensor_tensor(pos_all, pos_all, ed_lin[0:EP], ALU.add))
            V.tensor_copy(ed_idx[0:EP], pos_all).then_inc(map_idx_ready, 1)
            V.memset(d_adj, 0.0).then_inc(map_clear, 1)
            V.memset(d_live, 0.0).then_inc(turn, 1)
            dve.wait_ge(general_in, 16 * (2 * KF + T))
            done = k
            with dve.Fori(0, T) as t:
                at = KEYS + t * KEY_TURNS
                dve.wait_ge(turn, at)
                V.tensor_copy(d_x, x32[:, bass.ds(t, 1), :].rearrange("p o h -> p (o h)")).then_inc(turn, 1)
            s = d_s
            with dve.Fori(0, T) as t:
                base = done + t * ROW_STEPS
                k = 0
                at = ROWS + t * ROW_TURNS
                dve.wait_ge(turn, at)
                dve.wait_ge(rows_in, t * 32 + 32)
                V.tensor_copy(d_x, x32[:, bass.ds(t, 1), :].rearrange("p o h -> p (o h)"))
                step(V.tensor_copy(d_no[:], row_no[:, bass.ds(t, 1)]))
                step(V.reduce_sum(s[:, 0:1], d_adj, AX.X))
                step(V.reduce_sum(s[:, 1:2], d_live, AX.X))
                step(V.scalar_tensor_tensor(d_mask, col_no[:, 0:N], d_no[:], d_adj, ALU.is_equal, ALU.mult, accum_out=s[:, 2:3]))
                step(V.tensor_tensor(s[:, 0:1], s[:, 0:1], s[:, 1:2], ALU.subtract))
                step(V.tensor_tensor(s[:, 3:4], s[:, 0:1], s[:, 2:3], ALU.subtract))
                step(V.memset(s[:, 12:14], 0.0))
                V.tensor_scalar(d_mask, d_live, -1.0, -GONE, ALU.add, ALU.mult).then_inc(turn, 1)
                for h in range(HEADS):
                    here = at + 5 + HEAD_TURNS * h
                    dve.wait_ge(turn, here + 1)
                    for b, (i, j) in enumerate(SPANS):
                        step(V.scalar_tensor_tensor(d_score[:, i:j], acc[b][:, 0:j - i], 1.0 / float(np.sqrt(DK)), d_mask[:, i:j],
                                                    ALU.mult, ALU.add))
                    step(V.reduce_max(s[:, 10:11], d_score, AX.X))
                    step(V.tensor_scalar(s[:, 4:5], s[:, 10:11], TINY, -1.0, ALU.max, ALU.mult))
                    step(V.tensor_scalar(s[:, 5:6], s[:, 4:5], 1.0, None, ALU.mult))
                    V.tensor_scalar(s[:, 6:7], s[:, 4:5], TINY, None, ALU.add).then_inc(turn, 1)
                    dve.wait_ge(turn, here + 3)
                    step(V.scalar_tensor_tensor(s[:, 11:12], s[:, 8:9], s[:, 3:4], s[:, 7:8], ALU.mult, ALU.add))
                    step(V.tensor_tensor(s[:, 11:12], s[:, 11:12], s[:, 9:10], ALU.add))
                    step(V.reciprocal(s[:, 14:15], s[:, 11:12]))
                    step(V.tensor_scalar(s[:, 14:15], s[:, 14:15], 1.0 / HEADS, None, ALU.mult))
                    step(V.scalar_tensor_tensor(s[:, 12:14], s[:, 8:10], s[:, 14:15], s[:, 12:14], ALU.mult, ALU.add))
                    if h == 0:
                        ins = V.tensor_scalar(d_share, d_prob, s[:, 14:15], None, ALU.mult)
                    else:
                        ins = V.scalar_tensor_tensor(d_share, d_prob, s[:, 14:15], d_share, ALU.mult, ALU.add)
                    ins.then_inc(turn, 1)
                dve.wait_ge(turn, at + TAIL)
                step(V.tensor_tensor(d_live, d_adj, d_live, ALU.subtract))
                step(V.tensor_tensor(s[:, 15:16], s[:, 12:13], s[:, 2:3], ALU.mult))
                step(V.scalar_tensor_tensor(s[:, 16:17], s[:, 13:14], 1.0, s[:, 15:16], ALU.add, ALU.subtract))
                V.scalar_tensor_tensor(d_share, d_live, s[:, 12:13], d_share, ALU.mult, ALU.add).then_inc(turn, 1)
                dve.wait_ge(turn, at + TAIL + 4)
                step(V.scalar_tensor_tensor(d_y, d_x, s[:, 16:17], acc[3][:, :], ALU.mult, ALU.add))
                step(V.bn_stats(d_st[:, 0:6], d_y))
                V.tensor_copy(s[:, 17:18], s[:, 16:17])
                V.bn_aggr(d_st[:, 6:8], d_st[:, 0:6]).then_inc(turn, 1)
                dve.wait_ge(turn, at + TAIL + 6)
                step(V.reciprocal(d_st[:, 8:9], d_st[:, 10:11]))
                V.tensor_scalar(d_st[:, 9:10], d_st[:, 6:7], -1.0, d_st[:, 8:9], ALU.mult, ALU.mult).then_inc(turn, 1)
                dve.wait_ge(turn, at + TAIL + 8)
                V.tensor_copy(x_sb[:, bass.ds(t, 1), :].rearrange("p o h -> p (o h)"), d_x1).then_inc(turn, 1)
                assert k == ROW_STEPS, k
            with dve.Fori(0, T) as t:
                at = SUPPORT + t * SUPPORT_TURNS
                dve.wait_ge(turn, at)
                V.tensor_copy(d_x1, x_sb[:, bass.ds(t, 1), :].rearrange("p o h -> p (o h)")).then_inc(turn, 1)
                dve.wait_ge(turn, at + 3)
                V.scalar_tensor_tensor(x1T[:, 0, 1, :], tr[0][:, :], XS, x1T[:, 0, 0, :], ALU.mult, ALU.subtract).then_inc(turn, 1)
                dve.wait_ge(turn, at + 6)
                V.scalar_tensor_tensor(ss[:, 1, bass.ds(t, 1), :].rearrange("p o h -> p (o h)"), tr[1][:, :], SS / (XS * WS),
                                       ss[:, 0, bass.ds(t, 1), :].rearrange("p o h -> p (o h)"), ALU.mult, ALU.subtract).then_inc(turn, 1)
            dve.wait_ge(turn, FINISHED)

        def out_bank(t):
            return (acc + [tr[1]])[t % OUTS]

        def wqk_at(i):
            return range(3 * (i - T + 2), min(3 * (i - T + 3), 8)) if T - 2 <= i <= T else ()

        def y4(t):
            return (y if t % 4 < 2 else xd)[:, t % 2, :]

        def number(pe, n):
            a, b = CHUNKS[n], CHUNKS[n + 1]
            pe.wait_ge(flags_ready, n + 1)
            nc.tensor.matmul(acc[3][:, PRE:PRE + b - a], below16[0:EP, :], flag[0:EP, a:b], start=True, stop=True)
            nc.tensor.matmul(acc[3][:, TOT:TOT + b - a], ones16[0:EP, :], flag[0:EP, a:b], start=True, stop=True).then_inc(numbered, 1)

        def compact(pe, n):
            a, b = CHUNKS[n], CHUNKS[n + 1]
            pe.wait_ge(onehot_ready, n + 1)
            for c in range(a, b):
                last = nc.tensor.matmul(acc[3][:, CMP + 3 * n:CMP + 3 * n + 3], onehot[0:EP, (c - a) * P:(c - a + 1) * P], ed3[0:EP, c, :],
                                        start=(c == a), stop=(c == b - 1))
            last.then_inc(compacted, 1)

        @block.sync
        def _(sp):
            sp.dma_start(ed_i[0:EP], pairs.rearrange("(p c) two -> p c two", p=EP)).then_inc(edges_loaded, 16)
            for g in range(3):
                sp.dma_start(x_sb[:, 3 * g:3 * g + 3, :],
                             x[3 * g * P:(3 * g + 3) * P, :].rearrange("(t p) h -> p t h", p=P)).then_inc(x_loaded[g], 16)
                if g < 2:
                    sp.dma_start(stage[:, g, :], rows(adj, g)).then_inc(adj_loaded[g], 16)
            sp.dma_start(x_sb[:, 9, :], rows(x, 9)).then_inc(x_loaded[3], 16)
            sp.wait_ge(pad_zeroed, 1)
            sp.dma_start(x_sb[0:LAST, T - 1, :], rows(x, T - 1)).then_inc(x_loaded[3], 16)
            sp.dma_start(wraw[:, 2], w1.rearrange("(k p) o -> p k o", p=P)).then_inc(w1_loaded, 16)

            for t in range(2, T):
                if t >= RING:
                    sp.wait_ge(adj_cast, t - RING + 1)
                sp.dma_start(stage[0:width[t], t % RING, :], rows(adj, t)).then_inc(adj_loaded[t % RING], 16)
                if t in (5, 7):
                    sp.dma_start(wraw[:, t // 6], (wq, wk)[t // 6].rearrange("(k p) i -> p k i", p=P)).then_inc(wqk_loaded, 16)
                if t == 9:
                    for n, b in enumerate((bq, bk, b1)):
                        sp.dma_start(bias[:, n, :], b.partition_broadcast(P)).then_inc(bias_loaded, 16)
            with overflow(sp):
                general_sp(sp)
            for t in range(T):
                sp.wait_ge(z_normed, t + 1)
                sp.dma_start(rows(out, t), y4(t)[0:width[t]]).then_inc(out_stored[t % 4], 16)
            for b in range(4):
                sp.wait_ge(out_stored[b], 16 * len(range(b, T, 4)))

        @block.gpsimd
        def _(pool):
            nc.gpsimd.memset(x_sb[64:P, T - 1, :], 0.0).then_inc(pad_zeroed, 1)
            pool.wait_ge(pad_zeroed, 1)
            nc.gpsimd.memset(eps[:], EPS).then_inc(consts, 1)
            nc.gpsimd.memset(ident[:], 0.0).then_inc(pool_step, 1)
            nc.gpsimd.memset(ones[:], 1.0).then_inc(pool_step, 1)
            nc.gpsimd.memset(ones16[:], 1.0).then_inc(pool_step, 1)
            nc.gpsimd.memset(earlier[:], 1.0).then_inc(pool_step, 1)
            pool.wait_ge(pool_step, 4)
            nc.gpsimd.affine_select(out=ident[:], in_=ident[:], compare_op=ALU.not_equal, fill=1.0,
                                    base=0, pattern=[[-1, P]], channel_multiplier=1).then_inc(consts, 1)
            nc.gpsimd.affine_select(out=ident16[:], in_=ones16[:], compare_op=ALU.is_equal, fill=0.0,
                                    base=0, pattern=[[-1, P]], channel_multiplier=1).then_inc(consts, 1)
            nc.gpsimd.affine_select(out=below16[:], in_=ones16[:], compare_op=ALU.is_gt, fill=0.0,
                                    base=0, pattern=[[1, P]], channel_multiplier=-1).then_inc(consts, 1)
            for half in range(2):
                pool.wait_ge(consts, 4 + half)
                part = earlier[64 * half:64 * half + 64, :]
                nc.gpsimd.affine_select(out=part, in_=part, compare_op=ALU.is_gt, fill=0.0,
                                        base=0, pattern=[[-1, SLOTS]], channel_multiplier=1).then_inc(consts, 1)
            pool.wait_ge(consts, 6)
            nc.gpsimd.iota(slot_no[:].rearrange("p (a b) -> p a b", a=2), pattern=[[0, 2], [1, SLOTS]], base=0, channel_multiplier=0,
                           allow_small_or_imprecise_dtypes=True).then_inc(consts, 1)
            nc.gpsimd.iota(col_no[:], pattern=[[1, NP]], base=0, channel_multiplier=0,
                           allow_small_or_imprecise_dtypes=True).then_inc(consts, 1)
            nc.gpsimd.iota(row_no[:], pattern=[[P, T]], base=0, channel_multiplier=1,
                           allow_small_or_imprecise_dtypes=True).then_inc(consts, 1)
            pool.wait_ge(idx_ready, 1)
            for c in range(EC):
                nc.gpsimd.indirect_dma_start(
                    out=ed_adj[0:EP, c:c + 1], out_offset=None, in_=adj_flat,
                    in_offset=bass.IndirectOffsetOnAxis(ap=ed_idx[0:EP, c:c + 1], axis=0)).then_inc(edges_looked_up[c // CHUNK], 16)
            with overflow(pool):
                general_pool(pool)
            pool.wait_ge(slot_idx_ready, 1)
            pool.wait_ge(w1_lo, 1)
            nc.gpsimd.indirect_dma_start(
                out=xsub, out_offset=None, in_=x,
                in_offset=bass.IndirectOffsetOnAxis(ap=slot_i[:, 0:1], axis=0)).then_inc(xsub_in, 16)
            nc.gpsimd.indirect_dma_start(
                out=xobj, out_offset=None, in_=x,
                in_offset=bass.IndirectOffsetOnAxis(ap=slot_i[:, 1:2], axis=0)).then_inc(xobj_in, 16)
            pool.wait_ge(wqkT_ready, 8)
            for b in range(3):
                pool.wait_ge(sums_stored[b], 16 * len(range(b, T, 3)))
            nc.gpsimd.indirect_dma_start(
                out=gsub, out_offset=None, in_=sums_dram,
                in_offset=bass.IndirectOffsetOnAxis(ap=slot_i[:, 0:1], axis=0)).then_inc(gsub_in, 16)
            pool.wait_ge(same_ready, 1)
            for rows_in in (xsub_in, xobj_in, gsub_in):
                pool.wait_ge(rows_in, 16)
            nc.gpsimd.tensor_scalar(stackL[64:P, :], col_no[64:P, :], slot[64:P, 3:4], None, ALU.is_equal).then_inc(low_ready, 1)
            pool.wait_ge(low_ready, 1)
            pool.wait_ge(bias_loaded, 48)
            for t in range(T):
                pool.wait_ge(x1_transposed, t + 1)
                nc.gpsimd.tensor_tensor(x_sb[:, t, :], x_sb[:, t, :], bias[:, 2, :], ALU.add).then_inc(biased, 1)

        @block.scalar
        def _(act):
            def copy_adjT(t):
                for b in range(2):
                    n = min(8, T - 8 * b)
                    act.wait_ge(adj_transposed, 2 * t + b + 1)
                    nc.scalar.copy(adjT[:, 8 * b:8 * b + n, t * P:(t + 1) * P],
                                   tr16[b][:, 0:n * P].rearrange("p (k i) -> p k i", k=n)).then_inc(adjT_ready, 1)

            def cast_adj(t):
                act.wait_ge(adj_loaded[t % RING], 16 * (t // RING + 1))
                if t >= RING:
                    act.wait_ge(adj_transposed, 2 * (t - RING + 1))
                    act.wait_ge(adj_read, t - RING + 1)
                if t >= 3:
                    act.wait_ge(sums_stored[t % 3], 16 * (t // 3))
                nc.scalar.activation(adj16[:, t % RING, :], stage[:, t % RING, :], ACT.Copy,
                                     accum_out=sums[:, t % 3, H:H + 1]).then_inc(adj_cast, 1)

            def root(s):
                return nc.scalar.activation(s[:, 10:11], s[:, 7:8], ACT.Sqrt, bias=eps[:])

            for g in range(4):
                if g >= 2:
                    act.wait_ge(tr_zeroed, 1)
                    copy_adjT(g - 2)
                elif g == 1:
                    cast_adj(0)
                act.wait_ge(x_loaded[g], 16 if g < 3 else 32)
                hi = min(3 * g + 3, T)
                nc.scalar.mul(xs[:, 0, 3 * g:hi, :], x_sb[:, 3 * g:hi, :], XS).then_inc(x_hi, 1)
                if g == 1:
                    cast_adj(1)
            for i in range(T + 2):
                if i < T:
                    act.wait_ge(coefs_ready, i + 1)
                    if i >= 2:
                        act.wait_ge(y_ready, i - 1)
                    nc.scalar.mul(xd[:, i % 2, :], x_sb[:, i, :], co[:, i % 2, 4:5]).then_inc(xd_ready, 1)
                    if i == 0:
                        act.wait_ge(w1_loaded, 16)
                        nc.scalar.mul(whl[:, 0], wraw[:, 2], WS).then_inc(w1_hi, 1)
                    if i + 2 < T:
                        cast_adj(i + 2)
                    act.wait_ge(sums_done, i + 1)
                    nc.scalar.copy(sums[:, i % 3, 0:H], acc[i % 2][:, :]).then_inc(sums_copied, 1)
                if 1 <= i <= T:
                    act.wait_ge(x1_transposed, i)
                    if i >= 3:
                        act.wait_ge(support_done, i - 2)
                    nc.scalar.mul(x1T[:, (i - 1) % 2, 0, :], acc[4][:, :], XS).then_inc(x1T_hi, 1)
                if i < T:
                    act.wait_ge(moments_ready, i + 1)
                    root(st[:, i % 2]).then_inc(root_ready, 1)
                if i + 2 < T:
                    copy_adjT(i + 2)
                for n in wqk_at(i):
                    act.wait_ge(wqk_transposed, n + 1)
                    nc.scalar.copy(wT[:, n // 4, n % 4, :], tr[n % 3][:, :]).then_inc(wqkT_ready, 1)
                if i < T:
                    act.wait_ge(sums_copied, i + 1)
                    act.dma_start(sums_dram[i * P:(i + 1) * P, :], sums[:, i % 3, :]).then_inc(sums_stored[i % 3], 16)
                if i < T:
                    act.wait_ge(stats_ready, i + 1)
                    nc.scalar.activation(x_sb[:, i, :], y[:, i % 2, :], ACT.Identity, bias=st[:, i % 2, 9:10],
                                         scale=st[:, i % 2, 8:9]).then_inc(x1_ready, 1)
                if i >= 2:
                    act.wait_ge(support_done, i - 1)
                    nc.scalar.mul(ss[:, 0, i - 2, :], acc[2][:, :], SS / (XS * WS)).then_inc(support_hi, 1)
            with overflow(act):
                general_act(act)
            act.wait_ge(xsub_T, 1)
            nc.scalar.copy(xsT, tr[1][:, :]).then_inc(xsT_ready, 1)
            for n in range(2):
                act.wait_ge(cols_done, n + 1)
                nc.scalar.copy(stackL[0:64, 512 * n:512 * n + 512], tr[0][0:64, :]).then_inc(cols_copied, 1)
            act.wait_ge(exps_in, 1)
            nc.scalar.activation(score, score, ACT.Exp).then_inc(exps_done, 1)
            act.wait_ge(cols_done, 3)
            nc.scalar.copy(stackL[0:64, 1024:NP], tr[0][0:64, 0:NP - 1024]).then_inc(cols_copied, 1)
            for n in range(2):
                act.wait_ge(slot_moments, n + 1)
                root(st[:, n]).then_inc(slot_root, 1)
            act.wait_ge(change_ready, 1)
            nc.scalar.mul(stackR[64:P, 0, :], dx1[64:P, :], SS).then_inc(right_hi, 1)
            act.wait_ge(change_T, 1)
            nc.scalar.mul(dT[:, 0, :], tr[0][:, 0:KF * SLOTS], XS).then_inc(dT_hi, 1)
            act.wait_ge(dS_done, 1)
            nc.scalar.mul(stackR[0:64, 0, :], tr[2][0:64, :], SS / (XS * WS)).then_inc(right_hi, 1)
            act.wait_ge(z_moments, 1)
            root(st[:, 0]).then_inc(z_root, 1)
            for t in range(T):
                if t + 1 < T:
                    act.wait_ge(z_moments, t + 2)
                    root(st[:, (t + 1) % 2]).then_inc(z_root, 1)
                act.wait_ge(z_stats, t + 1)
                nc.scalar.activation(y4(t), y4(t), ACT.Identity, bias=st[:, t % 2, 9:10],
                                     scale=st[:, t % 2, 8:9]).then_inc(z_normed, 1)

        @block.vector
        def _(dve):
            steps = 0

            def step(ins):
                nonlocal steps
                steps += 1
                ins.then_inc(dve_step, 1)
                dve.wait_ge(dve_step, steps)

            V = nc.vector
            V.memset(tr[1][:, :], 0.0).then_inc(tr_zeroed, 1)
            dve.wait_ge(edges_loaded, 16)
            e_i, e, o2, eok = ed_i[0:EP], ed[0:EP], ok2[0:EP], ed_ok[0:EP]
            step(V.tensor_copy(e, e_i))
            step(V.tensor_scalar(o2, e, 0.0, float(N), ALU.is_lt, ALU.mult))
            step(V.tensor_tensor(e, e, o2, ALU.add))
            step(V.tensor_scalar(o2, e, float(N), None, ALU.is_lt))
            step(V.scalar_tensor_tensor(o2, e, 0.0, o2, ALU.is_ge, ALU.mult))
            ein, lin = ed_in[0:EP], ed_lin[0:EP]
            step(V.tensor_tensor(ein, o2[:, :, 0], o2[:, :, 1], ALU.mult))
            step(V.scalar_tensor_tensor(lin, e[:, :, 0], float(N), e[:, :, 1], ALU.mult, ALU.add))
            step(V.tensor_tensor(lin, lin, ein, ALU.mult))
            V.tensor_copy(ed_idx[0:EP], lin).then_inc(idx_ready, 1)
            step(V.tensor_tensor(eok, e[:, :, 0], e[:, :, 1], ALU.not_equal))
            step(V.tensor_tensor(eok, eok, ein, ALU.mult))
            V.memset(ed3[0:EP, :, 2:3], 1.0).then_inc(dve_step, 1)
            steps += 1
            step(V.tensor_tensor(ed3[0:EP, :, 0:2], e, ein.unsqueeze(2).broadcast_to([EP, EC, 2]), ALU.mult))
            def low_x(g):
                hi = min(3 * g + 3, T)
                dve.wait_ge(x_hi, g + 1)
                V.scalar_tensor_tensor(xs[:, 1, 3 * g:hi, :], x_sb[:, 3 * g:hi, :], XS, xs[:, 0, 3 * g:hi, :],
                                       ALU.mult, ALU.subtract).then_inc(x_lo, 1)

            def coefs(t):
                c, s = co[:, t % 2], sums[:, t % 3]
                dve.wait_ge(adj_cast, t + 1)
                if t >= 2:
                    dve.wait_ge(xd_ready, t - 1)
                step(V.scalar_tensor_tensor(junk16[:, 0:width[t]], adj16[:, t % RING, t * P:t * P + width[t]], 1.0,
                                            ident16[:, 0:width[t]], ALU.mult, ALU.mult, accum_out=s[:, H + 1:H + 2]))
                step(V.tensor_tensor(s[:, H:H + 1], s[:, H:H + 1], s[:, H + 1:H + 2], ALU.subtract))
                V.tensor_scalar(c[:, 0:1], s[:, H:H + 1], A0, 1.0, ALU.mult, ALU.add).then_inc(adj_read, 1)
                dve.wait_ge(adj_read, t + 1)
                step(V.reciprocal(c[:, 1:2], c[:, 0:1]))
                step(V.tensor_scalar(c[:, 2:3], c[:, 1:2], A0, None, ALU.mult))
                step(V.tensor_tensor(c[:, 3:4], c[:, 2:3], s[:, H + 1:H + 2], ALU.mult))
                step(V.scalar_tensor_tensor(c[:, 4:5], c[:, 1:2], 1.0, c[:, 3:4], ALU.add, ALU.subtract))
                V.tensor_scalar(c[:, 5:6], c[:, 2:3], 1.0 / XS, None, ALU.mult).then_inc(coefs_ready, 1)

            def moments(s, v):
                step(V.bn_stats(s[:, 0:6], v))
                return V.bn_aggr(s[:, 6:8], s[:, 0:6])

            def scale_shift(s):
                step(V.reciprocal(s[:, 8:9], s[:, 10:11]))
                return V.tensor_scalar(s[:, 9:10], s[:, 6:7], -1.0, s[:, 8:9], ALU.mult, ALU.mult)

            def flag_chunk(n):
                a, b = CHUNKS[n], CHUNKS[n + 1]
                dve.wait_ge(edges_looked_up[n], 16 * (b - a))
                V.scalar_tensor_tensor(flag[0:EP, a:b], ed_adj[0:EP, a:b], 1.0, eok[:, a:b],
                                       ALU.is_equal, ALU.mult).then_inc(flags_ready, 1)

            def number_chunk(n):
                a, b = CHUNKS[n], CHUNKS[n + 1]
                m = b - a
                dve.wait_ge(numbered, n + 1)
                step(V.tensor_tensor_scan(seen[:, a:b], ones[:, 0:m], acc[3][:, TOT:TOT + m],
                                          seen[:, a - 1:a] if n else 0.0, ALU.mult, ALU.add))
                step(V.tensor_tensor(pos[:, 0, 0:m], seen[:, a:b], acc[3][:, TOT:TOT + m], ALU.subtract))
                step(V.tensor_tensor(pos[:, 1, 0:m], pos[:, 0, 0:m], acc[3][:, PRE:PRE + m], ALU.add))
                step(V.tensor_scalar(pos[0:EP, 2, 0:m], flag[0:EP, a:b], -FAR, FAR, ALU.mult, ALU.add))
                step(V.tensor_tensor(pos[0:EP, 0, 0:m], pos[0:EP, 1, 0:m], pos[0:EP, 2, 0:m], ALU.add))
                if n:
                    dve.wait_ge(compacted, n)
                V.tensor_tensor(onehot[0:EP, 0:m * P].rearrange("p (c f) -> p c f", c=m),
                                pos[0:EP, 0, 0:m].unsqueeze(2).broadcast_to([EP, m, P]),
                                slot_no[0:EP].unsqueeze(1).broadcast_to([EP, m, P]),
                                ALU.is_equal).then_inc(onehot_ready, 1)

            fits = slot[:, 8:9]
            dve.wait_ge(consts, 9)
            low_x(0)
            low_x(1)
            coefs(0)
            low_x(2)
            low_x(3)
            for i in range(T + 2):
                if 0 <= i - 1 < NC:
                    flag_chunk(i - 1)
                if i + 1 < T:
                    coefs(i + 1)
                if i == 0:
                    dve.wait_ge(w1_hi, 1)
                    V.scalar_tensor_tensor(whl[:, 1], wraw[:, 2], WS, whl[:, 0], ALU.mult, ALU.subtract).then_inc(w1_lo, 1)
                if 1 <= i <= T:
                    dve.wait_ge(x1T_hi, i)
                    V.scalar_tensor_tensor(x1T[:, (i - 1) % 2, 1, :], acc[4][:, :], XS, x1T[:, (i - 1) % 2, 0, :],
                                           ALU.mult, ALU.subtract).then_inc(x1T_lo, 1)
                if i < T:
                    dve.wait_ge(sums_copied, i + 1)
                    dve.wait_ge(xd_ready, i + 1)
                    if i >= 2:
                        dve.wait_ge(x1_ready, i - 1)
                    V.scalar_tensor_tensor(y[:, i % 2, :], acc[i % 2][:, :], co[:, i % 2, 5:6], xd[:, i % 2, :],
                                           ALU.mult, ALU.add).then_inc(y_ready, 1)
                    dve.wait_ge(y_ready, i + 1)
                    moments(st[:, i % 2], y[:, i % 2, :]).then_inc(moments_ready, 1)
                    dve.wait_ge(root_ready, i + 1)
                    scale_shift(st[:, i % 2]).then_inc(stats_ready, 1)
                if 0 <= i - 1 < NC:
                    number_chunk(i - 1)
                if i == T:
                    V.tensor_copy(count_i[:], seen[:, EC - 1:EC]).then_inc(count_ready, 1)
                    step(V.tensor_scalar(fits, seen[:, EC - 1:EC], float(SLOTS), None, ALU.is_le))
                    dve.wait_ge(compacted, NC)
                    step(V.tensor_reduce(slot[:, 0:3], acc[3][:, CMP:CMP + 3 * NC].rearrange("p (n v) -> p v n", v=3),
                                         AX.X, ALU.add))
                    V.tensor_copy(slot_i[:], slot[:, 0:2]).then_inc(slot_idx_ready, 1)
                if i >= 2:
                    dve.wait_ge(support_hi, i - 1)
                    V.scalar_tensor_tensor(ss[:, 1, i - 2, :], acc[2][:, :], SS / (XS * WS), ss[:, 0, i - 2, :],
                                           ALU.mult, ALU.subtract).then_inc(support_lo, 1)
            with overflow(dve):
                general_dve(dve)
            sub, key, valid = slot[:, 3:4], slot[:, 4:5], slot[:, 2:3]
            step(V.tensor_scalar(slot[:, 5:6], valid, -1.0, FAR, ALU.add, ALU.mult))
            step(V.tensor_tensor(sub, slot[:, 0:1], slot[:, 5:6], ALU.add))
            step(V.scalar_tensor_tensor(key, sub, 2048.0, slot[:, 1:2], ALU.mult, ALU.add))
            eye = ident[0:64, 0:64]
            step(V.tensor_scalar(spread[0:64, 0:64], eye, sub[0:64], None, ALU.mult))
            step(V.tensor_scalar(spread[0:64, 64:128], eye, sub[0:64], None, ALU.mult))
            V.tensor_scalar(spread[0:64, 128:192], eye, key[0:64], None, ALU.mult).then_inc(spread_ready, 1)
            dve.wait_ge(subs_spread, 1)
            V.tensor_tensor(slot_row[:, :, :], tr[0][:, 0:SLOTS].unsqueeze(1).broadcast_to([P, T, SLOTS]),
                            row_no[:, :].unsqueeze(2).broadcast_to([P, T, SLOTS]), ALU.is_equal).then_inc(rows_ready, 1)
            step(V.tensor_scalar(same, tr[0][:, 0:P], sub, None, ALU.is_equal))
            V.tensor_scalar(keq, tr[0][:, P:P + SLOTS], key, None, ALU.is_equal).then_inc(same_ready, 1)
            dve.wait_ge(same_ready, 1)
            dup_row, dup_key, rep, keep = small[:, 0:1], small[:, 1:2], small[:, 2:3], small[:, 3:4]
            junk = small[:, 16:80]
            step(V.tensor_tensor_reduce(out=junk, in0=same[:, 0:SLOTS], in1=earlier[:], scale=1.0, scalar=0.0,
                                        op0=ALU.mult, op1=ALU.max, accum_out=dup_row))
            step(V.tensor_tensor_reduce(out=junk, in0=keq, in1=earlier[:], scale=1.0, scalar=0.0,
                                        op0=ALU.mult, op1=ALU.max, accum_out=dup_key))
            step(V.scalar_tensor_tensor(rep, dup_row, 0.0, valid, ALU.is_equal, ALU.mult))
            step(V.tensor_tensor(rep, rep, fits, ALU.mult))
            step(V.scalar_tensor_tensor(keep, dup_key, 0.0, valid, ALU.is_equal, ALU.mult))
            dve.wait_ge(xobj_T, 1)
            dve.wait_ge(wqkT_ready, 8)
            V.tensor_copy(xoT, tr[2][:, :]).then_inc(xoT_ready, 1)
            dve.wait_ge(bias_loaded, 48)
            dve.wait_ge(q_done, 1)
            step(V.tensor_tensor(q, tr[1][:, :], bias[:, 0, :], ALU.add))
            dve.wait_ge(k_done, 1)
            step(V.tensor_tensor(kk, tr[2][:, :], bias[:, 1, :], ALU.add))
            V.tensor_tensor(q, q, kk, ALU.mult).then_inc(qk_read, 1)
            dve.wait_ge(qk_read, 1)
            sc = small[:, 4:12]
            step(V.reduce_sum(sc, q.rearrange("p (h d) -> p h d", h=HEADS), AX.X))
            gone = slot[:, 6:7]
            step(V.tensor_scalar(gone, keep, -1.0, -GONE, ALU.add, ALU.mult))
            step(V.tensor_scalar(sc, sc, 1.0 / np.sqrt(DK), keep, ALU.mult, ALU.mult))
            step(V.tensor_scalar(sc, sc, gone, None, ALU.add))
            V.tensor_tensor(spread[0:64].rearrange("p (h g) -> p h g", h=HEADS), eye.unsqueeze(1).broadcast_to([64, HEADS, SLOTS]),
                            sc[0:64].unsqueeze(2).broadcast_to([64, HEADS, SLOTS]), ALU.mult).then_inc(scores_ready, 1)
            step(V.tensor_scalar(keq, same[:, 0:SLOTS], -1.0, -GONE, ALU.add, ALU.mult))
            V.memset(score[:, :, SLOTS:SLOTS + 1], 0.0).then_inc(dve_step, 1)
            V.memset(score[:, :, SLOTS + 1:SLOTS + 2], TINY).then_inc(dve_step, 1)
            steps += 2
            step(V.tensor_copy(score[:, :, SLOTS + 2], sc))
            dve.wait_ge(scores_spread, 1)
            step(V.tensor_tensor(score[:, :, 0:SLOTS], tr[1][:, :].rearrange("p (h g) -> p h g", h=HEADS),
                                 keq.unsqueeze(1).broadcast_to([P, HEADS, SLOTS]), ALU.add))
            top = small[:, 16:24]
            step(V.reduce_max(top, score[:, :, 0:SLOTS + 2], AX.X))
            V.tensor_tensor(score, score, top.unsqueeze(2).broadcast_to([P, HEADS, EXTRA]), ALU.subtract).then_inc(exps_in, 1)
            dve.wait_ge(gsub_in, 16)
            dve.wait_ge(live_done, 1)
            off = gsub[:, H:H + 1]
            aii = gsub[:, H + 1:H + 2]
            plain = slot[:, 7:8]
            step(V.tensor_tensor(plain, off, tr[2][:, 0:1], ALU.subtract))
            b = small[:, 24:32]
            step(V.tensor_scalar(b[:, 0:1], off, A0, 1.0, ALU.mult, ALU.add))
            step(V.reciprocal(b[:, 1:2], b[:, 0:1]))
            step(V.tensor_scalar(b[:, 2:3], b[:, 1:2], A0, None, ALU.mult))
            step(V.tensor_tensor(b[:, 3:4], b[:, 2:3], aii, ALU.mult))
            step(V.scalar_tensor_tensor(b[:, 4:5], b[:, 1:2], 1.0, b[:, 3:4], ALU.add, ALU.subtract))
            step(V.tensor_scalar(b[:, 5:6], b[:, 2:3], 1.0 / XS, None, ALU.mult))
            step(V.tensor_scalar(kk, xsub, b[:, 4:5], None, ALU.mult))
            step(V.scalar_tensor_tensor(kk, gsub[:, 0:H], b[:, 5:6], kk, ALU.mult, ALU.add))
            norm_a, norm_b = st[:, 0], st[:, 1]
            moments(norm_a, kk).then_inc(slot_moments, 1)
            dve.wait_ge(exps_done, 1)
            sumf, z = small[:, 44:52], small[:, 52:60]
            step(V.reduce_sum(sumf, score[:, :, 0:SLOTS], AX.X))
            step(V.scalar_tensor_tensor(z, score[:, :, SLOTS], plain, sumf, ALU.mult, ALU.add))
            step(V.tensor_tensor(z, z, score[:, :, SLOTS + 1], ALU.add))
            step(V.reciprocal(z, z))
            share8 = score[:, :, SLOTS:SLOTS + 3]
            step(V.tensor_tensor(share8, share8, z.unsqueeze(2).broadcast_to([P, HEADS, 3]), ALU.mult))
            cdw = small[:, 60:63]
            step(V.reduce_sum(cdw, share8.rearrange("p h c -> p c h"), AX.X))
            step(V.tensor_scalar(cdw, cdw, 1.0 / HEADS, None, ALU.mult))
            vv = small[:, 63:64]
            step(V.tensor_tensor(vv, cdw[:, 2:3], cdw[:, 0:1], ALU.subtract))
            step(V.tensor_tensor(vv, vv, keep, ALU.mult))
            V.tensor_scalar(vsame[0:64], same[0:64], vv[0:64], None, ALU.mult).then_inc(shares_ready, 1)
            n = small[:, 64:68]
            step(V.tensor_tensor(n[:, 0:1], cdw[:, 0:1], aii, ALU.mult))
            step(V.scalar_tensor_tensor(n[:, 1:2], cdw[:, 1:2], 1.0, n[:, 0:1], ALU.add, ALU.subtract))
            step(V.tensor_scalar(n[:, 2:3], cdw[:, 0:1], 1.0 / XS, None, ALU.mult))
            step(V.tensor_scalar(q, xsub, n[:, 1:2], None, ALU.mult))
            step(V.scalar_tensor_tensor(q, gsub[:, 0:H], n[:, 2:3], q, ALU.mult, ALU.add))
            dve.wait_ge(mixed, 1)
            step(V.tensor_tensor(q, q, tr[2][:, :], ALU.add))
            moments(norm_b, q).then_inc(slot_moments, 1)
            dve.wait_ge(slot_root, 1)
            step(scale_shift(norm_a))
            step(V.tensor_scalar(kk, kk, norm_a[:, 8:9], norm_a[:, 9:10], ALU.mult, ALU.add))
            dve.wait_ge(slot_root, 2)
            step(scale_shift(norm_b))
            step(V.tensor_scalar(q, q, norm_b[:, 8:9], norm_b[:, 9:10], ALU.mult, ALU.add))
            step(V.tensor_tensor(dx1, q, kk, ALU.subtract))
            V.tensor_scalar(dx1, dx1, rep, None, ALU.mult).then_inc(change_ready, 1)
            dve.wait_ge(dT_hi, 1)
            V.scalar_tensor_tensor(dT[:, 1, :], tr[0][:, 0:KF * SLOTS], XS, dT[:, 0, :], ALU.mult, ALU.subtract).then_inc(dT_lo, 1)
            dve.wait_ge(right_hi, 1)
            V.scalar_tensor_tensor(stackR[64:P, 1, :], dx1[64:P, :], SS, stackR[64:P, 0, :], ALU.mult, ALU.subtract).then_inc(right_lo, 1)
            dve.wait_ge(right_hi, 2)
            V.scalar_tensor_tensor(stackR[0:64, 1, :], tr[2][0:64, :], SS / (XS * WS), stackR[0:64, 0, :],
                                   ALU.mult, ALU.subtract).then_inc(right_lo, 1)
            for t in range(T):
                dve.wait_ge(out_done, t + 1)
                dve.wait_ge(biased, t + 1)
                if t >= 4:
                    dve.wait_ge(out_stored[t % 4], 16 * (t // 4))
                if t >= 2:
                    dve.wait_ge(z_normed, t - 1)
                V.scalar_tensor_tensor(y4(t), out_bank(t)[:, :], 1.0 / SS, x_sb[:, t, :], ALU.mult, ALU.add).then_inc(z_ready, 1)
                dve.wait_ge(z_ready, t + 1)
                moments(st[:, t % 2], y4(t)).then_inc(z_moments, 1)
                if t >= 1:
                    dve.wait_ge(z_root, t)
                    scale_shift(st[:, (t - 1) % 2]).then_inc(z_stats, 1)
            dve.wait_ge(z_root, T)
            scale_shift(st[:, (T - 1) % 2]).then_inc(z_stats, 1)

        @block.tensor
        def _(pe):
            mm = nc.tensor.matmul

            def transpose_adj(t):
                pe.wait_ge(adj_cast, t + 1)
                for b in range(2):
                    if t >= 1:
                        pe.wait_ge(adjT_ready, 2 * (t - 1) + b + 1)
                    for k in range(8 * b, min(8 * b + 8, T)):
                        last = nc.tensor.transpose(tr16[b][0:width[k], (k % 8) * P:(k % 8 + 1) * P],
                                                   adj16[:, t % RING, k * P:k * P + width[k]], ident16[:])
                    last.then_inc(adj_transposed, 1)

            pe.wait_ge(consts, 9)
            pe.wait_ge(tr_zeroed, 1)
            transpose_adj(0)
            for i in range(T + 2):
                if i < T:
                    pe.wait_ge(adjT_ready, 2 * (i + 1))
                    if i >= 2:
                        pe.wait_ge(y_ready, i - 1)
                    for k in range(T):
                        if i == 0 and k % 3 == 0:
                            if k == 6:
                                transpose_adj(1)
                            pe.wait_ge(x_lo, min(k // 3 + 1, 4))
                        for half in range(2):
                            last = mm(acc[i % 2][:, :], adjT[0:width[k], k, i * P:(i + 1) * P], xs[0:width[k], half, k, :],
                                      start=(k == 0 and half == 0), stop=(k == T - 1 and half == 1))
                    last.then_inc(sums_done, 1)
                if 1 <= i <= T:
                    pe.wait_ge(x1_ready, i)
                    if i >= 2:
                        pe.wait_ge(x1T_lo, i - 1)
                    for k in range(KF):
                        last = nc.tensor.transpose(acc[4][:, k * P:(k + 1) * P], x_sb[:, i - 1, k * P:(k + 1) * P], ident[:])
                    last.then_inc(x1_transposed, 1)
                if i + 2 < T:
                    transpose_adj(i + 2)
                for n in wqk_at(i):
                    pe.wait_ge(wqk_loaded, 32)
                    if n >= 3:
                        pe.wait_ge(wqkT_ready, n - 2)
                    else:
                        pe.wait_ge(adjT_ready, 2 * T)
                    for k in range(KF):
                        last = nc.tensor.transpose(tr[n % 3][:, k * P:(k + 1) * P],
                                                   wraw[:, n // 4, k, (n % 4) * P:(n % 4 + 1) * P], ident[:])
                    last.then_inc(wqk_transposed, 1)
                if 0 <= i - 2 < NC:
                    compact(pe, i - 2)
                if 0 <= i - 1 < NC:
                    number(pe, i - 1)
                if i >= 2:
                    pe.wait_ge(x1T_lo, i - 1)
                    pe.wait_ge(w1_lo, 1)
                    if i >= 3:
                        pe.wait_ge(support_lo, i - 2)
                    for k in range(KF):
                        for n, (a, b) in enumerate(((0, 0), (0, 1), (1, 0))):
                            last = mm(acc[2][:, :], x1T[:, i % 2, a, k * P:(k + 1) * P], whl[:, b, k, :],
                                      start=(k == 0 and n == 0), stop=(k == KF - 1 and n == 2))
                    last.then_inc(support_done, 1)
            with overflow(pe):
                general_pe(pe)

            def base(t, ks=range(T)):
                if t >= OUTS:
                    pe.wait_ge(z_ready, t - OUTS + 1)
                elif t == 3:
                    pe.wait_ge(slot_idx_ready, 1)
                for k in ks:
                    if t == 0 and k == T - 1:
                        pe.wait_ge(support_lo, T)
                    for half in range(2):
                        mm(out_bank(t)[:, :], adjT[0:width[k], k, t * P:(t + 1) * P], ss[0:width[k], half, k, :],
                           start=(k == 0 and half == 0), stop=False)

            def cols(n):
                lo, hi = 512 * n, min(512 * n + 512, NP)
                for k in range(T):
                    last = mm(tr[0][0:64, 0:hi - lo], slot_row[0:width[k], k, :], adjT[0:width[k], k, lo:hi],
                              start=(k == 0), stop=(k == T - 1))
                last.then_inc(cols_done, 1)

            pe.wait_ge(support_lo, T - 1)
            base(0)
            pe.wait_ge(spread_ready, 1)
            mm(tr[0][:, 0:192], ones[0:64, :], spread[0:64, 0:192], start=True, stop=True).then_inc(subs_spread, 1)
            pe.wait_ge(xsub_in, 16)
            for k in range(KF):
                last = nc.tensor.transpose(tr[1][:, k * P:(k + 1) * P], xsub[:, k * P:(k + 1) * P], ident[:])
            last.then_inc(xsub_T, 1)
            pe.wait_ge(xobj_in, 16)
            pe.wait_ge(slot_idx_ready, 1)
            for k in range(KF):
                last = nc.tensor.transpose(tr[2][:, k * P:(k + 1) * P], xobj[:, k * P:(k + 1) * P], ident[:])
            last.then_inc(xobj_T, 1)
            pe.wait_ge(rows_ready, 1)
            pe.wait_ge(same_ready, 1)
            cols(0)
            base(1)
            pe.wait_ge(xsT_ready, 1)
            for k in range(KF):
                last = mm(tr[1][:, :], xsT[:, k * P:(k + 1) * P], wT[:, 0, k, :], start=(k == 0), stop=(k == KF - 1))
            last.then_inc(q_done, 1)
            pe.wait_ge(xoT_ready, 1)
            for k in range(KF):
                last = mm(tr[2][:, :], xoT[:, k * P:(k + 1) * P], wT[:, 1, k, :], start=(k == 0), stop=(k == KF - 1))
            last.then_inc(k_done, 1)
            pe.wait_ge(cols_copied, 1)
            cols(1)
            base(2)
            pe.wait_ge(scores_ready, 1)
            mm(tr[1][:, :], ones[0:64, :], spread[0:64, :], start=True, stop=True).then_inc(scores_spread, 1)
            mm(tr[2][:, 0:1], same[0:64, :], small[0:64, 3:4], start=True, stop=True).then_inc(live_done, 1)
            pe.wait_ge(cols_copied, 2)
            cols(2)
            base(3)
            base(4, range(0, 5))
            pe.wait_ge(shares_ready, 1)
            mm(tr[2][:, :], vsame[0:64, :], xobj[0:64, :], start=True, stop=True).then_inc(mixed, 1)
            base(4, range(5, T))
            base(5, range(0, 4))
            pe.wait_ge(change_ready, 1)
            pe.wait_ge(cols_copied, 3)
            for k in range(KF):
                last = nc.tensor.transpose(tr[0][:, k * SLOTS:(k + 1) * SLOTS], dx1[0:64, k * P:(k + 1) * P], ident[0:64, 0:64])
            last.then_inc(change_T, 1)
            base(5, range(4, 7))
            pe.wait_ge(dT_lo, 1)
            for k in range(KF):
                for n, (a, b) in enumerate(((0, 0), (0, 1), (1, 0))):
                    last = mm(tr[2][0:64, :], dT[:, a, k * SLOTS:(k + 1) * SLOTS], whl[:, b, k, :],
                              start=(k == 0 and n == 0), stop=(k == KF - 1 and n == 2))
            last.then_inc(dS_done, 1)
            base(5, range(7, T))
            pe.wait_ge(low_ready, 1)
            pe.wait_ge(right_hi, 2)
            pe.wait_ge(right_lo, 2)

            def close(t):
                mm(out_bank(t)[:, :], stackL[:, t * P:(t + 1) * P], stackR[:, 0, :], start=False, stop=False)
                mm(out_bank(t)[:, :], stackL[:, t * P:(t + 1) * P], stackR[:, 1, :], start=False, stop=True).then_inc(out_done, 1)

            for t in range(OUTS):
                close(t)
            for t in range(OUTS, T):
                base(t)
                close(t)


_INS = ['x', 'adj', 'L0_gnn_rel_pair_index', 'L0_gnn_Wq', 'L0_gnn_bq', 'L0_gnn_Wk', 'L0_gnn_bk', 'L1_gnn_weight', 'L1_gnn_bias']


def kernel(**inputs):
    import numpy as _np
    import concourse.bacc as _bacc
    from concourse import mybir as _mybir
    from concourse.bass_utils import run_bass_kernel_spmd as _run

    nc = _bacc.Bacc("TRN2", target_bir_lowering=False, num_devices=1)
    arrays, args = {}, []
    for name in _INS:
        a = _np.ascontiguousarray(inputs[name])
        arrays[f"in_{name}"] = a
        args.append(nc.dram_tensor(f"in_{name}", a.shape, _mybir.dt.from_np(a.dtype), kind="ExternalInput").ap())
    args.append(nc.dram_tensor("out_0", (N, H), _mybir.dt.float32, kind="ExternalOutput").ap())
    resnorm_graph(nc, *args)
    r = _run(nc, [arrays], core_ids=[0])
    return r.results[0]["out_0"]
```

```python
import numpy as np
import concourse.bass as bass
from concourse import mybir
from contextlib import ExitStack


N = 1354
H = 512
E = 10000
HEADS = 8
DK = H // HEADS
P = 128
T = (N + P - 1) // P
LAST = N - (T - 1) * P
NP = T * P
KF = H // P
EP = 125
EC = E // EP
SLOTS = 64
CHUNKS = [0, 16, 32, 48, 64, 73, EC]
NC = len(CHUNKS) - 1
CHUNK = max(b - a for a, b in zip(CHUNKS, CHUNKS[1:]))
NUMBERED_AT = {4: 0, 6: 1, 8: 2, T: 3, T + 1: 4, T + 2: 5}
FLAGGED_AT = {3: 0, 5: 1, 8: 2, T - 1: 3}
SPANS = [(0, 512), (512, 1024), (1024, N)]
UNITS = KF * len(SPANS)
HALF = H // 2
BIASES = 1 + 2 * KF
OUTS = 6
RING = 3
CASTS = 2
SUMS = 4
COEFS = 4
GW = H + 2
XS = 64.0
WS = 256.0
TINY = float(np.float32(1e-7))
A0 = float(np.float32(np.exp(-1e-7)))
EPS = 1e-5
FAR = 4096.0
GONE = -1e30


def resnorm_graph(nc, x, adj, pairs, wq, bq, wk, bk, w1, b1, out):
    f32, f16, i32 = mybir.dt.float32, mybir.dt.float16, mybir.dt.int32
    ALU, ACT, AX = mybir.AluOpType, mybir.ActivationFunctionType, mybir.AxisListType
    width = [P] * (T - 1) + [LAST]

    with ExitStack() as ctx:
        def sb(name, shape, dt=f32):
            return ctx.enter_context(nc.sbuf_tensor(name, shape, dt))

        def sem(name):
            return ctx.enter_context(nc.semaphore(name))

        sums_dram = nc.dram_tensor("sums_dram", [NP, GW], f32, kind="Internal").ap()
        adjT_dram = nc.dram_tensor("adjT_dram", [NP, NP], f16, kind="Internal").ap()
        live_map = nc.dram_tensor("live_map", [N, N], f32, kind="Internal").ap()
        live_flat = live_map.rearrange("i (j o) -> (i j) o", o=1)
        adj_flat = adj.rearrange("i (j o) -> (i j) o", o=1)

        x_sb = sb("x_sb", [P, T, H])
        xs = sb("xs", [P, 2, T, H], f16)
        x1s = sb("x1s", [P, 2, T, H], f16)
        adjT = sb("adjT", [P, T, NP], f16)
        stage = sb("stage", [P, RING, N])
        room16 = sb("room16", [P, CASTS * NP], f16)
        adj16 = room16[:, 0:CASTS * N].rearrange("p (c n) -> p c n", c=CASTS)
        sums = sb("sums", [P, SUMS, H])
        counts = sb("counts", [P, T, 2])
        wraw = sb("wraw", [P, 3, KF, H])
        wT = sb("wT", [P, 2, KF, H])
        whl = sb("whl", [P, 2, KF, H], f16)
        bias = sb("bias", [P, H])
        bias_col = sb("bias_col", [P, 2, KF])
        xd = sb("xd", [P, 2, H])
        y = sb("y", [P, 2, H])
        co = sb("co", [P, COEFS, 8])
        st = sb("st", [P, 2, 12])
        last_st = sb("last_st", [P, 12])
        onehot = sb("onehot", [P, P * CHUNK], f16)
        stackL = sb("stackL", [P, NP], f16)
        junk16 = stackL[:, 0:P]
        stackR = sb("stackR", [P, 2, H], f16)

        ident = sb("ident", [P, P])
        ident16 = sb("ident16", [P, P], f16)
        ones = sb("ones", [P, P])
        ones16 = sb("ones16", [P, P], f16)
        below16 = sb("below16", [P, P], f16)
        slot_of = sb("slot_of", [P, P], f16)
        slot_no = sb("slot_no", [P, P, CHUNK], f16)
        earlier = sb("earlier", [P, SLOTS])
        col_no = sb("col_no", [P, NP], f16)
        eps = sb("eps", [P, 1])
        table_loader = sb("table_loader", [P, 3])
        row_no = sb("row_no", [P, T])

        ed_i = sb("ed_i", [P, EC, 2], i32)
        ed = sb("ed", [P, EC, 2])
        ok2 = y[:, 0, 0:2 * EC].rearrange("p (c two) -> p c two", two=2)
        ed_ok = sb("ed_ok", [P, EC])
        ed_in = sb("ed_in", [P, EC])
        ed_lin = sb("ed_lin", [P, EC])
        ed_idx = sb("ed_idx", [P, EC], i32)
        ed_adj = sb("ed_adj", [P, EC])
        ed3 = sb("ed3", [P, EC, 3], f16)
        flag = sb("flag", [P, EC], f16)
        seen = sb("seen", [P, EC])
        pos = sb("pos", [P, 3, CHUNK])
        pos16 = sb("pos16", [P, CHUNK], f16)
        pos_all = seen[0:EP]
        slot = sb("slot", [P, 16])
        slot_i = sb("slot_i", [P, 2], i32)
        count_i = sb("count_i", [P, 1], i32)

        raw = wraw[:, :, :, :].rearrange("p a b c -> p (a b c)")
        at = 2 * KF * H

        def take(n):
            nonlocal at
            at += n
            return raw[:, at - n:at]
        xsub, xobj, spread, same, keq, vsame, small = map(take, (H, H, H, P, SLOTS, P, 80))
        head_of = take(2)
        assert at <= 3 * KF * H
        at = 0
        EXTRA = SLOTS + 3
        gsub, q, kk, dx1 = map(take, (GW, H, H, H))
        xsT, xoT, kT_slots = (take(KF * SLOTS) for _ in range(3))
        qk = take(KF * P).rearrange("p (k two g) -> p k two g", k=KF, two=2)
        score = take(HEADS * EXTRA).rearrange("p (h g) -> p h g", h=HEADS)
        assert at <= 2 * KF * H
        dT = onehot[:, 0:2 * KF * SLOTS].rearrange("p (a n) -> p a n", a=2)
        mix = xs[:, :, :, :].rearrange("p a t h -> p (a t h)").rearrange("p (a k i) -> p a k i", a=2, k=KF)

        d_adj, d_live, d_mask, d_score = (raw[:, n * N:(n + 1) * N] for n in range(4))
        d_x = raw[:, 4 * N:4 * N + H]
        flat_stage = stage[:, :, :].rearrange("p r n -> p (r n)")
        d_prob, d_share = flat_stage[:, 0:N], flat_stage[:, N:2 * N]
        d_shareT = room16[:, :].bitcast(f32).rearrange("p (k i) -> p k i", k=T)
        d_xT, d_qT = y[:, 0, :], y[:, 1, :]
        d_x1, d_y = xd[:, 0, :], xd[:, 1, :]
        x32 = xs[:, :, :, :].rearrange("p a t h -> p (a t h)").bitcast(f32).rearrange("p (t h) -> p t h", t=T)
        kT = x1s[:, :, :, :].rearrange("p a t h -> p (a t h)").bitcast(f32).rearrange("p (k i) -> p k i", k=KF)
        d_no = sb("d_no", [P, 1])
        d_st = sb("d_st", [P, 12])
        d_s = sb("d_s", [P, 24])

        tr = [ctx.enter_context(nc.psum_tensor(f"tr{i}", [P, 512], f32)) for i in range(3)]
        tr16 = [b[:, :].bitcast(f16) for b in tr]
        acc = [ctx.enter_context(nc.psum_tensor(f"acc{i}", [P, 512], f32)) for i in range(5)]
        PRE, TOT, CMP = 0, CHUNK, 2 * CHUNK

        edges_loaded, w1_loaded, wq_loaded, wk_loaded, bias_loaded = map(sem, ("edges_loaded", "w1_loaded", "wq_loaded", "wk_loaded", "bias_loaded"))
        x_loaded = [sem(f"x_loaded{i}") for i in range(4)]
        adj_loaded = [sem(f"adj_loaded{i}") for i in range(RING)]
        counts_stored = sem("counts_stored")
        adjT_stored = [sem(f"adjT_stored{i}") for i in range(2)]
        sums_stored = [sem(f"sums_stored{i}") for i in range(SUMS)]
        edges_looked_up = [sem(f"edges_looked_up{i}") for i in range(NC)]
        pad_zeroed, tr_zeroed, consts, late_consts = map(sem, ("pad_zeroed", "tr_zeroed", "consts", "late_consts"))
        dve_step, pool_step = sem("dve_step"), sem("pool_step")
        x_hi, x_lo, w1_hi, w1_lo = map(sem, ("x_hi", "x_lo", "w1_hi", "w1_lo"))
        adj_cast, adj_transposed, adjT_ready, adj_read = map(sem, ("adj_cast", "adj_transposed", "adjT_ready", "adj_read"))
        sums_done, sums_copied, coefs_ready, xd_ready = map(sem, ("sums_done", "sums_copied", "coefs_ready", "xd_ready"))
        y_ready, stats_ready, x1_ready, x1_hi, x1_lo = map(sem, ("y_ready", "stats_ready", "x1_ready", "x1_hi", "x1_lo"))
        mix_done, mix_hi, mix_lo, keys_ready, dots_done = map(sem, ("mix_done", "mix_hi", "mix_lo", "keys_ready", "dots_done"))
        moments_ready, root_ready, slot_moments, slot_root = map(sem, ("moments_ready", "root_ready", "slot_moments", "slot_root"))
        idx_ready, flags_ready, numbered, onehot_ready, compacted = map(sem, ("idx_ready", "flags_ready", "numbered", "onehot_ready", "compacted"))
        wqk_transposed, wqkT_ready, count_ready = map(sem, ("wqk_transposed", "wqkT_ready", "count_ready"))
        slot_idx_ready, xsub_in, xobj_in, gsub_in = map(sem, ("slot_idx_ready", "xsub_in", "xobj_in", "gsub_in"))
        spread_ready, subs_spread, same_ready = map(sem, ("spread_ready", "subs_spread", "same_ready"))
        xsub_T, xobj_T, xsT_ready, xoT_ready, q_done, k_done = map(sem, ("xsub_T", "xobj_T", "xsT_ready", "xoT_ready", "q_done", "k_done"))
        cols_in, scores_ready, scores_spread = map(sem, ("cols_in", "scores_ready", "scores_spread"))
        live_done, exps_in, exps_done, shares_ready, mixed = map(sem, ("live_done", "exps_in", "exps_done", "shares_ready", "mixed"))
        qk_read, change_ready, change_T, dT_hi, dT_lo = map(sem, ("qk_read", "change_ready", "change_T", "dT_hi", "dT_lo"))
        dS_done, right_hi, right_lo, low_ready = map(sem, ("dS_done", "right_hi", "right_lo", "low_ready"))
        biased, out_done, z_ready, z_moments, z_root = map(sem, ("biased", "out_done", "z_ready", "z_moments", "z_root"))
        z_stats, z_normed, z_half_normed = map(sem, ("z_stats", "z_normed", "z_half_normed"))
        map_clear, map_idx_ready, map_zeroed, map_marked = map(sem, ("map_clear", "map_idx_ready", "map_zeroed", "map_marked"))
        general_in, rows_in, general_step = map(sem, ("general_in", "rows_in", "general_step"))
        turn = sem("turn")
        out_stored = [sem(f"out_stored{i}") for i in range(4)]

        block = ctx.enter_context(nc.Block())

        def rows(ap2d, t):
            return ap2d[t * P:t * P + width[t], :]

        KEYS = 1
        KEY_TURNS = 5
        ROWS = KEYS + T * KEY_TURNS
        HEAD_TURNS = 4
        TAIL = 5 + HEADS * HEAD_TURNS
        ROW_TURNS = TAIL + 9
        HALVES = ROWS + T * ROW_TURNS
        MIX = HALVES + 1
        MIX_TURNS = 2
        FINISHED = MIX + KF * MIX_TURNS
        ROW_STEPS = 7 + HEADS * 11 + 3 + 3

        def overflow(eng):
            eng.wait_ge(count_ready, 1)
            return eng.If(eng.value_load(count_i[0:1, 0:1], min_val=0, max_val=E) > SLOTS)

        def general_sp(sp):
            sp.wait_ge(turn, KEYS)
            for t in range(T):
                sp.dma_start(x32[0:width[t], t, :], rows(x, t)).then_inc(general_in, 16)
            sp.wait_ge(map_clear, 1)
            for t in range(T):
                sp.dma_start(rows(live_map, t), d_adj[0:width[t]]).then_inc(map_zeroed, 16)
            sp.wait_ge(map_marked, 16 * EC)
            for t in range(T):
                sp.wait_ge(turn, ROWS + t * ROW_TURNS)
                sp.dma_start(d_adj[0:width[t]], rows(adj, t)).then_inc(rows_in, 16)
                sp.dma_start(d_live[0:width[t]], rows(live_map, t)).then_inc(rows_in, 16)
            sp.wait_ge(turn, FINISHED)

        def general_pool(pool):
            pool.wait_ge(map_idx_ready, 1)
            pool.wait_ge(map_zeroed, 16 * T)
            for c in range(EC):
                nc.gpsimd.indirect_dma_start(
                    out=live_flat, out_offset=bass.IndirectOffsetOnAxis(ap=ed_idx[0:EP, c:c + 1], axis=0),
                    in_=ones[0:EP, 0:1], in_offset=None, bounds_check=N * N - 1, oob_is_err=False).then_inc(map_marked, 16)
                pool.wait_ge(map_marked, 16 * (c + 1))
            pool.wait_ge(turn, FINISHED)

        def general_pe(pe):
            mm = nc.tensor.matmul
            with pe.Fori(0, T) as t:
                at = KEYS + t * KEY_TURNS
                pe.wait_ge(turn, at + 1)
                for k in range(KF):
                    last = nc.tensor.transpose(tr[0][:, k * P:(k + 1) * P], d_x[:, k * P:(k + 1) * P], ident[:])
                last.then_inc(turn, 1)
                pe.wait_ge(turn, at + 3)
                for o in range(KF):
                    for k in range(KF):
                        last = mm(tr[1][:, o * P:(o + 1) * P], wT[:, 1, k, o * P:(o + 1) * P], d_xT[:, k * P:(k + 1) * P],
                                  start=(k == 0), stop=(k == KF - 1))
                last.then_inc(turn, 1)
            with pe.Fori(0, T) as t:
                at = ROWS + t * ROW_TURNS
                pe.wait_ge(turn, at + 1)
                for k in range(KF):
                    last = nc.tensor.transpose(tr[0][:, k * P:(k + 1) * P], d_x[:, k * P:(k + 1) * P], ident[:])
                last.then_inc(turn, 1)
                pe.wait_ge(turn, at + 3)
                for o in range(KF):
                    for k in range(KF):
                        last = mm(tr[1][:, o * P:(o + 1) * P], wT[:, 0, k, o * P:(o + 1) * P], d_xT[:, k * P:(k + 1) * P],
                                  start=(k == 0), stop=(k == KF - 1))
                last.then_inc(turn, 1)
                for h in range(HEADS):
                    lo, o = DK * (h % 2), h // 2
                    pe.wait_ge(turn, at + 5 + HEAD_TURNS * h)
                    for b, (i, j) in enumerate(SPANS):
                        last = mm(acc[b][:, 0:j - i], d_qT[lo:lo + DK, o * P:(o + 1) * P], kT[lo:lo + DK, o, i:j],
                                  start=True, stop=True)
                    last.then_inc(turn, 1)
                pe.wait_ge(turn, at + TAIL + 1)
                for k in range(T):
                    last = nc.tensor.transpose(tr[k // 4][0:width[k], (k % 4) * P:(k % 4 + 1) * P],
                                               d_share[:, k * P:k * P + width[k]], ident[:])
                last.then_inc(turn, 1)
                pe.wait_ge(turn, at + TAIL + 3)
                for k in range(T):
                    last = mm(acc[3][:, :], d_shareT[0:width[k], k, :], x32[0:width[k], k, :], start=(k == 0), stop=(k == T - 1))
                last.then_inc(turn, 1)
            with pe.Fori(0, KF) as f:
                pe.wait_ge(turn, MIX + f * MIX_TURNS)
                for b, (i, j) in enumerate(SPANS):
                    for k in range(T):
                        for half in range(2):
                            last = mm(acc[b][:, 0:j - i], x1s[0:width[k], half, k, bass.ts(f, P)], adjT[0:width[k], k, i:j],
                                      start=(k == 0 and half == 0), stop=(k == T - 1 and half == 1))
                last.then_inc(turn, 1)
            pe.wait_ge(turn, FINISHED)

        def general_act(act):
            A = nc.scalar
            with act.Fori(0, T) as t:
                at = KEYS + t * KEY_TURNS
                act.wait_ge(turn, at + 2)
                A.copy(d_xT, tr[0][:, :]).then_inc(turn, 1)
                act.wait_ge(turn, at + 4)
                for o in range(KF):
                    last = A.activation(kT[:, o, bass.ts(t, P)], tr[1][:, o * P:(o + 1) * P], ACT.Identity, bias=bias_col[:, 1, o:o + 1])
                last.then_inc(turn, 1)
            with act.Fori(0, T) as t:
                at = ROWS + t * ROW_TURNS
                act.wait_ge(turn, at + 2)
                A.copy(d_xT, tr[0][:, :]).then_inc(turn, 1)
                act.wait_ge(turn, at + 4)
                for o in range(KF):
                    last = A.activation(d_qT[:, o * P:(o + 1) * P], tr[1][:, o * P:(o + 1) * P], ACT.Identity, bias=bias_col[:, 0, o:o + 1])
                last.then_inc(turn, 1)
                for h in range(HEADS):
                    act.wait_ge(turn, at + 5 + HEAD_TURNS * h + 2)
                    A.activation(d_prob, d_score, ACT.Exp, bias=d_s[:, 4:5], accum_out=d_s[:, 7:8])
                    A.activation(d_s[:, 8:10], d_s[:, 5:7], ACT.Exp).then_inc(turn, 1)
                act.wait_ge(turn, at + TAIL + 2)
                for b in range(3):
                    n = min(4, T - 4 * b)
                    last = A.copy(d_shareT[:, 4 * b:4 * b + n, :], tr[b][:, 0:n * P].rearrange("p (k i) -> p k i", k=n))
                last.then_inc(turn, 1)
                act.wait_ge(turn, at + TAIL + 5)
                A.activation(d_st[:, 10:11], d_st[:, 7:8], ACT.Sqrt, bias=eps[:]).then_inc(turn, 1)
                act.wait_ge(turn, at + TAIL + 7)
                A.activation(d_x1, d_y, ACT.Identity, bias=d_st[:, 9:10], scale=d_st[:, 8:9]).then_inc(turn, 1)
            act.wait_ge(turn, FINISHED)

        def general_dve(dve):
            V = nc.vector
            done = 0
            k = 0
            base = 0

            def step(ins):
                nonlocal k
                k += 1
                ins.then_inc(general_step, 1)
                dve.wait_ge(general_step, base + k)

            dve.wait_ge(biased, T)
            dve.wait_ge(counts_stored, 16)
            for b in range(SUMS):
                dve.wait_ge(sums_stored[b], 16 * len(range(b, T, SUMS)))
            step(V.tensor_scalar(pos_all, flag[0:EP], -float(N * N), float(N * N), ALU.mult, ALU.add))
            step(V.tensor_tensor(pos_all, pos_all, ed_lin[0:EP], ALU.add))
            V.tensor_copy(ed_idx[0:EP], pos_all).then_inc(map_idx_ready, 1)
            V.memset(d_adj, 0.0).then_inc(map_clear, 1)
            V.memset(d_live, 0.0).then_inc(turn, 1)
            dve.wait_ge(general_in, 16 * T)
            done = k
            with dve.Fori(0, T) as t:
                at = KEYS + t * KEY_TURNS
                dve.wait_ge(turn, at)
                V.tensor_copy(d_x, x32[:, bass.ds(t, 1), :].rearrange("p o h -> p (o h)")).then_inc(turn, 1)
            s = d_s
            with dve.Fori(0, T) as t:
                base = done + t * ROW_STEPS
                k = 0
                at = ROWS + t * ROW_TURNS
                dve.wait_ge(turn, at)
                dve.wait_ge(rows_in, t * 32 + 32)
                V.tensor_copy(d_x, x32[:, bass.ds(t, 1), :].rearrange("p o h -> p (o h)"))
                step(V.tensor_copy(d_no[:], row_no[:, bass.ds(t, 1)]))
                step(V.reduce_sum(s[:, 0:1], d_adj, AX.X))
                step(V.reduce_sum(s[:, 1:2], d_live, AX.X))
                step(V.scalar_tensor_tensor(d_mask, col_no[:, 0:N], d_no[:], d_adj, ALU.is_equal, ALU.mult, accum_out=s[:, 2:3]))
                step(V.tensor_tensor(s[:, 0:1], s[:, 0:1], s[:, 1:2], ALU.subtract))
                step(V.tensor_tensor(s[:, 3:4], s[:, 0:1], s[:, 2:3], ALU.subtract))
                step(V.memset(s[:, 12:14], 0.0))
                V.tensor_scalar(d_mask, d_live, -1.0, -GONE, ALU.add, ALU.mult).then_inc(turn, 1)
                for h in range(HEADS):
                    here = at + 5 + HEAD_TURNS * h
                    dve.wait_ge(turn, here + 1)
                    for b, (i, j) in enumerate(SPANS):
                        step(V.scalar_tensor_tensor(d_score[:, i:j], acc[b][:, 0:j - i], 1.0 / float(np.sqrt(DK)), d_mask[:, i:j],
                                                    ALU.mult, ALU.add))
                    step(V.reduce_max(s[:, 10:11], d_score, AX.X))
                    step(V.tensor_scalar(s[:, 4:5], s[:, 10:11], TINY, -1.0, ALU.max, ALU.mult))
                    step(V.tensor_scalar(s[:, 5:6], s[:, 4:5], 1.0, None, ALU.mult))
                    V.tensor_scalar(s[:, 6:7], s[:, 4:5], TINY, None, ALU.add).then_inc(turn, 1)
                    dve.wait_ge(turn, here + 3)
                    step(V.scalar_tensor_tensor(s[:, 11:12], s[:, 8:9], s[:, 3:4], s[:, 7:8], ALU.mult, ALU.add))
                    step(V.tensor_tensor(s[:, 11:12], s[:, 11:12], s[:, 9:10], ALU.add))
                    step(V.reciprocal(s[:, 14:15], s[:, 11:12]))
                    step(V.tensor_scalar(s[:, 14:15], s[:, 14:15], 1.0 / HEADS, None, ALU.mult))
                    step(V.scalar_tensor_tensor(s[:, 12:14], s[:, 8:10], s[:, 14:15], s[:, 12:14], ALU.mult, ALU.add))
                    if h == 0:
                        ins = V.tensor_scalar(d_share, d_prob, s[:, 14:15], None, ALU.mult)
                    else:
                        ins = V.scalar_tensor_tensor(d_share, d_prob, s[:, 14:15], d_share, ALU.mult, ALU.add)
                    ins.then_inc(turn, 1)
                dve.wait_ge(turn, at + TAIL)
                step(V.tensor_tensor(d_live, d_adj, d_live, ALU.subtract))
                step(V.tensor_tensor(s[:, 15:16], s[:, 12:13], s[:, 2:3], ALU.mult))
                step(V.scalar_tensor_tensor(s[:, 16:17], s[:, 13:14], 1.0, s[:, 15:16], ALU.add, ALU.subtract))
                V.scalar_tensor_tensor(d_share, d_live, s[:, 12:13], d_share, ALU.mult, ALU.add).then_inc(turn, 1)
                dve.wait_ge(turn, at + TAIL + 4)
                step(V.scalar_tensor_tensor(d_y, d_x, s[:, 16:17], acc[3][:, :], ALU.mult, ALU.add))
                step(V.bn_stats(d_st[:, 0:6], d_y))
                V.tensor_copy(s[:, 17:18], s[:, 16:17])
                V.bn_aggr(d_st[:, 6:8], d_st[:, 0:6]).then_inc(turn, 1)
                dve.wait_ge(turn, at + TAIL + 6)
                step(V.reciprocal(d_st[:, 8:9], d_st[:, 10:11]))
                V.tensor_scalar(d_st[:, 9:10], d_st[:, 6:7], -1.0, d_st[:, 8:9], ALU.mult, ALU.mult).then_inc(turn, 1)
                dve.wait_ge(turn, at + TAIL + 8)
                V.tensor_copy(x_sb[:, bass.ds(t, 1), :].rearrange("p o h -> p (o h)"), d_x1).then_inc(turn, 1)
                assert k == ROW_STEPS, k
            with dve.Fori(0, T) as t:
                base = done + T * ROW_STEPS + t * 2
                k = 0
                tile = x_sb[:, bass.ds(t, 1), :]
                step(V.tensor_scalar(x1s[:, 0, bass.ds(t, 1), :], tile, XS, None, ALU.mult))
                step(V.scalar_tensor_tensor(x1s[:, 1, bass.ds(t, 1), :], tile, XS, x1s[:, 0, bass.ds(t, 1), :],
                                            ALU.mult, ALU.subtract))
                V.tensor_tensor(tile, tile, bias[:, :].unsqueeze(1), ALU.add)
            V.memset(mix[:, :, :, N:NP], 0.0).then_inc(turn, 1)
            with dve.Fori(0, KF) as f:
                base = done + T * (ROW_STEPS + 2) + f * 3
                k = 0
                at = MIX + f * MIX_TURNS
                dve.wait_ge(turn, at + 1)
                for b, (i, j) in enumerate(SPANS):
                    high = mix[:, 0, bass.ds(f, 1), i:j].rearrange("p o i -> p (o i)")
                    low = mix[:, 1, bass.ds(f, 1), i:j].rearrange("p o i -> p (o i)")
                    step(V.tensor_scalar(high, acc[b][:, 0:j - i], 1.0 / XS, None, ALU.mult))
                    last = V.scalar_tensor_tensor(low, acc[b][:, 0:j - i], 1.0 / XS, high, ALU.mult, ALU.subtract)
                last.then_inc(turn, 1)
            dve.wait_ge(turn, FINISHED)

        def out_bank(t):
            return (acc[3], tr[1], acc[2], acc[4], acc[0], acc[1])[t % OUTS]

        def last_bank(half):
            return (out_bank(T - 1), tr[0])[half]

        def sum_bank(i):
            return (acc[0], acc[1], tr[2])[i % 3]

        def mix_bank(u):
            return acc[(2, 4, 0, 1)[u % 4]]

        def wqk_at(i):
            return (i - 3,) if 3 <= i < 11 else ()

        def y4(t):
            return (y if t % 4 < 2 else xd)[:, t % 2, :]

        def number(pe, n):
            a, b = CHUNKS[n], CHUNKS[n + 1]
            pe.wait_ge(flags_ready, n + 1)
            nc.tensor.matmul(acc[3][:, PRE:PRE + b - a], below16[0:EP, :], flag[0:EP, a:b], start=True, stop=True)
            nc.tensor.matmul(acc[3][:, TOT:TOT + b - a], ones16[0:EP, :], flag[0:EP, a:b], start=True, stop=True).then_inc(numbered, 1)

        def compact(pe, n):
            a, b = CHUNKS[n], CHUNKS[n + 1]
            pe.wait_ge(onehot_ready, n + 1)
            for c in range(a, b):
                last = nc.tensor.matmul(acc[3][:, CMP + 3 * n:CMP + 3 * n + 3], onehot[0:EP, c - a:P * CHUNK:CHUNK], ed3[0:EP, c, :],
                                        start=(c == a), stop=(c == b - 1))
            last.then_inc(compacted, 1)

        def chunk_of(c):
            return max(n for n in range(NC) if CHUNKS[n] <= c)

        @block.sync
        def _(sp):
            sp.dma_start(ed_i[0:EP], pairs.rearrange("(p c) two -> p c two", p=EP)).then_inc(edges_loaded, 16)
            sp.dma_start(stage[:, 0, :], rows(adj, 0)).then_inc(adj_loaded[0], 16)
            for g in range(3):
                if g == 1:
                    sp.dma_start(stage[:, 1, :], rows(adj, 1)).then_inc(adj_loaded[1], 16)
                sp.dma_start(x_sb[:, 3 * g:3 * g + 3, :],
                             x[3 * g * P:(3 * g + 3) * P, :].rearrange("(t p) h -> p t h", p=P)).then_inc(x_loaded[g], 16)
            sp.dma_start(x_sb[:, 9, :], rows(x, 9)).then_inc(x_loaded[3], 16)
            sp.wait_ge(pad_zeroed, 1)
            sp.dma_start(x_sb[0:LAST, T - 1, :], rows(x, T - 1)).then_inc(x_loaded[3], 16)

            for t in range(2, T):
                if t >= RING:
                    sp.wait_ge(adj_cast, t - RING + 1)
                sp.dma_start(stage[0:width[t], t % RING, :], rows(adj, t)).then_inc(adj_loaded[t % RING], 16)
                if t == 3:
                    sp.dma_start(wraw[:, 0], wq.rearrange("(k p) i -> p k i", p=P)).then_inc(wq_loaded, 16)
                if t == 6:
                    sp.dma_start(wraw[:, 1], wk.rearrange("(k p) i -> p k i", p=P)).then_inc(wk_loaded, 16)
            sp.dma_start(wraw[:, 2], w1.rearrange("(k p) o -> p k o", p=P)).then_inc(w1_loaded, 16)
            sp.dma_start(bias[:, :], b1.partition_broadcast(P)).then_inc(bias_loaded, 16)
            for n, b in enumerate((bq, bk)):
                for k in range(KF):
                    sp.dma_start(bias_col[:, n, k:k + 1], b[k * P:(k + 1) * P].rearrange("(p o) -> p o", o=1)).then_inc(bias_loaded, 16)
            sp.wait_ge(adjT_ready, 2 * T)
            for k in range(T):
                if k >= 2:
                    sp.wait_ge(adjT_stored[k % 2], 16 * (k // 2))
                sp.dma_start(adjT_dram[k * P:(k + 1) * P, :], adjT[:, k, :]).then_inc(adjT_stored[k % 2], 16)
            with overflow(sp):
                general_sp(sp)
            for t in range(T):
                sp.wait_ge(z_normed, t + 1)
                if t == T - 1:
                    sp.wait_ge(z_half_normed, 1)
                sp.dma_start(rows(out, t), y4(t)[0:width[t]]).then_inc(out_stored[t % 4], 16)
            for b in range(4):
                sp.wait_ge(out_stored[b], 16 * len(range(b, T, 4)))

        @block.gpsimd
        def _(pool):
            nc.gpsimd.memset(x_sb[64:P, T - 1, :], 0.0).then_inc(pad_zeroed, 1)
            pool.wait_ge(pad_zeroed, 1)
            nc.gpsimd.memset(eps[:], EPS).then_inc(consts, 1)
            nc.gpsimd.memset(ident[:], 0.0).then_inc(pool_step, 1)
            nc.gpsimd.memset(ones[:], 1.0).then_inc(pool_step, 1)
            nc.gpsimd.memset(ones16[:], 1.0).then_inc(pool_step, 1)
            pool.wait_ge(pool_step, 3)
            nc.gpsimd.affine_select(out=ident[:], in_=ident[:], compare_op=ALU.not_equal, fill=1.0,
                                    base=0, pattern=[[-1, P]], channel_multiplier=1).then_inc(consts, 1)
            nc.gpsimd.affine_select(out=ident16[:], in_=ones16[:], compare_op=ALU.is_equal, fill=0.0,
                                    base=0, pattern=[[-1, P]], channel_multiplier=1).then_inc(consts, 1)
            nc.gpsimd.affine_select(out=below16[:], in_=ones16[:], compare_op=ALU.is_gt, fill=0.0,
                                    base=0, pattern=[[1, P]], channel_multiplier=-1).then_inc(consts, 1)
            nc.gpsimd.iota(slot_of[:].rearrange("p (a b) -> p a b", a=2), pattern=[[0, 2], [1, SLOTS]], base=0, channel_multiplier=0,
                           allow_small_or_imprecise_dtypes=True).then_inc(consts, 1)
            pool.wait_ge(idx_ready, 1)
            for c in range(EC):
                nc.gpsimd.indirect_dma_start(
                    out=ed_adj[0:EP, c:c + 1], out_offset=None, in_=adj_flat,
                    in_offset=bass.IndirectOffsetOnAxis(ap=ed_idx[0:EP, c:c + 1], axis=0)).then_inc(edges_looked_up[chunk_of(c)], 16)
            nc.gpsimd.memset(earlier[:], 1.0).then_inc(late_consts, 1)
            for n in range(NC):
                pool.wait_ge(edges_looked_up[n], 16 * (CHUNKS[n + 1] - CHUNKS[n]))
            for half in range(2):
                pool.wait_ge(late_consts, 1 + half)
                part = earlier[64 * half:64 * half + 64, :]
                nc.gpsimd.affine_select(out=part, in_=part, compare_op=ALU.is_gt, fill=0.0,
                                        base=0, pattern=[[-1, SLOTS]], channel_multiplier=1).then_inc(late_consts, 1)
            pool.wait_ge(late_consts, 3)
            nc.gpsimd.iota(row_no[:], pattern=[[P, T]], base=0, channel_multiplier=1,
                           allow_small_or_imprecise_dtypes=True).then_inc(late_consts, 1)
            nc.gpsimd.iota(col_no[:], pattern=[[1, NP]], base=0, channel_multiplier=0,
                           allow_small_or_imprecise_dtypes=True).then_inc(late_consts, 1)
            pool.wait_ge(slot_idx_ready, 1)
            pool.wait_ge(w1_lo, 1)
            nc.gpsimd.indirect_dma_start(
                out=xobj, out_offset=None, in_=x,
                in_offset=bass.IndirectOffsetOnAxis(ap=slot_i[:, 1:2], axis=0)).then_inc(xobj_in, 16)
            nc.gpsimd.indirect_dma_start(
                out=xsub, out_offset=None, in_=x,
                in_offset=bass.IndirectOffsetOnAxis(ap=slot_i[:, 0:1], axis=0)).then_inc(xsub_in, 16)
            pool.wait_ge(wqkT_ready, 8)
            pool.wait_ge(counts_stored, 16)
            for b in range(SUMS):
                pool.wait_ge(sums_stored[b], 16 * len(range(b, T, SUMS)))
            nc.gpsimd.indirect_dma_start(
                out=gsub, out_offset=None, in_=sums_dram,
                in_offset=bass.IndirectOffsetOnAxis(ap=slot_i[:, 0:1], axis=0)).then_inc(gsub_in, 16)
            for b in range(2):
                pool.wait_ge(adjT_stored[b], 16 * len(range(b, T, 2)))
            nc.gpsimd.indirect_dma_start(
                out=stackL[0:64, :], out_offset=None, in_=adjT_dram,
                in_offset=bass.IndirectOffsetOnAxis(ap=slot_i[0:64, 0:1], axis=0)).then_inc(cols_in, 16)
            pool.wait_ge(same_ready, 1)
            pool.wait_ge(late_consts, 5)
            for rows_in in (xsub_in, xobj_in, cols_in, gsub_in):
                pool.wait_ge(rows_in, 16)
            nc.gpsimd.tensor_scalar(stackL[64:P, :], col_no[64:P, :], slot[64:P, 3:4], None, ALU.is_equal).then_inc(low_ready, 1)
            pool.wait_ge(low_ready, 1)
            pool.wait_ge(bias_loaded, 16 * BIASES)
            pool.wait_ge(x1_lo, T)
            with pool.Fori(0, T) as t:
                tile = x_sb[:, bass.ds(t, 1), :].rearrange("p o h -> p (o h)")
                nc.gpsimd.tensor_tensor(tile, tile, bias[:, :], ALU.add).then_inc(biased, 1)
            with overflow(pool):
                general_pool(pool)

        @block.scalar
        def _(act):
            def copy_adjT(t):
                for b in range(2):
                    n = min(8, T - 8 * b)
                    act.wait_ge(adj_transposed, 2 * t + b + 1)
                    nc.scalar.copy(adjT[:, 8 * b:8 * b + n, t * P:(t + 1) * P],
                                   tr16[b][:, 0:n * P].rearrange("p (k i) -> p k i", k=n)).then_inc(adjT_ready, 1)

            def cast_adj(t):
                act.wait_ge(adj_loaded[t % RING], 16 * (t // RING + 1))
                if t >= CASTS:
                    act.wait_ge(adj_transposed, 2 * (t - CASTS + 1))
                    act.wait_ge(adj_read, t - CASTS + 1)
                nc.scalar.activation(adj16[:, t % CASTS, :], stage[:, t % RING, :], ACT.Copy,
                                     accum_out=counts[:, t, 0:1]).then_inc(adj_cast, 1)

            def root(s):
                return nc.scalar.activation(s[:, 10:11], s[:, 7:8], ACT.Sqrt, bias=eps[:])

            def high_x(g):
                act.wait_ge(x_loaded[g], 16 if g < 3 else 32)
                for t in range(3 * g, min(3 * g + 3, T)):
                    nc.scalar.mul(xs[:, 0, t, :], x_sb[:, t, :], XS).then_inc(x_hi, 1)

            def own_share(i):
                act.wait_ge(coefs_ready, i + 1)
                if i >= 2:
                    act.wait_ge(y_ready, i - 1)
                nc.scalar.mul(xd[:, i % 2, :], x_sb[:, i, :], co[:, i % COEFS, 4:5]).then_inc(xd_ready, 1)

            act.wait_ge(consts, 1)
            nc.scalar.activation(table_loader[:, 0:1], eps[:], ACT.Sqrt)
            cast_adj(0)
            act.wait_ge(tr_zeroed, 1)
            copy_adjT(0)
            cast_adj(1)
            copy_adjT(1)
            high_x(2)
            high_x(3)
            cast_adj(2)
            own_share(0)
            cast_adj(3)
            copy_adjT(2)

            def normalise(i):
                act.wait_ge(stats_ready, i + 1)
                nc.scalar.activation(x_sb[:, i, :], y[:, i % 2, :], ACT.Identity, bias=st[:, i % 2, 9:10],
                                     scale=st[:, i % 2, 8:9]).then_inc(x1_ready, 1)

            def take_sums(i):
                act.wait_ge(sums_done, i + 1)
                if i >= SUMS:
                    act.wait_ge(sums_stored[i % SUMS], 16 * (i // SUMS))
                nc.scalar.copy(sums[:, i % SUMS, :], sum_bank(i)[:, :]).then_inc(sums_copied, 1)
                if 1 <= i and i + 2 < T:
                    copy_adjT(i + 2)
                if i + 1 < T:
                    own_share(i + 1)

            def take_root(i):
                act.wait_ge(moments_ready, i + 1)
                root(st[:, i % 2]).then_inc(root_ready, 1)

            def store_sums(i):
                act.wait_ge(sums_copied, i + 1)
                act.dma_start(sums_dram[i * P:(i + 1) * P, 0:H], sums[:, i % SUMS, :]).then_inc(sums_stored[i % SUMS], 16)

            take_sums(0)
            take_sums(1)
            take_root(0)
            cast_adj(4)
            store_sums(0)
            normalise(0)
            take_root(1)
            normalise(1)
            store_sums(1)
            for i in range(2, T):
                if i >= 3:
                    normalise(i - 1)
                take_sums(i)
                if i == 2:
                    cast_adj(i + 3)
                take_root(i)
                if 2 < i < T - 3:
                    cast_adj(i + 3)
                for n in wqk_at(i):
                    act.wait_ge(wqk_transposed, n + 1)
                    nc.scalar.copy(wT[:, n // 4, n % 4, :], acc[(2, 4)[n % 2]][:, :]).then_inc(wqkT_ready, 1)
                store_sums(i)
            act.wait_ge(adj_read, T)
            act.dma_start(sums_dram.rearrange("(t p) c -> p t c", p=P)[:, :, H:GW], counts[:, :, :]).then_inc(counts_stored, 16)
            normalise(T - 1)

            def mix_high(u):
                i, j = SPANS[u // KF]
                act.wait_ge(mix_done, u + 1)
                nc.scalar.mul(mix[:, 0, u % KF, i:j], mix_bank(u)[:, 0:j - i], 1.0 / XS).then_inc(mix_hi, 1)

            act.wait_ge(w1_loaded, 16)
            nc.scalar.mul(whl[:, 0], wraw[:, 2], WS).then_inc(w1_hi, 1)
            mix_high(0)
            mix_high(1)
            mix_high(2)
            act.wait_ge(xsub_T, 1)
            nc.scalar.copy(xsT, tr[1][:, 0:KF * SLOTS]).then_inc(xsT_ready, 1)
            mix_high(3)
            act.wait_ge(k_done, 1)
            act.wait_ge(bias_loaded, 16 * BIASES)
            for k in range(KF):
                last = nc.scalar.activation(kT_slots[:, k * SLOTS:(k + 1) * SLOTS], tr[2][:, k * SLOTS:(k + 1) * SLOTS],
                                            ACT.Identity, bias=bias_col[:, 1, k:k + 1])
            last.then_inc(keys_ready, 1)
            nc.scalar.activation(table_loader[:, 1:2], eps[:], ACT.Exp)
            act.wait_ge(exps_in, 1)
            nc.scalar.activation(score, score, ACT.Exp).then_inc(exps_done, 1)
            nc.scalar.activation(table_loader[:, 2:3], eps[:], ACT.Sqrt)
            act.wait_ge(slot_moments, 1)
            root(st[:, 0]).then_inc(slot_root, 1)
            mix_high(4)
            mix_high(5)
            act.wait_ge(slot_moments, 2)
            root(st[:, 1]).then_inc(slot_root, 1)
            mix_high(6)
            act.wait_ge(change_T, 1)
            nc.scalar.mul(dT[:, 0, :], tr[0][:, 0:KF * SLOTS], XS).then_inc(dT_hi, 1)
            act.wait_ge(change_ready, 1)
            nc.scalar.mul(stackR[64:P, 0, :], dx1[64:P, :], WS).then_inc(right_hi, 1)
            mix_high(7)
            act.wait_ge(dS_done, 1)
            nc.scalar.mul(stackR[0:64, 0, :], tr[2][0:64, :], 1.0 / XS).then_inc(right_hi, 1)
            mix_high(8)
            mix_high(9)
            mix_high(10)
            mix_high(11)
            with overflow(act):
                general_act(act)
            for t in range(T):
                act.wait_ge(z_moments, t + 1)
                root(st[:, t % 2]).then_inc(z_root, 1)
                act.wait_ge(z_stats, t + 1)
                part = y4(t) if t < T - 1 else y4(t)[:, 0:HALF]
                nc.scalar.activation(part, part, ACT.Identity, bias=st[:, t % 2, 9:10],
                                     scale=st[:, t % 2, 8:9]).then_inc(z_normed, 1)

        @block.vector
        def _(dve):
            steps = 0

            def step(ins):
                nonlocal steps
                steps += 1
                ins.then_inc(dve_step, 1)
                dve.wait_ge(dve_step, steps)

            V = nc.vector
            V.memset(tr[1][:, :], 0.0).then_inc(tr_zeroed, 1)
            dve.wait_ge(edges_loaded, 16)
            e_i, e, o2, eok = ed_i[0:EP], ed[0:EP], ok2[0:EP], ed_ok[0:EP]
            step(V.tensor_copy(e, e_i))
            step(V.tensor_scalar(o2, e, 0.0, float(N), ALU.is_lt, ALU.mult))
            step(V.tensor_tensor(e, e, o2, ALU.add))
            step(V.tensor_scalar(o2, e, float(N), None, ALU.is_lt))
            step(V.scalar_tensor_tensor(o2, e, 0.0, o2, ALU.is_ge, ALU.mult))
            ein, lin = ed_in[0:EP], ed_lin[0:EP]
            step(V.tensor_tensor(ein, o2[:, :, 0], o2[:, :, 1], ALU.mult))
            step(V.scalar_tensor_tensor(lin, e[:, :, 0], float(N), e[:, :, 1], ALU.mult, ALU.add))
            step(V.tensor_tensor(lin, lin, ein, ALU.mult))
            V.tensor_copy(ed_idx[0:EP], lin).then_inc(idx_ready, 1)
            step(V.tensor_tensor(eok, e[:, :, 0], e[:, :, 1], ALU.not_equal))
            step(V.tensor_tensor(eok, eok, ein, ALU.mult))
            V.memset(ed3[0:EP, :, 2:3], 1.0).then_inc(dve_step, 1)
            steps += 1
            step(V.tensor_tensor(ed3[0:EP, :, 0:2], e, ein.unsqueeze(2).broadcast_to([EP, EC, 2]), ALU.mult))
            def split_x(g):
                tiles = range(3 * g, min(3 * g + 3, T))
                if g < 2:
                    dve.wait_ge(x_loaded[g], 16)
                    step(V.tensor_scalar(xs[:, 0, tiles[0]:tiles[-1] + 1, :], x_sb[:, tiles[0]:tiles[-1] + 1, :], XS, None, ALU.mult))
                for n, t in enumerate(tiles):
                    if g >= 2:
                        dve.wait_ge(x_hi, 3 * (g - 2) + n + 1)
                    V.scalar_tensor_tensor(xs[:, 1, t, :], x_sb[:, t, :], XS, xs[:, 0, t, :],
                                           ALU.mult, ALU.subtract).then_inc(x_lo, 1)

            def coefs(t):
                c, s = co[:, t % COEFS], counts[:, t]
                dve.wait_ge(adj_cast, t + 1)
                if t >= COEFS:
                    dve.wait_ge(xd_ready, t - COEFS + 1)
                V.scalar_tensor_tensor(junk16[:, 0:width[t]], adj16[:, t % CASTS, t * P:t * P + width[t]], 1.0,
                                       ident16[:, 0:width[t]], ALU.mult, ALU.mult, accum_out=s[:, 1:2]).then_inc(adj_read, 1)
                dve.wait_ge(adj_read, t + 1)
                step(V.tensor_scalar(c[:, 0:1], s[:, 1:2], -A0, 1.0, ALU.mult, ALU.add))
                step(V.scalar_tensor_tensor(c[:, 1:2], s[:, 0:1], A0, c[:, 0:1], ALU.mult, ALU.add))
                step(V.reciprocal(c[:, 2:3], c[:, 1:2]))
                V.tensor_scalar(c[:, 5:6], c[:, 2:3], A0 / XS, None, ALU.mult)
                V.tensor_scalar(c[:, 4:5], c[:, 0:1], c[:, 2:3], 1.0, ALU.mult, ALU.add).then_inc(coefs_ready, 1)

            def moments(s, v):
                step(V.bn_stats(s[:, 0:6], v))
                return V.bn_aggr(s[:, 6:8], s[:, 0:6])

            def scale_shift(s):
                step(V.reciprocal(s[:, 8:9], s[:, 10:11]))
                return V.tensor_scalar(s[:, 9:10], s[:, 6:7], -1.0, s[:, 8:9], ALU.mult, ALU.mult)

            def flag_chunk(n):
                a, b = CHUNKS[n], CHUNKS[n + 1]
                dve.wait_ge(edges_looked_up[n], 16 * (b - a))
                V.scalar_tensor_tensor(flag[0:EP, a:b], ed_adj[0:EP, a:b], 1.0, eok[:, a:b],
                                       ALU.is_equal, ALU.mult).then_inc(flags_ready, 1)

            def number_chunk(n):
                a, b = CHUNKS[n], CHUNKS[n + 1]
                m = b - a
                dve.wait_ge(numbered, n + 1)
                step(V.tensor_tensor_scan(seen[:, a:b], ones[:, 0:m], acc[3][:, TOT:TOT + m],
                                          seen[:, a - 1:a] if n else 0.0, ALU.mult, ALU.add))
                step(V.tensor_tensor(pos[:, 0, 0:m], seen[:, a:b], acc[3][:, TOT:TOT + m], ALU.subtract))
                step(V.tensor_tensor(pos[:, 1, 0:m], pos[:, 0, 0:m], acc[3][:, PRE:PRE + m], ALU.add))
                step(V.tensor_scalar(pos[0:EP, 2, 0:m], flag[0:EP, a:b], -FAR, FAR, ALU.mult, ALU.add))
                step(V.tensor_tensor(pos16[0:EP, 0:m], pos[0:EP, 1, 0:m], pos[0:EP, 2, 0:m], ALU.add))
                if n:
                    dve.wait_ge(compacted, n)
                V.tensor_tensor(onehot[0:EP, 0:P * CHUNK].rearrange("p (f c) -> p f c", f=P)[:, :, 0:m],
                                pos16[0:EP, 0:m].unsqueeze(1).broadcast_to([EP, P, m]),
                                slot_no[0:EP, :, 0:m], ALU.is_equal).then_inc(onehot_ready, 1)

            def mix_low(u):
                i, j = SPANS[u // KF]
                dve.wait_ge(mix_hi, u + 1)
                V.scalar_tensor_tensor(mix[:, 1, u % KF, i:j], mix_bank(u)[:, 0:j - i], 1.0 / XS, mix[:, 0, u % KF, i:j],
                                       ALU.mult, ALU.subtract).then_inc(mix_lo, 1)

            fits = slot[:, 8:9]
            dve.wait_ge(consts, 5)
            split_x(0)
            split_x(1)
            coefs(0)
            split_x(2)
            split_x(3)
            coefs(1)
            coefs(2)
            coefs(3)
            step(V.tensor_copy(slot_no[:, :, :], slot_of[:, :].unsqueeze(2).broadcast_to([P, P, CHUNK])))

            def add_own(i):
                dve.wait_ge(sums_copied, i + 1)
                dve.wait_ge(xd_ready, i + 1)
                if i >= 2:
                    dve.wait_ge(x1_ready, i - 1)
                V.scalar_tensor_tensor(y[:, i % 2, :], sum_bank(i)[:, :], co[:, i % COEFS, 5:6], xd[:, i % 2, :],
                                       ALU.mult, ALU.add).then_inc(y_ready, 1)
                dve.wait_ge(y_ready, i + 1)
                moments(st[:, i % 2], y[:, i % 2, :]).then_inc(moments_ready, 1)

            def scale_shift_of(i):
                dve.wait_ge(root_ready, i + 1)
                scale_shift(st[:, i % 2]).then_inc(stats_ready, 1)

            def split_x1(i):
                dve.wait_ge(x1_ready, i + 1)
                V.tensor_scalar(x1s[:, 0, i, :], x_sb[:, i, :], XS, None, ALU.mult).then_inc(x1_hi, 1)
                dve.wait_ge(x1_hi, i + 1)
                V.scalar_tensor_tensor(x1s[:, 1, i, :], x_sb[:, i, :], XS, x1s[:, 0, i, :],
                                       ALU.mult, ALU.subtract).then_inc(x1_lo, 1)

            add_own(0)
            add_own(1)
            scale_shift_of(0)
            scale_shift_of(1)
            coefs(4)
            split_x1(0)
            for i in range(2, T):
                if i in FLAGGED_AT:
                    flag_chunk(FLAGGED_AT[i])
                if i == T - 1:
                    split_x1(i - 1)
                add_own(i)
                scale_shift_of(i)
                if i < T - 1:
                    split_x1(i - 1)
                if i + 3 < T:
                    coefs(i + 3)
                if i in NUMBERED_AT:
                    number_chunk(NUMBERED_AT[i])
            split_x1(T - 1)
            number_chunk(NUMBERED_AT[T])
            flag_chunk(NUMBERED_AT[T + 1])
            V.memset(mix[:, :, :, N:NP], 0.0)
            number_chunk(NUMBERED_AT[T + 1])
            dve.wait_ge(w1_hi, 1)
            V.scalar_tensor_tensor(whl[:, 1], wraw[:, 2], WS, whl[:, 0], ALU.mult, ALU.subtract).then_inc(w1_lo, 1)
            mix_low(0)
            flag_chunk(NUMBERED_AT[T + 2])
            number_chunk(NUMBERED_AT[T + 2])
            V.tensor_copy(count_i[:], seen[:, EC - 1:EC]).then_inc(count_ready, 1)
            step(V.tensor_scalar(fits, seen[:, EC - 1:EC], float(SLOTS), None, ALU.is_le))
            dve.wait_ge(compacted, NC)
            step(V.tensor_reduce(slot[:, 0:3], acc[3][:, CMP:CMP + 3 * NC].rearrange("p (n v) -> p v n", v=3),
                                 AX.X, ALU.add))
            V.tensor_copy(slot_i[:], slot[:, 0:2]).then_inc(slot_idx_ready, 1)
            sub, key, valid = slot[:, 3:4], slot[:, 4:5], slot[:, 2:3]
            step(V.tensor_scalar(slot[:, 5:6], valid, -1.0, FAR, ALU.add, ALU.mult))
            step(V.tensor_tensor(sub, slot[:, 0:1], slot[:, 5:6], ALU.add))
            step(V.scalar_tensor_tensor(key, sub, 2048.0, slot[:, 1:2], ALU.mult, ALU.add))
            eye = ident[0:64, 0:64]
            step(V.tensor_scalar(spread[0:64, 0:64], eye, sub[0:64], None, ALU.mult))
            step(V.tensor_scalar(spread[0:64, 64:128], eye, sub[0:64], None, ALU.mult))
            V.tensor_scalar(spread[0:64, 128:192], eye, key[0:64], None, ALU.mult).then_inc(spread_ready, 1)
            mix_low(1)
            dve.wait_ge(late_consts, 4)
            V.tensor_scalar(head_of[:, 0:1], row_no[:, 0:1], float(DK), None, ALU.is_lt)
            V.tensor_scalar(head_of[:, 1:2], row_no[:, 0:1], float(DK), None, ALU.is_ge)
            dve.wait_ge(subs_spread, 1)
            step(V.tensor_scalar(same, tr[0][:, 0:P], sub, None, ALU.is_equal))
            V.tensor_scalar(keq, tr[0][:, P:P + SLOTS], key, None, ALU.is_equal).then_inc(same_ready, 1)
            dve.wait_ge(same_ready, 1)
            dup_row, dup_key, rep, keep = small[:, 0:1], small[:, 1:2], small[:, 2:3], small[:, 3:4]
            junk = small[:, 16:80]
            step(V.tensor_tensor_reduce(out=junk, in0=same[:, 0:SLOTS], in1=earlier[:], scale=1.0, scalar=0.0,
                                        op0=ALU.mult, op1=ALU.max, accum_out=dup_row))
            step(V.tensor_tensor_reduce(out=junk, in0=keq, in1=earlier[:], scale=1.0, scalar=0.0,
                                        op0=ALU.mult, op1=ALU.max, accum_out=dup_key))
            step(V.scalar_tensor_tensor(rep, dup_row, 0.0, valid, ALU.is_equal, ALU.mult))
            step(V.tensor_tensor(rep, rep, fits, ALU.mult))
            step(V.scalar_tensor_tensor(keep, dup_key, 0.0, valid, ALU.is_equal, ALU.mult))
            dve.wait_ge(xobj_T, 1)
            dve.wait_ge(wqkT_ready, 8)
            V.tensor_copy(xoT, tr[2][:, 0:KF * SLOTS]).then_inc(xoT_ready, 1)
            mix_low(2)
            mix_low(3)
            dve.wait_ge(bias_loaded, 16 * BIASES)
            dve.wait_ge(q_done, 1)
            dve.wait_ge(keys_ready, 1)
            for k in range(KF):
                last = V.scalar_tensor_tensor(qk[:, k], tr[1][:, k * SLOTS:(k + 1) * SLOTS].unsqueeze(1).broadcast_to([P, 2, SLOTS]),
                                              bias_col[:, 0, k:k + 1],
                                              kT_slots[:, k * SLOTS:(k + 1) * SLOTS].unsqueeze(1).broadcast_to([P, 2, SLOTS]),
                                              ALU.add, ALU.mult)
            last.then_inc(qk_read, 1)
            sc = small[:, 4:12]
            gone = slot[:, 6:7]
            step(V.tensor_scalar(gone, keep, -1.0, -GONE, ALU.add, ALU.mult))
            dve.wait_ge(dots_done, 1)
            step(V.tensor_scalar(sc, tr[2][:, 0:HEADS], 1.0 / np.sqrt(DK), keep, ALU.mult, ALU.mult))
            step(V.tensor_scalar(sc, sc, gone, None, ALU.add))
            V.tensor_tensor(spread[0:64].rearrange("p (h g) -> p h g", h=HEADS), eye.unsqueeze(1).broadcast_to([64, HEADS, SLOTS]),
                            sc[0:64].unsqueeze(2).broadcast_to([64, HEADS, SLOTS]), ALU.mult).then_inc(scores_ready, 1)
            step(V.tensor_scalar(keq, same[:, 0:SLOTS], -1.0, -GONE, ALU.add, ALU.mult))
            V.memset(score[:, :, SLOTS:SLOTS + 1], 0.0).then_inc(dve_step, 1)
            V.memset(score[:, :, SLOTS + 1:SLOTS + 2], TINY).then_inc(dve_step, 1)
            steps += 2
            step(V.tensor_copy(score[:, :, SLOTS + 2], sc))
            dve.wait_ge(scores_spread, 1)
            step(V.tensor_tensor(score[:, :, 0:SLOTS], tr[1][:, :].rearrange("p (h g) -> p h g", h=HEADS),
                                 keq.unsqueeze(1).broadcast_to([P, HEADS, SLOTS]), ALU.add))
            top = small[:, 16:24]
            step(V.reduce_max(top, score[:, :, 0:SLOTS + 2], AX.X))
            V.tensor_tensor(score, score, top.unsqueeze(2).broadcast_to([P, HEADS, EXTRA]), ALU.subtract).then_inc(exps_in, 1)
            dve.wait_ge(gsub_in, 16)
            dve.wait_ge(live_done, 1)
            aii = gsub[:, H + 1:H + 2]
            plain, off = slot[:, 7:8], slot[:, 9:10]
            step(V.tensor_tensor(off, gsub[:, H:H + 1], aii, ALU.subtract))
            step(V.tensor_tensor(plain, off, tr[2][:, HEADS:HEADS + 1], ALU.subtract))
            b = small[:, 24:32]
            step(V.tensor_scalar(b[:, 0:1], off, A0, 1.0, ALU.mult, ALU.add))
            step(V.reciprocal(b[:, 1:2], b[:, 0:1]))
            step(V.tensor_scalar(b[:, 2:3], b[:, 1:2], A0, None, ALU.mult))
            step(V.tensor_tensor(b[:, 3:4], b[:, 2:3], aii, ALU.mult))
            step(V.scalar_tensor_tensor(b[:, 4:5], b[:, 1:2], 1.0, b[:, 3:4], ALU.add, ALU.subtract))
            step(V.tensor_scalar(b[:, 5:6], b[:, 2:3], 1.0 / XS, None, ALU.mult))
            step(V.tensor_scalar(kk, xsub, b[:, 4:5], None, ALU.mult))
            step(V.scalar_tensor_tensor(kk, gsub[:, 0:H], b[:, 5:6], kk, ALU.mult, ALU.add))
            norm_a, norm_b = st[:, 0], st[:, 1]
            moments(norm_a, kk).then_inc(slot_moments, 1)
            dve.wait_ge(exps_done, 1)
            sumf, z = small[:, 44:52], small[:, 52:60]
            step(V.reduce_sum(sumf, score[:, :, 0:SLOTS], AX.X))
            step(V.scalar_tensor_tensor(z, score[:, :, SLOTS], plain, sumf, ALU.mult, ALU.add))
            step(V.tensor_tensor(z, z, score[:, :, SLOTS + 1], ALU.add))
            step(V.reciprocal(z, z))
            share8 = score[:, :, SLOTS:SLOTS + 3]
            step(V.tensor_tensor(share8, share8, z.unsqueeze(2).broadcast_to([P, HEADS, 3]), ALU.mult))
            cdw = small[:, 60:63]
            step(V.reduce_sum(cdw, share8.rearrange("p h c -> p c h"), AX.X))
            step(V.tensor_scalar(cdw, cdw, 1.0 / HEADS, None, ALU.mult))
            vv = small[:, 63:64]
            step(V.tensor_tensor(vv, cdw[:, 2:3], cdw[:, 0:1], ALU.subtract))
            step(V.tensor_tensor(vv, vv, keep, ALU.mult))
            V.tensor_scalar(vsame[0:64], same[0:64], vv[0:64], None, ALU.mult).then_inc(shares_ready, 1)
            n = small[:, 64:68]
            step(V.tensor_tensor(n[:, 0:1], cdw[:, 0:1], aii, ALU.mult))
            step(V.scalar_tensor_tensor(n[:, 1:2], cdw[:, 1:2], 1.0, n[:, 0:1], ALU.add, ALU.subtract))
            step(V.tensor_scalar(n[:, 2:3], cdw[:, 0:1], 1.0 / XS, None, ALU.mult))
            step(V.tensor_scalar(q, xsub, n[:, 1:2], None, ALU.mult))
            step(V.scalar_tensor_tensor(q, gsub[:, 0:H], n[:, 2:3], q, ALU.mult, ALU.add))
            mix_low(4)
            mix_low(5)
            dve.wait_ge(mixed, 1)
            step(V.tensor_tensor(q, q, tr[2][:, :], ALU.add))
            moments(norm_b, q).then_inc(slot_moments, 1)
            dve.wait_ge(slot_root, 1)
            step(scale_shift(norm_a))
            step(V.tensor_scalar(kk, kk, norm_a[:, 8:9], norm_a[:, 9:10], ALU.mult, ALU.add))
            dve.wait_ge(slot_root, 2)
            step(scale_shift(norm_b))
            step(V.tensor_scalar(q, q, norm_b[:, 8:9], norm_b[:, 9:10], ALU.mult, ALU.add))
            step(V.tensor_tensor(dx1, q, kk, ALU.subtract))
            V.tensor_scalar(dx1, dx1, rep, None, ALU.mult).then_inc(change_ready, 1)
            mix_low(6)
            dve.wait_ge(dT_hi, 1)
            V.scalar_tensor_tensor(dT[:, 1, :], tr[0][:, 0:KF * SLOTS], XS, dT[:, 0, :], ALU.mult, ALU.subtract).then_inc(dT_lo, 1)
            dve.wait_ge(right_hi, 1)
            V.scalar_tensor_tensor(stackR[64:P, 1, :], dx1[64:P, :], WS, stackR[64:P, 0, :], ALU.mult, ALU.subtract).then_inc(right_lo, 1)
            mix_low(7)
            dve.wait_ge(right_hi, 2)
            V.scalar_tensor_tensor(stackR[0:64, 1, :], tr[2][0:64, :], 1.0 / XS, stackR[0:64, 0, :],
                                   ALU.mult, ALU.subtract).then_inc(right_lo, 1)
            for u in range(8, UNITS):
                mix_low(u)
            with overflow(dve):
                general_dve(dve)
            for t in range(T - 1):
                dve.wait_ge(out_done, t + 1)
                dve.wait_ge(biased, t + 1)
                if t >= 4:
                    dve.wait_ge(out_stored[t % 4], 16 * (t // 4))
                if t >= 2:
                    dve.wait_ge(z_normed, t - 1)
                V.scalar_tensor_tensor(y4(t), out_bank(t)[:, :], 1.0 / WS, x_sb[:, t, :], ALU.mult, ALU.add).then_inc(z_ready, 1)
                dve.wait_ge(z_ready, t + 1)
                moments(st[:, t % 2], y4(t)).then_inc(z_moments, 1)
                dve.wait_ge(z_root, t + 1)
                scale_shift(st[:, t % 2]).then_inc(z_stats, 1)
            t = T - 1
            dve.wait_ge(biased, T)
            dve.wait_ge(out_stored[t % 4], 16 * (t // 4))
            dve.wait_ge(z_normed, t - 1)
            for half in range(2):
                part = y4(t)[:, half * HALF:(half + 1) * HALF]
                dve.wait_ge(out_done, T + half)
                V.scalar_tensor_tensor(part, last_bank(half)[:, 0:HALF], 1.0 / WS, x_sb[:, t, half * HALF:(half + 1) * HALF],
                                       ALU.mult, ALU.add).then_inc(z_ready, 1)
                dve.wait_ge(z_ready, T + half)
                ins = V.bn_stats(last_st[:, 6 * half:6 * half + 6], part)
            step(ins)
            V.bn_aggr(st[:, t % 2, 6:8], last_st[:, 0:12]).then_inc(z_moments, 1)
            dve.wait_ge(z_root, T)
            scale_shift(st[:, t % 2]).then_inc(z_stats, 1)
            dve.wait_ge(z_stats, T)
            V.tensor_scalar(part, part, st[:, t % 2, 8:9], st[:, t % 2, 9:10], ALU.mult, ALU.add).then_inc(z_half_normed, 1)

        @block.tensor
        def _(pe):
            mm = nc.tensor.matmul

            def transpose_adj(t):
                pe.wait_ge(adj_cast, t + 1)
                for b in range(2):
                    if t >= 1:
                        pe.wait_ge(adjT_ready, 2 * (t - 1) + b + 1)
                    for k in range(8 * b, min(8 * b + 8, T)):
                        last = nc.tensor.transpose(tr16[b][0:width[k], (k % 8) * P:(k % 8 + 1) * P],
                                                   adj16[:, t % CASTS, k * P:k * P + width[k]], ident16[:])
                    last.then_inc(adj_transposed, 1)

            pe.wait_ge(consts, 5)
            pe.wait_ge(tr_zeroed, 1)
            def keep_warm(n):
                for _ in range(n):
                    mm(tr[2][:, 0:P], ones16[:], ones16[:], start=True, stop=True)

            keep_warm(28)
            transpose_adj(0)
            keep_warm(24)

            def sum_neighbours(i, ks):
                for k in ks:
                    if i == 0:
                        pe.wait_ge(x_lo, k + 1)
                    for half in range(2):
                        last = mm(sum_bank(i)[:, :], adjT[0:width[k], k, i * P:(i + 1) * P], xs[0:width[k], half, k, :],
                                  start=(k == 0 and half == 0), stop=(k == T - 1 and half == 1))
                    if k == T - 1:
                        last.then_inc(sums_done, 1)

            pe.wait_ge(adjT_ready, 2)
            sum_neighbours(0, range(0, 3))
            transpose_adj(1)
            pe.wait_ge(adjT_ready, 4)
            sum_neighbours(1, range(0, 3))
            sum_neighbours(0, range(3, 6))
            sum_neighbours(1, range(3, 6))
            sum_neighbours(0, range(6, 9))
            sum_neighbours(1, range(6, 9))
            transpose_adj(2)
            sum_neighbours(0, range(9, T))
            sum_neighbours(1, range(9, T))
            for i in range(1, T):
                if i >= 2:
                    pe.wait_ge(adjT_ready, 2 * (i + 1))
                    if i >= 3:
                        pe.wait_ge(y_ready, i - 2)
                    sum_neighbours(i, range(T))
                if i + 2 < T:
                    transpose_adj(i + 2)
                for n in wqk_at(i):
                    pe.wait_ge((wq_loaded, wk_loaded)[n // 4], 16)
                    if n >= 2:
                        pe.wait_ge(wqkT_ready, n - 1)
                    for k in range(KF):
                        last = nc.tensor.transpose(acc[(2, 4)[n % 2]][:, k * P:(k + 1) * P],
                                                   wraw[:, n // 4, k, (n % 4) * P:(n % 4 + 1) * P], ident[:])
                    last.then_inc(wqk_transposed, 1)
                if i in NUMBERED_AT:
                    if NUMBERED_AT[i] >= 1:
                        compact(pe, NUMBERED_AT[i] - 1)
                    number(pe, NUMBERED_AT[i])

            def mix_rows(first, last):
                for n in range(first, last):
                    u, k = divmod(n, T)
                    i, j = SPANS[u // KF]
                    f = u % KF
                    if k == 0:
                        if u < 2:
                            pe.wait_ge(wqkT_ready, 7 + u)
                        elif u < 4:
                            pe.wait_ge(y_ready, T - 3 + u)
                        else:
                            pe.wait_ge(mix_lo, u - 3)
                    if u == 0:
                        pe.wait_ge(x1_lo, k + 1)
                    for half in range(2):
                        ins = mm(mix_bank(u)[:, 0:j - i], x1s[0:width[k], half, k, f * P:(f + 1) * P], adjT[0:width[k], k, i:j],
                                 start=(k == 0 and half == 0), stop=(k == T - 1 and half == 1))
                    if k == T - 1:
                        ins.then_inc(mix_done, 1)

            mix_rows(0, 2)
            compact(pe, NUMBERED_AT[T] - 1)
            number(pe, NUMBERED_AT[T])
            mix_rows(2, 9)
            mix_rows(11, 17)
            mix_rows(9, 11)
            mix_rows(17, 19)
            compact(pe, NUMBERED_AT[T])
            number(pe, NUMBERED_AT[T + 1])
            mix_rows(19, 35)
            compact(pe, NUMBERED_AT[T + 1])
            number(pe, NUMBERED_AT[T + 2])
            mix_rows(35, 39)
            compact(pe, NUMBERED_AT[T + 2])
            mix_rows(39, 44)

            pe.wait_ge(spread_ready, 1)
            mm(tr[0][:, 0:192], ones[0:64, :], spread[0:64, 0:192], start=True, stop=True).then_inc(subs_spread, 1)
            mix_rows(44, 48)
            pe.wait_ge(xobj_in, 16)
            for k in range(KF):
                last = nc.tensor.transpose(tr[2][:, k * SLOTS:(k + 1) * SLOTS], xobj[0:64, k * P:(k + 1) * P], ident[0:64, 0:64])
            last.then_inc(xobj_T, 1)
            mix_rows(48, 50)
            pe.wait_ge(xsub_in, 16)
            for k in range(KF):
                last = nc.tensor.transpose(tr[1][:, k * SLOTS:(k + 1) * SLOTS], xsub[0:64, k * P:(k + 1) * P], ident[0:64, 0:64])
            last.then_inc(xsub_T, 1)
            mix_rows(50, 52)

            def project(bank, n, rows_T):
                for o in range(KF):
                    for k in range(KF):
                        last = mm(bank[:, o * SLOTS:(o + 1) * SLOTS], wT[:, n, k, o * P:(o + 1) * P],
                                  rows_T[:, k * SLOTS:(k + 1) * SLOTS], start=(k == 0), stop=(k == KF - 1))
                return last

            pe.wait_ge(xoT_ready, 1)
            project(tr[2], 1, xoT).then_inc(k_done, 1)
            pe.wait_ge(xsT_ready, 1)
            project(tr[1], 0, xsT).then_inc(q_done, 1)
            mix_rows(52, 56)
            pe.wait_ge(qk_read, 1)
            for k in range(KF):
                last = mm(tr[2][:, 2 * k:2 * k + 2], qk[:, k].rearrange("p two g -> p (two g)"), head_of, start=True, stop=True)
            last.then_inc(dots_done, 1)
            mix_rows(56, 60)
            pe.wait_ge(scores_ready, 1)
            mm(tr[1][:, :], ones[0:64, :], spread[0:64, :], start=True, stop=True).then_inc(scores_spread, 1)
            mm(tr[2][:, HEADS:HEADS + 1], same[0:64, :], small[0:64, 3:4], start=True, stop=True).then_inc(live_done, 1)
            mix_rows(60, 82)
            pe.wait_ge(shares_ready, 1)
            mm(tr[2][:, :], vsame[0:64, :], xobj[0:64, :], start=True, stop=True).then_inc(mixed, 1)
            mix_rows(82, 100)
            pe.wait_ge(change_ready, 1)
            for k in range(KF):
                last = nc.tensor.transpose(tr[0][:, k * SLOTS:(k + 1) * SLOTS], dx1[0:64, k * P:(k + 1) * P], ident[0:64, 0:64])
            last.then_inc(change_T, 1)
            mix_rows(100, 108)
            pe.wait_ge(dT_lo, 1)
            pe.wait_ge(w1_lo, 1)
            for k in range(KF):
                for n, (a, b) in enumerate(((0, 0), (0, 1), (1, 0))):
                    last = mm(tr[2][0:64, :], dT[:, a, k * SLOTS:(k + 1) * SLOTS], whl[:, b, k, :],
                              start=(k == 0 and n == 0), stop=(k == KF - 1 and n == 2))
            last.then_inc(dS_done, 1)
            mix_rows(108, UNITS * T)
            with overflow(pe):
                general_pe(pe)
            def transform(bank, t, columns):
                for k in range(KF):
                    for n, (a, b) in enumerate(((0, 0), (0, 1), (1, 0))):
                        mm(bank, mix[:, a, k, t * P:(t + 1) * P], whl[:, b, k, columns], start=(k == 0 and n == 0), stop=False)
                if t == 0:
                    pe.wait_ge(cols_in, 16)
                    pe.wait_ge(low_ready, 1)
                    pe.wait_ge(right_hi, 2)
                    pe.wait_ge(right_lo, 2)
                for half in range(2):
                    last = mm(bank, stackL[:, t * P:(t + 1) * P], stackR[:, half, columns], start=False, stop=(half == 1))
                last.then_inc(out_done, 1)

            for t in range(T):
                if t >= OUTS:
                    pe.wait_ge(z_ready, t - OUTS + 1)
                else:
                    pe.wait_ge(mix_lo, (4, 4, 9, 10, 11, 12)[t])
                if t < T - 1:
                    transform(out_bank(t)[:, :], t, slice(0, H))
            for half in range(2):
                transform(last_bank(half)[:, 0:HALF], T - 1, slice(half * HALF, (half + 1) * HALF))


_INS = ['x', 'adj', 'L0_gnn_rel_pair_index', 'L0_gnn_Wq', 'L0_gnn_bq', 'L0_gnn_Wk', 'L0_gnn_bk', 'L1_gnn_weight', 'L1_gnn_bias']


def kernel(**inputs):
    import numpy as _np
    import concourse.bacc as _bacc
    from concourse import mybir as _mybir
    from concourse.bass_utils import run_bass_kernel_spmd as _run

    nc = _bacc.Bacc("TRN2", target_bir_lowering=False, num_devices=1)
    arrays, args = {}, []
    for name in _INS:
        a = _np.ascontiguousarray(inputs[name])
        arrays[f"in_{name}"] = a
        args.append(nc.dram_tensor(f"in_{name}", a.shape, _mybir.dt.from_np(a.dtype), kind="ExternalInput").ap())
    args.append(nc.dram_tensor("out_0", (N, H), _mybir.dt.float32, kind="ExternalOutput").ap())
    resnorm_graph(nc, *args)
    r = _run(nc, [arrays], core_ids=[0])
    return r.results[0]["out_0"]
```
